# Optimizing a Trainium2 kernel written in Bass

```python
import numpy as np
import jax
import jax.numpy as jnp

def _softmax(x, axis=-1):
    return jax.nn.softmax(x, axis=axis)

def _gelu(x):
    return jax.nn.gelu(x, approximate=True)

def _silu(x):
    return jax.nn.silu(x)

def _sigmoid(x):
    return jax.nn.sigmoid(x)

def _layernorm(x, axis=-1, eps=1e-05):
    m = jnp.mean(x, axis=axis, keepdims=True)
    v = jnp.var(x, axis=axis, keepdims=True)
    return (x - m) / jnp.sqrt(v + eps)

def _scatter_add(tgt, idx, src, axis=0):
    return tgt.at[idx].add(src)

def _segment_sum(src, seg, n):
    return jax.ops.segment_sum(src, seg, n)
kernel_name = 'mk_audio_tower_d2_tok_audfeat512_r4_b7d00c'

def setup_inputs(seed: int=0):
    np.random.seed(seed)
    _w = jnp.asarray

    def _rec_inputs():
        import jax
        import jax.numpy as jnp
        _rk = jax.random.key(seed)
        x = -3.53888e-05 + 1.00021 * jax.random.normal(jax.random.fold_in(_rk, 1), (64, 256, 23), jnp.float32)
        return x
    x = _rec_inputs()

    def _L0_tok_setup():
        import jax, jax.numpy as jnp
        import numpy as np
        CONTEXT = 5
        DILATION = 1
        BN_EPS = 1e-05

        def _tdnn_forward(x, W, b, gamma, beta):
            B, T, D = x.shape
            L = T - (CONTEXT - 1) * DILATION
            frames = jnp.stack([jax.lax.dynamic_slice_in_dim(x, k * DILATION, L, axis=1) for k in range(CONTEXT)], axis=2)
            patches = frames.reshape(B, L, CONTEXT * D)
            y = jnp.einsum('blf,of->blo', patches, W) + b
            y = jax.nn.relu(y)
            mean = jnp.mean(y, axis=(0, 1))
            var = jnp.var(y, axis=(0, 1))
            y = (y - mean) * jax.lax.rsqrt(var + BN_EPS) * gamma + beta
            return y
        key = jax.random.key(seed)
        k1, k2, k3 = jax.random.split(key, 3)
        B, T, D, O = (64, 1024, 23, 128)
        x = jax.random.normal(k1, (B, T, D), dtype=jnp.float32)
        fan_in = D * CONTEXT
        bound = 1.0 / np.sqrt(fan_in)
        W = jax.random.uniform(k2, (O, fan_in), dtype=jnp.float32, minval=-bound, maxval=bound)
        b = jax.random.uniform(k3, (O,), dtype=jnp.float32, minval=-bound, maxval=bound)
        gamma = jnp.ones((O,), dtype=jnp.float32)
        beta = jnp.zeros((O,), dtype=jnp.float32)
        return {'x': x, 'W': W, 'b': b, 'gamma': gamma, 'beta': beta}
    _L0_tok_all = _L0_tok_setup()
    _L0_tok_in = {k: v for k, v in _L0_tok_all.items() if k in ('W', 'b', 'gamma', 'beta')}
    del _L0_tok_all

    def _L0_attn_setup():
        import jax, jax.numpy as jnp
        import numpy as np
        STAGES = 3
        CAUSAL = True

        def _positional_encoding(T, W):
            half = W // 2
            t = jnp.arange(T, dtype=jnp.float32)
            freqs = 10000.0 ** (-jnp.arange(half, dtype=jnp.float32) / half)
            phi = t[:, None] * freqs[None, :]
            return jnp.concatenate([jnp.sin(phi), jnp.cos(phi)], axis=-1)
        key = jax.random.key(seed)
        k1, k2, k3 = jax.random.split(key, 3)
        B, T, W = (4, 512, 128)
        X = jax.random.normal(k1, (B, T, W), dtype=jnp.float32)
        W_proj = jax.random.normal(k2, (W, W, STAGES + 1), dtype=jnp.float32) * 0.02
        W_filt = jax.random.normal(k3, (W, W, STAGES), dtype=jnp.float32) * 0.02
        return {'X': X, 'W_proj': W_proj, 'W_filt': W_filt}
    _L0_attn_all = _L0_attn_setup()
    _L0_attn_in = {k: v for k, v in _L0_attn_all.items() if k in ('W_proj', 'W_filt')}
    del _L0_attn_all

    def _L0_ffn_setup():
        import jax, jax.numpy as jnp
        import numpy as np
        B, L, H, E, F, C = (8, 2048, 128, 8, 256, 2)
        key = jax.random.key(seed)
        ks = jax.random.split(key, 4)
        x = jax.random.normal(ks[0], (B, L, H), jnp.float32)
        Wg = jax.random.normal(ks[1], (H, E), jnp.float32) * H ** (-0.5)
        W1 = jax.random.normal(ks[2], (E, H, F), jnp.float32) * H ** (-0.5)
        b1 = jnp.zeros((E, F), jnp.float32)
        W2 = jax.random.normal(ks[3], (E, F, H), jnp.float32) * F ** (-0.5)
        b2 = jnp.zeros((E, H), jnp.float32)
        return {'x': x, 'Wg': Wg, 'W1': W1, 'b1': b1, 'W2': W2, 'b2': b2}
    _L0_ffn_all = _L0_ffn_setup()
    _L0_ffn_in = {k: v for k, v in _L0_ffn_all.items() if k in ('Wg', 'W1', 'b1', 'W2', 'b2')}
    del _L0_ffn_all

    def _L1_attn_setup():
        import jax, jax.numpy as jnp
        import numpy as np
        import math
        HEADS = 8
        key = jax.random.key(seed)
        ks = jax.random.split(key, 9)
        B, T, E = (2, 512, 128)
        s = 1.0 / math.sqrt(E)
        return {'x': jax.random.normal(ks[0], (B, T, E), jnp.float32), 'wq': jax.random.normal(ks[1], (E, E), jnp.float32) * s, 'bq': jax.random.normal(ks[2], (E,), jnp.float32) * s, 'wk': jax.random.normal(ks[3], (E, E), jnp.float32) * s, 'bk': jax.random.normal(ks[4], (E,), jnp.float32) * s, 'wv': jax.random.normal(ks[5], (E, E), jnp.float32) * s, 'bv': jax.random.normal(ks[6], (E,), jnp.float32) * s, 'wg': jax.random.normal(ks[7], (E, E), jnp.float32) * s, 'bg': jax.random.normal(ks[8], (E,), jnp.float32) * s}
    _L1_attn_all = _L1_attn_setup()
    _L1_attn_in = {k: v for k, v in _L1_attn_all.items() if k in ('wq', 'bq', 'wk', 'bk', 'wv', 'bv', 'wg', 'bg')}
    del _L1_attn_all

    def _L1_ffn_setup():
        import jax, jax.numpy as jnp
        import numpy as np
        B, S, D = (8, 512, 128)
        FF = 512
        E = 8
        key = jax.random.key(seed)
        ks = jax.random.split(key, 7)
        s = 1.0 / np.sqrt(D)
        sf = 1.0 / np.sqrt(FF)
        return {'x': jax.random.normal(ks[0], (B, S, D), dtype=jnp.float32), 'Wg': jax.random.uniform(ks[1], (D, E), jnp.float32, -s, s), 'bg': jax.random.uniform(ks[2], (E,), jnp.float32, -s, s), 'W1': jax.random.uniform(ks[3], (E, D, FF), jnp.float32, -s, s), 'b1': jax.random.uniform(ks[4], (E, FF), jnp.float32, -s, s), 'W2': jax.random.uniform(ks[5], (E, FF, D), jnp.float32, -sf, sf), 'b2': jax.random.uniform(ks[6], (E, D), jnp.float32, -sf, sf)}
    _L1_ffn_all = _L1_ffn_setup()
    _L1_ffn_in = {k: v for k, v in _L1_ffn_all.items() if k in ('Wg', 'bg', 'W1', 'b1', 'W2', 'b2')}
    del _L1_ffn_all
    return {'x': x, 'L0_tok_W': _L0_tok_in['W'], 'L0_tok_b': _L0_tok_in['b'], 'L0_tok_gamma': _L0_tok_in['gamma'], 'L0_tok_beta': _L0_tok_in['beta'], 'L0_attn_W_proj': _L0_attn_in['W_proj'], 'L0_attn_W_filt': _L0_attn_in['W_filt'], 'L0_ffn_Wg': _L0_ffn_in['Wg'], 'L0_ffn_W1': _L0_ffn_in['W1'], 'L0_ffn_b1': _L0_ffn_in['b1'], 'L0_ffn_W2': _L0_ffn_in['W2'], 'L0_ffn_b2': _L0_ffn_in['b2'], 'L1_attn_wq': _L1_attn_in['wq'], 'L1_attn_bq': _L1_attn_in['bq'], 'L1_attn_wk': _L1_attn_in['wk'], 'L1_attn_bk': _L1_attn_in['bk'], 'L1_attn_wv': _L1_attn_in['wv'], 'L1_attn_bv': _L1_attn_in['bv'], 'L1_attn_wg': _L1_attn_in['wg'], 'L1_attn_bg': _L1_attn_in['bg'], 'L1_ffn_Wg': _L1_ffn_in['Wg'], 'L1_ffn_bg': _L1_ffn_in['bg'], 'L1_ffn_W1': _L1_ffn_in['W1'], 'L1_ffn_b1': _L1_ffn_in['b1'], 'L1_ffn_W2': _L1_ffn_in['W2'], 'L1_ffn_b2': _L1_ffn_in['b2']}

def reference(x, L0_tok_W, L0_tok_b, L0_tok_gamma, L0_tok_beta, L0_attn_W_proj, L0_attn_W_filt, L0_ffn_Wg, L0_ffn_W1, L0_ffn_b1, L0_ffn_W2, L0_ffn_b2, L1_attn_wq, L1_attn_bq, L1_attn_wk, L1_attn_bk, L1_attn_wv, L1_attn_bv, L1_attn_wg, L1_attn_bg, L1_ffn_Wg, L1_ffn_bg, L1_ffn_W1, L1_ffn_b1, L1_ffn_W2, L1_ffn_b2):
    import jax
    import jax.numpy as jnp

    def _L0_tok_ref(x, W, b, gamma, beta):
        import jax, jax.numpy as jnp
        import numpy as np
        CONTEXT = 5
        DILATION = 1
        BN_EPS = 1e-05

        def _tdnn_forward(x, W, b, gamma, beta):
            B, T, D = x.shape
            L = T - (CONTEXT - 1) * DILATION
            frames = jnp.stack([jax.lax.dynamic_slice_in_dim(x, k * DILATION, L, axis=1) for k in range(CONTEXT)], axis=2)
            patches = frames.reshape(B, L, CONTEXT * D)
            y = jnp.einsum('blf,of->blo', patches, W) + b
            y = jax.nn.relu(y)
            mean = jnp.mean(y, axis=(0, 1))
            var = jnp.var(y, axis=(0, 1))
            y = (y - mean) * jax.lax.rsqrt(var + BN_EPS) * gamma + beta
            return y
        return _tdnn_forward(x, W, b, gamma, beta)

    def _L0_attn_ref(X, W_proj, W_filt):
        import jax, jax.numpy as jnp
        import numpy as np
        STAGES = 3
        CAUSAL = True

        def _positional_encoding(T, W):
            half = W // 2
            t = jnp.arange(T, dtype=jnp.float32)
            freqs = 10000.0 ** (-jnp.arange(half, dtype=jnp.float32) / half)
            phi = t[:, None] * freqs[None, :]
            return jnp.concatenate([jnp.sin(phi), jnp.cos(phi)], axis=-1)
        B, T, W = X.shape
        x = jnp.einsum('btw,wvs->btvs', X, W_proj)
        pe = _positional_encoding(T, W)
        f = jnp.einsum('tw,wvs->tvs', pe, W_filt)
        if CAUSAL:
            x = jnp.concatenate([x, jnp.zeros_like(x)], axis=1)
            f = jnp.concatenate([f, jnp.zeros_like(f)], axis=0)
        n = x.shape[1]
        Ff = jnp.fft.rfft(f, axis=0)
        y = x[..., 0]
        for i in range(STAGES):
            Fy = jnp.fft.rfft(y, axis=1)
            y = jnp.fft.irfft(Fy * Ff[None, :, :, i], n=n, axis=1) * x[..., i + 1]
        if CAUSAL:
            y = y[:, :T]
        return y

    def _L0_ffn_ref(x, Wg, W1, b1, W2, b2):
        import jax, jax.numpy as jnp
        import numpy as np
        B, L, H, E, F, C = (8, 2048, 128, 8, 256, 2)
        b, l, h = x.shape
        e = Wg.shape[1]
        k = min(max(int(l * C / e), 1), l)
        S = jax.nn.softmax(x @ Wg, axis=-1)
        St = jnp.swapaxes(S, 1, 2)
        G, I = jax.lax.top_k(St, k)
        ex = jnp.take_along_axis(x[:, None], I[..., None], axis=2)
        hmid = jax.nn.gelu(jnp.einsum('bekh,ehf->bekf', ex, W1) + b1[None, :, None, :], approximate=False)
        out = jnp.einsum('bekf,efh->bekh', hmid, W2) + b2[None, :, None, :]
        vals = G[..., None] * out
        new_x = jnp.zeros_like(x).at[jnp.arange(b)[:, None, None], I].add(vals)
        return new_x

    def _L1_attn_ref(x, wq, bq, wk, bk, wv, bv, wg, bg):
        import jax, jax.numpy as jnp
        import numpy as np
        import math
        HEADS = 8
        B, T, E = x.shape
        H = HEADS
        D = E // H
        gammas = 1.0 - 2.0 ** (-5.0 - jnp.arange(H, dtype=jnp.float32))
        q = (x @ wq.T + bq).reshape(B, T, H, D)
        k = (x @ wk.T + bk).reshape(B, T, H, D)
        v = (x @ wv.T + bv).reshape(B, T, H, D)
        idx = jnp.arange(T)
        rel = idx[None, :] - idx[:, None]
        decay = jnp.where(rel[None] >= 0, gammas[:, None, None] ** rel[None].astype(jnp.float32), 0.0)
        scores = jnp.einsum('bihd,bjhd->bhij', q, k) / math.sqrt(D)
        scores = scores * decay[None]
        out = jnp.einsum('bhij,bjhd->bihd', scores, v).reshape(B, T, E)
        gate = jax.nn.silu(x @ wg.T + bg)
        return gate * out

    def _L1_ffn_ref(x, Wg, bg, W1, b1, W2, b2):
        import jax, jax.numpy as jnp
        import numpy as np
        B, S, D = (8, 512, 128)
        FF = 512
        E = 8
        b, s, d = x.shape
        xf = x.reshape(-1, d)
        logits = xf @ Wg + bg
        probs = jax.nn.softmax(logits, axis=-1)
        pmax = jnp.max(probs, axis=-1)
        routes = jnp.argmax(probs, axis=-1)
        xs = xf * pmax[:, None]
        out_tok = jnp.zeros_like(xf)
        for e in range(E):
            h = jax.nn.relu(xs @ W1[e] + b1[e])
            y = h @ W2[e] + b2[e]
            out_tok = jnp.where((routes == e)[:, None], y, out_tok)
        order = jnp.argsort(routes)
        return out_tok[order].reshape(b, s, d)
    h = _L0_tok_ref(x, L0_tok_W, L0_tok_b, L0_tok_gamma, L0_tok_beta)
    h = h + _L0_attn_ref(_layernorm(h, axis=-1), L0_attn_W_proj, L0_attn_W_filt)
    h = h + _L0_ffn_ref(_layernorm(h, axis=-1), L0_ffn_Wg, L0_ffn_W1, L0_ffn_b1, L0_ffn_W2, L0_ffn_b2)
    h = h + _L1_attn_ref(_layernorm(h, axis=-1), L1_attn_wq, L1_attn_bq, L1_attn_wk, L1_attn_bk, L1_attn_wv, L1_attn_bv, L1_attn_wg, L1_attn_bg)
    h = h + _L1_ffn_ref(_layernorm(h, axis=-1), L1_ffn_Wg, L1_ffn_bg, L1_ffn_W1, L1_ffn_b1, L1_ffn_W2, L1_ffn_b2)
    return h

_drawn_inputs = setup_inputs


def setup_inputs(seed=0):
    import zlib

    import numpy as np

    out = dict(_drawn_inputs(seed))
    spreads = {'L0_tok_gamma': (1.0, 0.2),
     'L0_tok_beta': (0.0, 0.1),
     'L0_ffn_b1': (0.0, 0.1),
     'L0_ffn_b2': (0.0, 0.1)}
    factors = {'L1_ffn_Wg': 8.0,
     'L1_ffn_bg': 8.0,
     'L1_ffn_W1': 8.0,
     'L1_ffn_b1': 8.0,
     'L1_ffn_W2': 7.916,
     'L1_ffn_b2': 33.513}
    for name, (base, spread) in spreads.items():
        noise = np.random.default_rng([zlib.crc32(name.encode()), seed]).standard_normal(out[name].shape)
        drawn = base * np.exp(spread * noise) if base else spread * noise
        out[name] = jnp.asarray(drawn.astype(out[name].dtype))
    for name, factor in factors.items():
        out[name] = (out[name] * factor).astype(out[name].dtype)
    return out
```

```python
from contextlib import ExitStack

import concourse.bass as bass
from concourse import mybir

FP32 = mybir.dt.float32
BF16 = mybir.dt.bfloat16
I32 = mybir.dt.int32
ALU = mybir.AluOpType
ACT = mybir.ActivationFunctionType
AX = mybir.AxisListType

B, T_IN, D_IN = 64, 256, 23
CTX = 5
L = T_IN - CTX + 1
HALF = L // 2
NT = 2 * B
TOK = B * L
F = 128
QT = 4
QN = QT * HALF
QF = QT * F
NQ = NT // QT
PATCH = CTX * D_IN
EPS = 1e-5
STAGES = 3
PAD = 3 * HALF
E = 8
TOPK = L * 2 // E
F0 = 256
F1 = 512
HEADS = 8
HD = F // HEADS
CG = 32
NG = F // CG
QC = 4
NS = CG // QC
RB = 256
REG = TOK + RB
DUMMY_IN = E * REG
DUMMY_OUT = TOK
NK = (TOK + E * (RB - 1)) // RB
NK += NK % 2
TR = 6


def apart(eng):
    eng.nop(nofuse=True)


class Chain:

    def __init__(self, eng, sem, at=0, per=0, base=0):
        self.eng, self.sem, self.n, self.start = eng, sem, 0, at * per + base

    def sig(self, ins):
        ins.then_inc(self.sem, 1)
        self.n += 1

    def wait(self):
        self.eng.wait_ge(self.sem, self.start + self.n)

    def link(self, ins):
        self.sig(ins)
        self.wait()


class Tools:
    def __init__(self, nc, top):
        self.nc, self.top = nc, top

    def sem(self, name):
        return self.top.enter_context(self.nc.semaphore(name))

    def sb(self, ctx, name, shape, dt=FP32):
        return ctx.enter_context(self.nc.sbuf_tensor(name, list(shape), dt))

    def ps(self, ctx, name, dt=FP32):
        return ctx.enter_context(self.nc.psum_tensor(name, [128, 2048 // (4 if dt == FP32 else 2)], dt))


def tdnn(nc, k, d, ident, small, bn, fm, filt_dram):
    ctx = ExitStack()
    with ctx:
        U = 2
        tok_w = k.sb(ctx, "tok_w", [PATCH + 1, F])
        patch = k.sb(ctx, "patch", [HALF, U, QT, PATCH + 1])
        patch_t = k.sb(ctx, "patch_t", [PATCH + 1, U, QN])
        stats = k.sb(ctx, "stats", [F, NQ * 6])
        mv = k.sb(ctx, "mv", [F, 2])
        rs = k.sb(ctx, "rs", [F, 4])
        nhalf = k.sb(ctx, "nhalf", [F, 1])
        pe_t = k.sb(ctx, "pe_t", [F, L])
        w_filt = k.sb(ctx, "w_filt", [F, F * STAGES])
        filt = k.sb(ctx, "filt", [F, 2, STAGES, PAD])
        p_win = [k.ps(ctx, f"p_win{u}") for u in range(U)]
        p_y = [k.ps(ctx, f"p_y{u}") for u in range(U)]
        p_filt = [k.ps(ctx, f"p_filt{s}") for s in range(STAGES)]

        consts = k.sem("consts")
        win_in = [k.sem(f"win_in{u}") for u in range(U)]
        ones_set = k.sem("ones_set")
        win_t = k.sem("win_t")
        win_copied = k.sem("win_copied")
        y_done = k.sem("y_done")
        relu_done = k.sem("relu_done")
        bn_step = k.sem("bn_step")
        rstd_done = k.sem("rstd_done")
        nhalf_set = k.sem("nhalf_set")
        filt_pe = k.sem("filt_pe")
        filt_zero = k.sem("filt_zero")
        filt_copied = k.sem("filt_copied")
        filt_out = k.sem("filt_out")
        block = ctx.enter_context(nc.Block())

        @block.sync
        def _(sp):
            sp.dma_start(tok_w[:, :], d["tok_w"]).then_inc(consts, 16)
            sp.dma_start(ident[:, :], d["ident"]).then_inc(consts, 16)
            sp.dma_start(small[:, :], d["small"]).then_inc(consts, 16)
            sp.dma_start(pe_t[:, :], d["pe_t"]).then_inc(consts, 16)
            sp.dma_start(w_filt[:, :], d["w_filt"]).then_inc(consts, 16)
            sp.wait_ge(ones_set, U)
            with sp.Fori(0, NQ // U) as i:
                for u in range(U):
                    sp.wait_ge(win_copied, i * U + u + 1)
                    for b in range(2):
                        at = d["x"][bass.ds((i * U + u) * (2 * T_IN * D_IN) + b * T_IN * D_IN, 1)]
                        src = bass.AP(at.tensor, at.offset, [[D_IN, HALF], [HALF * D_IN, 2], [1, PATCH]])
                        sp.dma_start(patch[:, u, 2 * b:2 * b + 2, 0:PATCH], src).then_inc(win_in[u], 16)
            sp.wait_ge(filt_zero, 1)
            sp.wait_ge(filt_copied, 2 * STAGES)
            sp.dma_start(filt_dram.ap().rearrange("r s c t -> c r s t"), filt[:, :, :, :]).then_inc(filt_out, 16)
            sp.wait_ge(filt_out, 16)

        @block.tensor
        def _(pe):
            pe.wait_ge(consts, 80)
            for s in range(STAGES):
                wf = w_filt[:, :].rearrange("p (c s) -> p s c", s=STAGES)[:, s, :]
                pe.matmul(p_filt[s][:, 0:L], wf, pe_t[:, :], start=True, stop=True).then_inc(filt_pe, 1)
            with pe.Fori(0, NQ // U) as i:
                for u in range(U):
                    pe.wait_ge(win_in[u], i * 32 + 32)
                    pe.wait_ge(win_copied, i * U + u + 1)
                    for j in range(QT):
                        m = pe.transpose(p_win[u][0:PATCH + 1, j * HALF:(j + 1) * HALF], patch[:, u, j, :],
                                         ident[0:HALF, 0:HALF])
                    m.then_inc(win_t, 1)
                for u in range(U):
                    pe.wait_ge(win_copied, i * U + u + 1 + U)
                    pe.wait_ge(relu_done, i * U + u + 1)
                    pe.matmul(p_y[u][:, 0:QN], tok_w[:, :], patch_t[:, u, :], start=True, stop=True).then_inc(y_done, 1)

        @block.scalar
        def _(act):
            act.sem_inc(win_copied, U)
            act.sem_inc(relu_done, U)
            for s in range(STAGES):
                act.wait_ge(filt_pe, s + 1)
                act.activation(filt[:, 0, s, HALF:HALF + L], p_filt[s][:, 0:L], ACT.Copy).then_inc(filt_copied, 1)
                act.activation(filt[:, 1, s, 0:L], p_filt[s][:, L - 1::-1], ACT.Copy).then_inc(filt_copied, 1)
            with act.Fori(0, NQ // U) as i:
                for u in range(U):
                    act.wait_ge(win_t, i * U + u + 1)
                    act.activation(patch_t[:, u, :], p_win[u][0:PATCH + 1, 0:QN], ACT.Copy).then_inc(win_copied, 1)
                for u in range(U):
                    act.wait_ge(y_done, i * U + u + 1)
                    apart(act)
                    act.activation(fm[:, bass.ds((i * U + u) * QN, QN)], p_y[u][:, 0:QN], ACT.Relu).then_inc(relu_done, 1)

        @block.gpsimd
        def _(pool):
            pool.memset(nhalf[:, :], -0.5).then_inc(nhalf_set, 1)
            pool.memset(filt[:, 0, :, 0:HALF], 0.0).then_inc(nhalf_set, 1)
            pool.memset(filt[:, 1, :, L:PAD], 0.0).then_inc(filt_zero, 1)
            pool.wait_ge(nhalf_set, 2)
            pool.wait_ge(bn_step, 2)
            pool.tensor_tensor(out=rs[:, 1:2], in0=rs[:, 0:1], in1=nhalf[:, :], op=ALU.pow).then_inc(rstd_done, 1)

        @block.vector
        def _(dve):
            for u in range(U):
                dve.memset(patch[:, u, :, PATCH:PATCH + 1], 1.0).then_inc(ones_set, 1)
            with dve.Fori(0, NQ) as i:
                dve.wait_ge(relu_done, i + 1 + U)
                dve.bn_stats(stats[:, bass.ds(i * 6, 6)], fm[:, bass.ds(i * QN, QN)]).then_inc(ones_set, 1)
            dve.wait_ge(ones_set, U + NQ)
            ch = Chain(dve, bn_step)
            ch.link(dve.bn_aggr(mv[:, :], stats[:, :]))
            ch.sig(dve.tensor_scalar(rs[:, 0:1], mv[:, 1:2], EPS, None, ALU.add))
            dve.wait_ge(consts, 80)
            dve.wait_ge(rstd_done, 1)
            ch.link(dve.tensor_tensor(bn[:, 0:1], small[:, 0:1], rs[:, 1:2], ALU.mult))
            ch.link(dve.tensor_tensor(rs[:, 2:3], mv[:, 0:1], bn[:, 0:1], ALU.mult))
            ch.link(dve.tensor_tensor(bn[:, 1:2], small[:, 1:2], rs[:, 2:3], ALU.subtract))


def first_norm(nc, k, d, ident, bn, fm, fm_rev, h0_dram):
    ctx = ExitStack()
    with ctx:
        U = 4
        hn = k.sb(ctx, "hn", [F, U, QN])
        ht = k.sb(ctx, "ht", [HALF, U, QF])
        xn = k.sb(ctx, "xn", [HALF, U, QF])
        lst = k.sb(ctx, "lst", [HALF, U, QT, 6])
        lmv = k.sb(ctx, "lmv", [HALF, U, QT, 2])
        lve = k.sb(ctx, "lve", [HALF, U, QT])
        lrs = k.sb(ctx, "lrs", [HALF, U, QT])
        nhalf = k.sb(ctx, "nhalf_b", [HALF, QT])
        p_h = [k.ps(ctx, f"p_h{u}") for u in range(U)]
        p_x = [k.ps(ctx, f"p_x{u}") for u in range(U)]

        hn_ready = k.sem("hn_ready")
        h_done = k.sem("h_done")
        ht_copied = k.sem("ht_copied")
        h0_out = [k.sem(f"h0_out{u}") for u in range(U)]
        var_done = k.sem("var_done")
        rstd_done = k.sem("rstd_done_b")
        pool_step = k.sem("pool_step_b")
        dve_step = k.sem("dve_step_b")
        xn_ready = k.sem("xn_ready")
        xt_done = k.sem("xt_done")
        fm_copied = k.sem("fm_copied")
        rev_copied = k.sem("rev_copied")
        block = ctx.enter_context(nc.Block())

        @block.sync
        def _(sp):
            with sp.Fori(0, NQ // U) as i:
                for u in range(U):
                    sp.wait_ge(ht_copied, i * U + u + 1 + U)
                    sp.dma_start(h0_dram[:, bass.ds((i * U + u) * QF, QF)], ht[:, u, :]).then_inc(h0_out[u], 16)
            for u in range(U):
                sp.wait_ge(h0_out[u], 16 * (NQ // U + 1))

        @block.tensor
        def _(pe):
            with pe.Fori(0, NQ // U) as i:
                for u in range(U):
                    pe.wait_ge(hn_ready, i * U + u + 1)
                    pe.wait_ge(ht_copied, i * U + u + 1)
                    for j in range(QT):
                        m = pe.transpose(p_h[u][0:HALF, j * F:(j + 1) * F], hn[:, u, j * HALF:(j + 1) * HALF], ident[:, :])
                    m.then_inc(h_done, 1)
                for u in range(U):
                    pe.wait_ge(xn_ready, i * U + u + 1)
                    pe.wait_ge(rev_copied, i * U + u + 1)
                    for j in range(QT):
                        m = pe.transpose(p_x[u][:, j * HALF:(j + 1) * HALF], xn[:, u, j * F:(j + 1) * F],
                                         ident[0:HALF, 0:HALF])
                    m.then_inc(xt_done, 1)

        @block.scalar
        def _(act):
            act.sem_inc(ht_copied, U)
            for u in range(U):
                act.sem_inc(h0_out[u], 16)
            with act.Fori(0, NQ // U) as i:
                for u in range(U):
                    act.activation(hn[:, u, :], fm[:, bass.ds((i * U + u) * QN, QN)], ACT.Identity,
                                   bias=bn[:, 1:2], scale=bn[:, 0:1]).then_inc(hn_ready, 1)
                for u in range(U):
                    act.wait_ge(h_done, i * U + u + 1)
                    act.wait_ge(h0_out[u], i * 16 + 16)
                    act.activation(ht[:, u, :], p_h[u][0:HALF, :], ACT.Copy).then_inc(ht_copied, 1)
                for u in range(U):
                    act.wait_ge(xt_done, i * U + u + 1)
                    apart(act)
                    act.activation(fm[:, bass.ds((i * U + u) * QN, QN)], p_x[u][:, 0:QN], ACT.Copy).then_inc(fm_copied, 1)

        @block.gpsimd
        def _(pool):
            ch = Chain(pool, pool_step)
            ch.link(pool.memset(nhalf[:, :], -0.5))
            with pool.Fori(0, NQ // U) as i:
                for u in range(U):
                    pool.wait_ge(var_done, i * U + u + 1)
                    apart(pool)
                    pc = Chain(pool, pool_step, i, U, 1 + u)
                    pc.link(pool.tensor_scalar(lve[:, u, :], lmv[:, u, :, 1], EPS, None, ALU.add))
                    pool.tensor_tensor(out=lrs[:, u, :], in0=lve[:, u, :], in1=nhalf[:, :], op=ALU.pow).then_inc(rstd_done, 1)

        @block.vector
        def _(dve):
            dve.sem_inc(rev_copied, U)
            with dve.Fori(0, NQ // U) as i:
                ch = Chain(dve, dve_step, i, U)
                for u in range(U):
                    dve.wait_ge(ht_copied, i * U + u + 1 + U)
                    for j in range(QT):
                        m = dve.bn_stats(lst[:, u, j, :], ht[:, u, j * F:(j + 1) * F])
                    ch.link(m)
                    apart(dve)
                    for j in range(QT):
                        m = dve.bn_aggr(lmv[:, u, j, :], lst[:, u, j, :])
                    m.then_inc(var_done, 1)
                for u in range(U):
                    dve.wait_ge(rstd_done, i * U + u + 1)
                    for j in range(QT):
                        m = dve.tensor_scalar(xn[:, u, j * F:(j + 1) * F], ht[:, u, j * F:(j + 1) * F],
                                              lmv[:, u, j, 0:1], lrs[:, u, j:j + 1], ALU.subtract, ALU.mult)
                    m.then_inc(xn_ready, 1)
                for u in range(U):
                    dve.wait_ge(fm_copied, i * U + u + 1)
                    rev = fm_rev[:, bass.ds((i * U + u) * QN, QN)].rearrange("p (j t) -> p j t", j=QT)
                    src = p_x[u][:, 0:QN].rearrange("p (j t) -> p j t", j=QT)[:, :, ::-1]
                    dve.tensor_copy(rev, src).then_inc(rev_copied, 1)


def convolutions(nc, k, d, fm, fm_rev, filt_dram, att_dram):
    ctx = ExitStack()
    with ctx:
        w_proj = k.sb(ctx, "w_proj", [F, NG, 2, 2 * CG])
        x = k.sb(ctx, "x", [HALF, 2, 2, 2, CG * B])
        toep = k.sb(ctx, "toep", [HALF, TR, 2, L])
        p_p = [k.ps(ctx, f"p_p{r}") for r in range(4)]
        p_c = [k.ps(ctx, f"p_c{r}") for r in range(4)]
        NB = 8
        BANKS = (B // NB) * 2 * 2
        STEPS = STAGES * NS
        TILES = 2 * STEPS

        w_in = k.sem("w_in")
        toep_in = [k.sem(f"toep_in{r}") for r in range(TR)]
        proj_done = k.sem("proj_done")
        proj_copied = k.sem("proj_copied")
        conv_done = k.sem("conv_done")
        prod_done = k.sem("prod_done")
        att_out = k.sem("att_out")
        att_stored = k.sem("att_stored")
        block = ctx.enter_context(nc.Block())

        def banks():
            for o in (1, 0):
                for bg in range(B // NB):
                    for half in range(2):
                        yield o, bg, half

        def place(s):
            return s % 2, s // 2

        @block.sync
        def _(sp):
            sp.dma_start(w_proj[:, :, :, :], d["w_proj"]).then_inc(w_in, 16)
            with sp.Fori(0, NG) as g:
                for m in range(TILES):
                    s, c = m // (2 * NS), (m % (2 * NS)) * 2
                    kind, first = ((1, 0), (0, 1), (1, 0))[s]
                    at = filt_dram.ap().rearrange("r s c t -> (r s c t)")[
                        bass.ds(g * (CG * PAD) + ((kind * STAGES + s) * F + c) * PAD + first, 1)]
                    src = bass.AP(at.tensor, at.offset, [[1, HALF], [PAD, 2], [1, L]])
                    sp.wait_ge(conv_done, g * TILES + m + 1)
                    sp.dma_start(toep[:, m % TR, :, :], src).then_inc(toep_in[m % TR], 16)

        @block.tensor
        def _(pe):
            pe.wait_ge(w_in, 16)
            with pe.Fori(0, NG) as g:
                for n, (o, bg, half) in enumerate(banks()):
                    pe.wait_ge(proj_copied, g * BANKS + n + 1)
                    src = fm_rev if o else fm
                    for b in range(NB):
                        tile = 2 * (bg * NB + b) + half
                        m = pe.matmul(p_p[n % 4][0:HALF, b * 64:(b + 1) * 64], src[:, tile * HALF:(tile + 1) * HALF],
                                      w_proj[:, bass.ds(g, 1), o, :], start=True, stop=True)
                    m.then_inc(proj_done, 1)
                pe.wait_ge(proj_copied, g * BANKS + BANKS + 4)
                for n in range(STEPS):
                    s, q = n // NS, n % NS
                    o, p = place(s)
                    pe.wait_ge(prod_done, g * STEPS + n + 1)
                    for t in range(2):
                        r = 2 * n + t
                        pe.wait_ge(toep_in[r % TR], g * (16 * TILES // TR) + 16 * (r // TR) + 16)
                        for c in range(2):
                            ch = q * QC + 2 * t + c
                            col = (2 * t + c) * B
                            tt = toep[:, r % TR, c, :]
                            near, far = (tt[:, HALF:L], tt[:, 0:HALF]) if s % 2 == 0 else (tt[:, 0:HALF], tt[:, HALF:L])
                            y0 = x[:, o, 0, p, ch * B:(ch + 1) * B]
                            y1 = x[:, o, 1, p, ch * B:(ch + 1) * B]
                            out = p_c[n % 4]
                            pe.matmul(out[0:HALF, col:col + B], near, y0, start=True, stop=True)
                            pe.matmul(out[0:HALF, QC * B + col:QC * B + col + B], far, y0, start=True, stop=False)
                            m = pe.matmul(out[0:HALF, QC * B + col:QC * B + col + B], near, y1, start=False, stop=True)
                        m.then_inc(conv_done, 1)

        @block.scalar
        def _(act):
            act.sem_inc(proj_copied, 4)
            with act.Fori(0, NG) as g:
                for n, (o, bg, half) in enumerate(banks()):
                    if n == 0:
                        act.wait_ge(prod_done, g * STEPS + 4)
                    if n == BANKS // 2:
                        act.wait_ge(att_stored, g + 1)
                    act.wait_ge(proj_done, g * BANKS + n + 1)
                    dst = x[:, o, half, :, :].rearrange("t p (c b) -> t (p c) b", b=B)[:, :, bg * NB:(bg + 1) * NB]
                    src = p_p[n % 4][0:HALF, :].rearrange("t (b k) -> t k b", b=NB)
                    act.activation(dst, src, ACT.Copy).then_inc(proj_copied, 1)

        @block.gpsimd
        def _(pool):
            pool.sem_inc(att_stored, 1)
            with pool.Fori(0, NG) as g:
                pool.wait_ge(prod_done, g * STEPS + STEPS + 4)
                pool.dma_start(att_dram[bass.ds(g, 1), :, :, :].rearrange("o t h n -> (o t) h n"),
                               x[:, 0, :, 0, :]).then_inc(att_out, 16)
                pool.wait_ge(att_out, g * 16 + 16)
                pool.sem_inc(att_stored, 1)

        @block.vector
        def _(dve):
            dve.sem_inc(conv_done, TR)
            dve.sem_inc(prod_done, 4)
            with dve.Fori(0, NG) as g:
                for n in range(STEPS):
                    s, q = n // NS, n % NS
                    o, p = place(s + 1)
                    dve.wait_ge(conv_done, g * TILES + 2 * n + 2 + TR)
                    nxt = x[:, o, :, p, q * QC * B:(q + 1) * QC * B]
                    y = p_c[n % 4][0:HALF, :].rearrange("t (h n) -> t h n", h=2)
                    if s < STAGES - 1:
                        dve.tensor_tensor(nxt, y, nxt, ALU.mult).then_inc(prod_done, 1)
                    else:
                        for half in range(2):
                            dst = x[:, 0, half, 0, :].rearrange("t (b c) -> t c b", b=B)[:, q * QC:(q + 1) * QC, :]
                            m = dve.tensor_tensor(dst, y[:, half, :].rearrange("t (c b) -> t c b", c=QC),
                                                  nxt[:, half, :].rearrange("t (c b) -> t c b", c=QC), ALU.mult)
                        m.then_inc(prod_done, 1)


def attach_norm(nc, k, d, ident, h0_dram, att_dram, h, xf, s_tok):
    ctx = ExitStack()
    with ctx:
        U = 4
        flip = k.sb(ctx, "flip", [HALF, HALF])
        wg0 = k.sb(ctx, "wg0", [F, E])
        h0 = k.sb(ctx, "h0", [HALF, U, QF])
        att = k.sb(ctx, "att", [HALF, U, NG, 2, 2 * CG])
        xn = k.sb(ctx, "xn_d", [HALF, U, QF])
        xt = k.sb(ctx, "xt_d", [F, U, QN])
        lst = k.sb(ctx, "lst_d", [HALF, U, QT, 6])
        lmv = k.sb(ctx, "lmv_d", [HALF, U, QT, 2])
        lve = k.sb(ctx, "lve_d", [HALF, U, QT])
        lrs = k.sb(ctx, "lrs_d", [HALF, U, QT])
        nhalf = k.sb(ctx, "nhalf_d", [HALF, QT])
        p_f = [k.ps(ctx, f"p_f{r}") for r in range(2)]
        p_x = [k.ps(ctx, f"p_xd{u}") for u in range(U)]
        p_l = [k.ps(ctx, f"p_l{r}") for r in range(2)]

        consts = k.sem("consts_d")
        quad_in = [k.sem(f"quad_in{u}") for u in range(U)]
        flipped = k.sem("flipped")
        joined = k.sem("joined")
        var_done = k.sem("var_done_d")
        pool_step = k.sem("pool_step_d")
        dve_step = k.sem("dve_step_d")
        rstd_done = k.sem("rstd_done_d")
        xn_ready = k.sem("xn_ready_d")
        xt_done = k.sem("xt_done_d")
        xt_copied = k.sem("xt_copied_d")
        xf_copied = k.sem("xf_copied")
        log_done = k.sem("log_done")
        log_copied = k.sem("log_copied")
        block = ctx.enter_context(nc.Block())

        @block.sync
        def _(sp):
            sp.dma_start(flip[:, :], d["flip"]).then_inc(consts, 16)
            sp.dma_start(wg0[:, :], d["wg0"]).then_inc(consts, 16)
            with sp.Fori(0, NQ // U) as i:
                for u in range(U):
                    sp.wait_ge(joined, i * U + u + 1)
                    sp.dma_start(h0[:, u, :], h0_dram[:, bass.ds((i * U + u) * QF, QF)]).then_inc(quad_in[u], 16)
                    for g in range(NG):
                        sp.dma_start(att[:, u, g, :, :],
                                     att_dram[g, :, :, bass.ds((i * U + u) * 2 * CG, 2 * CG)]).then_inc(quad_in[u], 16)

        @block.tensor
        def _(pe):
            pe.wait_ge(consts, 32)
            with pe.Fori(0, NQ // U) as i:
                for u in range(U):
                    n = i * U + u
                    pe.wait_ge(quad_in[u], i * 80 + 80)
                    pe.wait_ge(joined, n + 3)
                    for j in range(QT):
                        b, half = j // 2, j % 2
                        m = pe.matmul(p_f[u % 2][0:HALF, j * F:(j + 1) * F], flip[:, :],
                                      att[:, u, :, half, b * CG:(b + 1) * CG], start=True, stop=True)
                    m.then_inc(flipped, 1)
                for u in range(U):
                    n = i * U + u
                    pe.wait_ge(xn_ready, n + 1)
                    pe.wait_ge(xt_copied, n + 1)
                    for j in range(QT):
                        m = pe.transpose(p_x[u][:, j * HALF:(j + 1) * HALF], xn[:, u, j * F:(j + 1) * F],
                                         ident[0:HALF, 0:HALF])
                    m.then_inc(xt_done, 1)
                for u in range(U):
                    n = i * U + u
                    pe.wait_ge(xt_copied, n + 1 + U)
                    pe.wait_ge(log_copied, n + 3)
                    for j in range(QT):
                        m = pe.matmul(p_l[u % 2][0:HALF, j * E:(j + 1) * E], xt[:, u, j * HALF:(j + 1) * HALF],
                                      wg0[:, :], start=True, stop=True)
                    m.then_inc(log_done, 1)

        @block.scalar
        def _(act):
            act.sem_inc(xt_copied, U)
            with act.Fori(0, NQ // U) as i:
                for u in range(U):
                    n = i * U + u
                    act.wait_ge(log_copied, n + 1)
                    act.wait_ge(xf_copied, n + 1)
                    act.wait_ge(xt_done, n + 1)
                    act.activation(xt[:, u, :], p_x[u][:, 0:QN], ACT.Copy).then_inc(xt_copied, 1)

        @block.gpsimd
        def _(pool):
            ch = Chain(pool, pool_step)
            pool.sem_inc(xf_copied, U)
            ch.link(pool.memset(nhalf[:, :], -0.5))
            with pool.Fori(0, NQ // U) as i:
                pc = Chain(pool, pool_step, i, U, 1)
                for u in range(U):
                    pool.wait_ge(var_done, i * U + u + 1)
                    apart(pool)
                    pc.link(pool.tensor_scalar(lve[:, u, :], lmv[:, u, :, 1], EPS, None, ALU.add))
                    pool.tensor_tensor(out=lrs[:, u, :], in0=lve[:, u, :], in1=nhalf[:, :], op=ALU.pow).then_inc(rstd_done, 1)
                for u in range(U):
                    n = i * U + u
                    pool.wait_ge(xt_copied, n + 1 + U)
                    apart(pool)
                    pool.tensor_copy(xf[:, bass.ds(n * QN, QN)], xt[:, u, :]).then_inc(xf_copied, 1)

        @block.vector
        def _(dve):
            dve.sem_inc(joined, U)
            dve.sem_inc(log_copied, U)
            with dve.Fori(0, NQ // U) as i:
                ch = Chain(dve, dve_step, i, U)
                for u in range(U):
                    n = i * U + u
                    dve.wait_ge(flipped, n + 1)
                    apart(dve)
                    dve.tensor_tensor(h[:, bass.ds(n * QF, QF)], p_f[u % 2][0:HALF, :], h0[:, u, :], ALU.add).then_inc(joined, 1)
                    dve.wait_ge(joined, n + 1 + U)
                    apart(dve)
                    for j in range(QT):
                        m = dve.bn_stats(lst[:, u, j, :], h[:, bass.ds(n * QF + j * F, F)])
                    ch.link(m)
                    apart(dve)
                    for j in range(QT):
                        m = dve.bn_aggr(lmv[:, u, j, :], lst[:, u, j, :])
                    m.then_inc(var_done, 1)
                for u in range(U):
                    n = i * U + u
                    dve.wait_ge(rstd_done, n + 1)
                    apart(dve)
                    for j in range(QT):
                        m = dve.tensor_scalar(xn[:, u, j * F:(j + 1) * F], h[:, bass.ds(n * QF + j * F, F)],
                                              lmv[:, u, j, 0:1], lrs[:, u, j:j + 1], ALU.subtract, ALU.mult)
                    m.then_inc(xn_ready, 1)
                for u in range(U):
                    n = i * U + u
                    dve.wait_ge(log_done, n + 1)
                    apart(dve)
                    src = p_l[u % 2][0:HALF, 0:QT * E].rearrange("t (b h e) -> t h b e", b=2, h=2)
                    dve.tensor_copy(s_tok[:, :, bass.ds(n * 2, 2), :], src).then_inc(log_copied, 1)


def choose(nc, k, d, ident, h, s_tok, g_tok):
    ctx = ExitStack()
    with ctx:
        BG = 16
        NBG = B // BG
        mx = k.sb(ctx, "mx", [HALF, NT])
        st = k.sb(ctx, "st", [128, NBG, L])
        work = k.sb(ctx, "work", [128, NBG, L])
        m8 = k.sb(ctx, "m8", [128, NBG, 8])
        above = k.sb(ctx, "above", [128, NBG, L])
        equal = k.sb(ctx, "equal", [128, NBG, L])
        rank = k.sb(ctx, "rank", [128, NBG, L])
        gate = k.sb(ctx, "gate", [128, NBG, L])
        ones = k.sb(ctx, "ones_e", [128, L])
        count = k.sb(ctx, "count", [128, NBG])
        room = k.sb(ctx, "room", [128, NBG])
        b2d = k.sb(ctx, "b2d", [128, BG * F])
        p_s = [k.ps(ctx, f"p_s{r}") for r in range(2)]
        p_g = [k.ps(ctx, f"p_g{r}") for r in range(2)]
        p_b = [k.ps(ctx, f"p_b{r}") for r in range(4)]

        dve_step = k.sem("dve_step_e")
        shifted = k.sem("shifted")
        exps = k.sem("exps")
        probs = k.sem("probs")
        s_t = k.sem("s_t")
        gates = k.sem("gates")
        g_t = k.sem("g_t")
        b2_zero = k.sem("b2_zero")
        b2_in = k.sem("b2_in")
        b2_done = k.sem("b2_done")
        b2_added = k.sem("b2_added")
        block = ctx.enter_context(nc.Block())
        s_flat = s_tok[:, :, :, :].rearrange("t h b e -> t (h b) e")

        @block.sync
        def _(sp):
            sp.wait_ge(b2_zero, 1)
            for b in range(BG):
                sp.dma_start(b2d[b * E:(b + 1) * E, b * F:(b + 1) * F], d["b2_0"]).then_inc(b2_in, 16)
            sp.wait_ge(b2_in, 16 * BG)

        @block.gpsimd
        def _(pool):
            pool.memset(b2d[:, :], 0.0).then_inc(b2_zero, 1)

        @block.scalar
        def _(act):
            act.wait_ge(shifted, 1)
            act.activation(s_flat, s_flat, ACT.Exp).then_inc(exps, 1)

        @block.tensor
        def _(pe):
            pe.wait_ge(probs, 1)
            for g in range(NBG):
                for half in range(2):
                    col = (g % 2) * L + half * HALF
                    m = pe.transpose(p_s[g // 2][:, col:col + HALF],
                                     s_tok[:, half, g * BG:(g + 1) * BG, :].rearrange("t b e -> t (b e)"),
                                     ident[0:HALF, 0:HALF])
                if g % 2:
                    m.then_inc(s_t, 1)
            pe.wait_ge(gates, NBG)
            for half in range(2):
                for g in range(NBG):
                    m = pe.transpose(p_g[half][0:HALF, g * 128:(g + 1) * 128], gate[:, g, half * HALF:(half + 1) * HALF],
                                     ident[:, :])
                m.then_inc(g_t, 1)
            pe.wait_ge(b2_in, 16 * BG)
            for n in range(2 * NBG * 4):
                g, half, sub = n // 8, n // 4 % 2, n % 4
                if n >= 4:
                    pe.wait_ge(b2_added, n - 3)
                pe.matmul(p_b[n % 4][0:HALF, :], gate[:, g, half * HALF:(half + 1) * HALF],
                          b2d[:, sub * 4 * F:(sub + 1) * 4 * F], start=True, stop=True).then_inc(b2_done, 1)

        @block.vector
        def _(dve):
            ch = Chain(dve, dve_step)
            ch.link(dve.tensor_reduce(mx[:, :], s_flat, AX.X, ALU.max))
            dve.tensor_tensor(s_flat, s_flat, mx[:, :].unsqueeze(2).to_broadcast([HALF, NT, E]), ALU.subtract).then_inc(shifted, 1)
            dve.wait_ge(exps, 1)
            ch.link(dve.tensor_reduce(mx[:, :], s_flat, AX.X, ALU.add))
            ch.link(dve.reciprocal(mx[:, :], mx[:, :]))
            dve.tensor_tensor(s_flat, s_flat, mx[:, :].unsqueeze(2).to_broadcast([HALF, NT, E]), ALU.mult).then_inc(probs, 1)
            ch.link(dve.memset(ones[:, :], 1.0))
            for r in range(NBG // 2):
                dve.wait_ge(s_t, r + 1)
                ch.link(dve.tensor_copy(st[:, 2 * r:2 * r + 2, :], p_s[r][:, 0:2 * L].rearrange("p (g t) -> p g t", g=2)))
            rounds = (TOPK + 7) // 8
            for r in range(rounds):
                for g in range(NBG):
                    m = dve.max(m8[:, g, :], (st if r == 0 else work)[:, g, :])
                ch.link(m)
                if r < rounds - 1:
                    for g in range(NBG):
                        m = dve.match_replace(work[:, g, :], m8[:, g, :], (st if r == 0 else work)[:, g, :], -1.0)
                    ch.link(m)
            at = TOPK - 1 - 8 * (rounds - 1)
            for g in range(NBG):
                kth = m8[:, g, at:at + 1]
                dve.tensor_scalar(above[:, g, :], st[:, g, :], kth, None, ALU.is_gt, ALU.add, accum_out=count[:, g:g + 1])
                m = dve.tensor_scalar(equal[:, g, :], st[:, g, :], kth, None, ALU.is_equal)
            ch.link(m)
            ch.link(dve.tensor_scalar(room[:, :], count[:, :], -1.0, float(TOPK), ALU.mult, ALU.add))
            for g in range(NBG):
                m = dve.tensor_tensor_scan(rank[:, g, :], ones[:, :], equal[:, g, :], 0.0, ALU.mult, ALU.add)
            ch.link(m)
            for g in range(NBG):
                m = dve.scalar_tensor_tensor(work[:, g, :], rank[:, g, :], room[:, g:g + 1], equal[:, g, :], ALU.is_le, ALU.mult)
            ch.link(m)
            ch.link(dve.tensor_tensor(above[:, :, :], above[:, :, :], work[:, :, :], ALU.add))
            dve.tensor_tensor(gate[:, :, :], above[:, :, :], st[:, :, :], ALU.mult).then_inc(gates, NBG)
            for half in range(2):
                dve.wait_ge(g_t, half + 1)
                dve.tensor_copy(g_tok[:, half, :, :].rearrange("t b e -> t (b e)"), p_g[half][0:HALF, :])
            for n in range(2 * NBG * 4):
                g, half, sub = n // 8, n // 4 % 2, n % 4
                tiles = h[:, :].rearrange("t (b h f) -> t h b f", h=2, f=F)[:, half, g * BG + sub * 4:g * BG + sub * 4 + 4, :]
                dve.wait_ge(b2_done, n + 1)
                dve.tensor_tensor(tiles, p_b[n % 4][0:HALF, :].rearrange("t (b f) -> t b f", b=4), tiles, ALU.add).then_inc(b2_added, 1)
            dve.wait_ge(b2_added, 2 * NBG * 4)


def mixture0(nc, k, d, h, xf, g_tok):
    ctx = ExitStack()
    with ctx:
        CH = F0 // F
        w1 = k.sb(ctx, "w1_0", [F, E, F0])
        w2 = k.sb(ctx, "w2_0", [F, E, CH, F])
        b1 = k.sb(ctx, "b1_0", [F, E, CH])
        hid = k.sb(ctx, "hid", [F, 4, CH, QN])
        gq = k.sb(ctx, "gq", [HALF, 2, 2, E])
        acc = k.sb(ctx, "acc", [HALF, QF])
        p_1 = [[k.ps(ctx, f"p_1{r}{c}") for c in range(CH)] for r in range(2)]
        p_2 = [k.ps(ctx, f"p_2{r}") for r in range(4)]

        w_in = k.sem("w_in_f")
        w1_done = k.sem("w1_done")
        gelu_done = k.sem("gelu_done")
        w2_done = k.sem("w2_done")
        acc_done = k.sem("acc_done")
        gq_copied = k.sem("gq_copied")
        block = ctx.enter_context(nc.Block())

        @block.sync
        def _(sp):
            sp.dma_start(w1[:, :, :], d["w1_0"]).then_inc(w_in, 16)
            sp.dma_start(b1[:, :, :], d["b1_0"]).then_inc(w_in, 16)
            sp.dma_start(w2[:, :, :, :], d["w2_0"]).then_inc(w_in, 16)

        @block.tensor
        def _(pe):
            pe.wait_ge(w_in, 48)

            def down(n, e):
                pe.wait_ge(gelu_done, n * 2 + 2 + 4)
                pe.wait_ge(acc_done, n + 1)
                for j in range(QT):
                    for c in range(CH):
                        m = pe.matmul(p_2[e % 4][0:HALF, j * F:(j + 1) * F], hid[:, e % 4, c, j * HALF:(j + 1) * HALF],
                                      w2[:, e, c, :], start=(c == 0), stop=(c == CH - 1))
                m.then_inc(w2_done, 1)

            with pe.Fori(0, NQ) as i:
                for e in range(E):
                    n = i * E + e
                    pe.wait_ge(gelu_done, n * 2 + 2)
                    for c in range(CH):
                        pe.matmul(p_1[e % 2][c][:, 0:QN], w1[:, e, c * F:(c + 1) * F], xf[:, bass.ds(i * QN, QN)],
                                  start=True, stop=True).then_inc(w1_done, 1)
                    if e:
                        down(n - 1, e - 1)
                down(i * E + E - 1, E - 1)

        @block.scalar
        def _(act):
            act.sem_inc(gelu_done, 4)
            act.wait_ge(w_in, 48)
            with act.Fori(0, NQ) as i:
                for e in range(E):
                    n = i * E + e
                    act.wait_ge(w2_done, n + 1)
                    for c in range(CH):
                        act.wait_ge(w1_done, n * 2 + c + 1)
                        act.activation(hid[:, e % 4, c, :], p_1[e % 2][c][:, 0:QN], ACT.Gelu,
                                       bias=b1[:, e, c:c + 1]).then_inc(gelu_done, 1)

        @block.vector
        def _(dve):
            dve.sem_inc(w2_done, 4)
            dve.sem_inc(acc_done, 4)
            with dve.Fori(0, NQ) as i:
                dve.wait_ge(acc_done, i * E + 4)
                apart(dve)
                dve.tensor_copy(gq[:, :, :, :], g_tok[:, :, bass.ds(i * 2, 2), :]).then_inc(gq_copied, 1)
                dve.wait_ge(gq_copied, i + 1)
                for e in range(E):
                    n = i * E + e
                    dve.wait_ge(acc_done, n + 4)
                    dve.wait_ge(w2_done, n + 1 + 4)
                    apart(dve)
                    for j in range(QT):
                        at = bass.ds(i * QF + j * F, F)
                        a = acc[:, j * F:(j + 1) * F]
                        m = dve.scalar_tensor_tensor(h[:, at] if e == E - 1 else a, p_2[e % 4][0:HALF, j * F:(j + 1) * F],
                                                     gq[:, j % 2, j // 2, e:e + 1], h[:, at] if e == 0 else a,
                                                     ALU.mult, ALU.add)
                    m.then_inc(acc_done, 1)


def retain_and_route(nc, k, d, ident, small, h, base, xs_dram, h3_dram):
    ctx = ExitStack()
    with ctx:
        W = 3 * HALF
        wq = k.sb(ctx, "wq", [F, F])
        wk = k.sb(ctx, "wk", [F, F])
        wvg = k.sb(ctx, "wvg", [F, 2 * F])
        bvg = k.sb(ctx, "bvg", [HALF, 2 * F])
        wg1 = k.sb(ctx, "wg1", [F, E])
        bg1 = k.sb(ctx, "bg1", [HALF, E])
        prio = k.sb(ctx, "prio", [HALF, E])
        before_f = k.sb(ctx, "before_f", [HALF, HALF])
        before = k.sb(ctx, "before", [HALF, HALF], BF16)
        ones = k.sb(ctx, "ones_g", [HALF, HALF], BF16)
        decay = k.sb(ctx, "decay", [HALF, HEADS, W])
        nhalf = k.sb(ctx, "nhalf_g", [HALF, QT])

        def norm_buffers(name):
            return (k.sb(ctx, "lst_" + name, [HALF, 2, QT, 6]), k.sb(ctx, "lmv_" + name, [HALF, 2, QT, 2]),
                    k.sb(ctx, "lve_" + name, [HALF, 2, QT]), k.sb(ctx, "lrs_" + name, [HALF, 2, QT]))

        prep_norm = norm_buffers("p")
        route_norm = norm_buffers("r")
        xn = k.sb(ctx, "xn_g", [HALF, 2, QF])
        xt = k.sb(ctx, "xt_g", [F, 2, QN])
        q_even = k.sb(ctx, "q_even", [F, 2, QN])
        q_odd = k.sb(ctx, "q_odd", [F, 2, QN])
        kt = k.sb(ctx, "kt", [F, 2, QN])
        vg = k.sb(ctx, "vg", [HALF, 2, QT, 2 * F])
        silu = k.sb(ctx, "silu", [HALF, 2, QF])
        probs = k.sb(ctx, "probs_g", [HALF, 4, W])
        gated = k.sb(ctx, "gated", [HALF, QF])
        h3 = k.sb(ctx, "h3", [HALF, 2, QF])
        xr = k.sb(ctx, "xr", [HALF, 2, QF])
        xrt = k.sb(ctx, "xrt", [F, QN])
        xs = k.sb(ctx, "xs", [HALF, 2, QF])
        lg = k.sb(ctx, "lg", [HALF, QT, E])
        ez = k.sb(ctx, "ez", [HALF, QT, E])
        eq = k.sb(ctx, "eq", [HALF, QT, E])
        hot = k.sb(ctx, "hot", [HALF, QT, E], BF16)
        pz = k.sb(ctx, "pz", [HALF, QT, E])
        r4 = k.sb(ctx, "r4", [HALF, 6, QT])
        idx = k.sb(ctx, "idx", [HALF, 2, QT], I32)
        p_a = k.ps(ctx, "p_a")
        p_b = k.ps(ctx, "p_bq")
        p_s = [k.ps(ctx, f"p_sc{r}") for r in range(2)]
        p_o = [k.ps(ctx, f"p_o{u}") for u in range(2)]
        p_r = k.ps(ctx, "p_r")
        p_l = k.ps(ctx, "p_lr")

        consts = k.sem("consts_g")
        set_up = k.sem("set_up")
        prep_step = k.sem("prep_step")
        route_step = k.sem("route_step")
        pool_prep = k.sem("pool_prep")
        pool_route = k.sem("pool_route")
        var_p = k.sem("var_p")
        var_r = k.sem("var_r")
        rstd_p = k.sem("rstd_p")
        rstd_r = k.sem("rstd_r")
        xn_ready = k.sem("xn_ready_g")
        xt_done = k.sem("xt_done_g")
        xt_copied = k.sem("xt_copied_g")
        q_done = k.sem("q_done")
        q_copied = k.sem("q_copied")
        k_done = k.sem("k_done")
        k_copied = k.sem("k_copied")
        vg_done = k.sem("vg_done")
        v_added = k.sem("v_added")
        silu_done = k.sem("silu_done")
        s_done = k.sem("s_done")
        decayed = k.sem("decayed")
        av_done = k.sem("av_done")
        h3_done = k.sem("h3_done")
        h3_out = [k.sem(f"h3_out{u}") for u in range(2)]
        xr_ready = k.sem("xr_ready")
        xr_done = k.sem("xr_done")
        xr_copied = k.sem("xr_copied")
        lg_done = k.sem("lg_done")
        z_ready = k.sem("z_ready")
        ez_done = k.sem("ez_done")
        hot_ready = k.sem("hot_ready")
        pre_done = k.sem("pre_done")
        idx_done = k.sem("idx_done")
        sent = [k.sem(f"sent{u}") for u in range(2)]
        xs_free = k.sem("xs_free")
        block = ctx.enter_context(nc.Block())

        NH = 2 * HEADS
        HEAD = [2 * (n % 4) + n // 4 % 2 for n in range(NH)]

        @block.sync
        def _(sp):
            for name, to in (("wq", wq), ("wk", wk), ("wvg", wvg), ("wg1", wg1), ("before", before_f)):
                sp.dma_start(to[:, :], d[name]).then_inc(consts, 16)
            sp.dma_start(decay[:, :, :], d["decay"]).then_inc(consts, 16)
            for name, to, n in (("bvg", bvg, 2 * F), ("bg1", bg1, E), ("prio", prio, E), ("region", base, E)):
                sp.dma_start(to[:, :], bass.AP(d[name].tensor, 0, [[0, HALF], [1, n]])).then_inc(consts, 16)

            def store(q, u):
                sp.wait_ge(h3_done, q + 1 + 2)
                dst = h3_dram[bass.ds(q * QN, QN), :].rearrange("(j t) f -> t j f", j=QT)
                sp.dma_start(dst, h3[:, u, :].rearrange("t (j f) -> t j f", j=QT)).then_inc(h3_out[u], 16)

            with sp.Fori(0, NQ // 2) as j:
                for u in range(2):
                    store(j * 2 + u, u)
            for u in range(2):
                sp.wait_ge(h3_out[u], 16 * (NQ // 2 + 1))

        @block.tensor
        def _(pe):
            pe.wait_ge(consts, 160)
            pe.wait_ge(set_up, 3)

            def prep_x(q, u):
                pe.wait_ge(xn_ready, q + 1)
                pe.wait_ge(v_added, q * 2 + 2)
                for j in range(QT):
                    m = pe.transpose(p_a[:, j * HALF:(j + 1) * HALF], xn[:, u, j * F:(j + 1) * F], ident[0:HALF, 0:HALF])
                m.then_inc(xt_done, 1)

            def prep_q(q, u):
                pe.wait_ge(xt_copied, q + 1)
                pe.matmul(p_b[:, 0:QN], wq[:, :], xt[:, u, :], start=True, stop=True).then_inc(q_done, 1)

            def prep_k(q, u):
                pe.matmul(p_a[:, 0:QN], wk[:, :], xt[:, u, :], start=True, stop=True).then_inc(k_done, 1)

            def prep_v(q, u):
                pe.wait_ge(q_copied, q * 2 + 2)
                for b in range(2):
                    if b:
                        pe.wait_ge(k_copied, q + 1)
                    for half in range(2):
                        j = 2 * b + half
                        m = pe.matmul((p_b, p_a)[b][0:HALF, half * 2 * F:(half + 1) * 2 * F],
                                      xt[:, u, j * HALF:(j + 1) * HALF], wvg[:, :], start=True, stop=True)
                    m.then_inc(vg_done, 1)

            def scores(q, u, n):
                if n == 0:
                    pe.wait_ge(q_copied, q * 2 + 2)
                    pe.wait_ge(k_copied, q + 1)
                pe.wait_ge(decayed, q * NH + n + 1)
                b, head = n // HEADS, HEAD[n]
                rows = slice(head // 2 * 32, head // 2 * 32 + 32)
                qq = (q_even, q_odd)[head % 2]
                at = b * L
                pe.matmul(p_s[n % 2][0:HALF, 0:HALF], kt[rows, u, at:at + HALF], qq[rows, u, at:at + HALF],
                          start=True, stop=True)
                pe.matmul(p_s[n % 2][0:HALF, HALF:W], kt[rows, u, at + HALF:at + L], qq[rows, u, at:at + L],
                          start=True, stop=True).then_inc(s_done, 1)

            def values(q, u, n):
                if n == 0:
                    pe.wait_ge(h3_done, q + 1)
                    pe.wait_ge(v_added, q * 2 + 2 + 2)
                pe.wait_ge(decayed, q * NH + n + 1 + 2)
                b, head = n // HEADS, HEAD[n]
                pr = probs[:, n % 4, :]
                hd = slice(head * HD, (head + 1) * HD)
                to = [p_o[u][0:HALF, (2 * b + half) * F + head * HD:(2 * b + half) * F + (head + 1) * HD] for half in range(2)]
                pe.matmul(to[0], pr[:, 0:HALF], vg[:, u, 2 * b, hd], start=True, stop=False)
                pe.matmul(to[0], pr[:, HALF:2 * HALF], vg[:, u, 2 * b + 1, hd], start=False, stop=True)
                pe.matmul(to[1], pr[:, 2 * HALF:W], vg[:, u, 2 * b + 1, hd], start=True, stop=True).then_inc(av_done, 1)

            def route_x(q, u):
                pe.wait_ge(xr_ready, q + 1)
                pe.wait_ge(xr_copied, q + 1)
                for j in range(QT):
                    m = pe.transpose(p_r[:, j * HALF:(j + 1) * HALF], xr[:, u, j * F:(j + 1) * F], ident[0:HALF, 0:HALF])
                m.then_inc(xr_done, 1)

            def route_logits(q):
                pe.wait_ge(xr_copied, q + 2)
                pe.wait_ge(idx_done, q + 1)
                for j in range(QT):
                    m = pe.matmul(p_l[0:HALF, j * E:(j + 1) * E], xrt[:, j * HALF:(j + 1) * HALF], wg1[:, :],
                                  start=True, stop=True)
                m.then_inc(lg_done, 1)

            def route_places(q):
                pe.wait_ge(hot_ready, q + 1)
                for j in range(QT + 1):
                    to = p_l[0:HALF, (QT + j) * E:(QT + j + 1) * E]
                    if j < QT:
                        m = pe.matmul(to, before[:, :], hot[:, j, :], start=True, stop=(j == 0))
                    for i in range(j):
                        m = pe.matmul(to, ones[:, :], hot[:, i, :], start=(j == QT and i == 0), stop=(i == j - 1))
                m.then_inc(pre_done, 1)

            def quad(q, u, prep, route):
                for n in range(NH):
                    scores(q, u, n)
                    if n:
                        values(q, u, n - 1)
                    if prep:
                        if n == 5:
                            prep_x(q + 1, 1 - u)
                        if n == 8:
                            prep_q(q + 1, 1 - u)
                        if n == 9:
                            prep_k(q + 1, 1 - u)
                        if n == 12:
                            prep_v(q + 1, 1 - u)
                    if route:
                        if n == 6:
                            route_x(q - 1, 1 - u)
                        if n == 10:
                            route_logits(q - 1)
                values(q, u, NH - 1)
                if route:
                    route_places(q - 1)

            prep_x(0, 0)
            prep_q(0, 0)
            prep_k(0, 0)
            prep_v(0, 0)
            quad(0, 0, True, False)
            quad(1, 1, True, True)
            with pe.Fori(1, NQ // 2 - 1) as t:
                quad(t * 2, 0, True, True)
                quad(t * 2 + 1, 1, True, True)
            quad(NQ - 2, 0, True, True)
            quad(NQ - 1, 1, False, True)
            route_x(NQ - 1, 1)
            route_logits(NQ - 1)
            route_places(NQ - 1)

        @block.scalar
        def _(act):
            act.sem_inc(xr_copied, 1)
            for u in range(2):
                act.sem_inc(h3_out[u], 16)
            act.wait_ge(set_up, 3)

            def prep_x(q, u):
                act.wait_ge(vg_done, q * 2 + 2)
                act.wait_ge(xt_done, q + 1 + 2)
                act.activation(xt[:, u, :], p_a[:, 0:QN], ACT.Copy).then_inc(xt_copied, 1)

            def prep_qk(q, u):
                act.wait_ge(s_done, q * NH + NH)
                act.wait_ge(q_done, q + 1)
                act.activation(q_even[:, u, :], p_b[:, 0:QN], ACT.Identity, bias=small[:, 6:7], scale=small[:, 2:3]).then_inc(q_copied, 1)
                act.activation(q_odd[:, u, :], p_b[:, 0:QN], ACT.Identity, bias=small[:, 7:8], scale=small[:, 3:4]).then_inc(q_copied, 1)
                act.wait_ge(k_done, q + 1)
                act.activation(kt[:, u, :], p_a[:, 0:QN], ACT.Identity, bias=small[:, 5:6]).then_inc(k_copied, 1)

            def prep_silu(q, u):
                act.wait_ge(h3_done, q + 1)
                act.wait_ge(v_added, q * 2 + 2 + 2)
                act.activation(silu[:, u, :].rearrange("t (j f) -> t j f", j=QT), vg[:, u, :, F:2 * F], ACT.Silu).then_inc(silu_done, 1)

            def route_x(q):
                act.wait_ge(lg_done, q + 1)
                act.wait_ge(xr_done, q + 1 + 2)
                act.activation(xrt[:, :], p_r[:, 0:QN], ACT.Copy).then_inc(xr_copied, 1)

            def route_exp(q):
                act.wait_ge(z_ready, q + 1)
                act.activation(ez[:, :, :], lg[:, :, :], ACT.Exp).then_inc(ez_done, 1)

            def quad(q, u, prep, route):
                if prep:
                    prep_x(q + 1, 1 - u)
                if route:
                    route_x(q - 1)
                if prep:
                    prep_qk(q + 1, 1 - u)
                if route:
                    route_exp(q - 1)
                if prep:
                    prep_silu(q + 1, 1 - u)

            prep_x(0, 0)
            prep_qk(0, 0)
            prep_silu(0, 0)
            quad(0, 0, True, False)
            quad(1, 1, True, True)
            with act.Fori(1, NQ // 2 - 1) as t:
                quad(t * 2, 0, True, True)
                quad(t * 2 + 1, 1, True, True)
            quad(NQ - 2, 0, True, True)
            quad(NQ - 1, 1, False, True)
            route_x(NQ - 1)
            route_exp(NQ - 1)

        @block.gpsimd
        def _(pool):
            pool.memset(nhalf[:, :], -0.5).then_inc(set_up, 1)
            pool.wait_ge(set_up, 3)

            def rstd(q, u, var, bufs, step, done):
                _, lmv, lve, lrs = bufs
                pool.wait_ge(var, q + 1)
                apart(pool)
                ch = Chain(pool, step, q, 1)
                ch.link(pool.tensor_scalar(lve[:, u, :], lmv[:, u, :, 1], EPS, None, ALU.add))
                pool.tensor_tensor(out=lrs[:, u, :], in0=lve[:, u, :], in1=nhalf[:, :], op=ALU.pow).then_inc(done, 1)

            def send(q, u, t):
                if not (isinstance(q, int) and q == 0):
                    pool.wait_ge(sent[1 - u], (t + u) * 64)
                    pool.sem_inc(xs_free, 1)
                pool.wait_ge(idx_done, q + 2)
                apart(pool)
                for j in range(QT):
                    pool.indirect_dma_start(xs_dram[:, :], bass.IndirectOffsetOnAxis(ap=idx[:, u, j:j + 1], axis=0),
                                            xs[:, u, j * F:(j + 1) * F], None).then_inc(sent[u], 16)

            def quad(q, u, t, prep, route):
                if route:
                    rstd(q - 1, 1 - u, var_r, route_norm, pool_route, rstd_r)
                if prep:
                    rstd(q + 1, 1 - u, var_p, prep_norm, pool_prep, rstd_p)
                if route:
                    send(q - 1, 1 - u, t - 1 if u == 0 else t)

            rstd(0, 0, var_p, prep_norm, pool_prep, rstd_p)
            quad(0, 0, 0, True, False)
            quad(1, 1, 0, True, True)
            with pool.Fori(1, NQ // 2 - 1) as t:
                quad(t * 2, 0, t, True, True)
                quad(t * 2 + 1, 1, t, True, True)
            quad(NQ - 2, 0, NQ // 2 - 1, True, True)
            quad(NQ - 1, 1, NQ // 2 - 1, False, True)
            rstd(NQ - 1, 1, var_r, route_norm, pool_route, rstd_r)
            send(NQ - 1, 1, NQ // 2 - 1)
            for u in range(2):
                pool.wait_ge(sent[u], 64 * (NQ // 2))

        @block.vector
        def _(dve):
            for s, n in ((xt_done, 2), (vg_done, 4), (v_added, 2), (s_done, 32), (decayed, 2), (av_done, 32),
                         (h3_done, 2), (xr_done, 2), (lg_done, 1), (idx_done, 1), (xs_free, 2)):
                dve.sem_inc(s, n)
            dve.wait_ge(consts, 160)
            dve.tensor_copy(before[:, :], before_f[:, :])
            dve.memset(ones[:, :], 1.0)
            dve.tensor_tensor(small[:, 6:7], small[:, 4:5], small[:, 2:3], ALU.mult).then_inc(set_up, 1)
            dve.tensor_tensor(small[:, 7:8], small[:, 4:5], small[:, 3:4], ALU.mult).then_inc(set_up, 1)

            def stats(ch, u, bufs, src, var):
                lst, lmv, _, _ = bufs
                for j in range(QT):
                    m = dve.bn_stats(lst[:, u, j, :], src(j))
                ch.link(m)
                apart(dve)
                for j in range(QT):
                    m = dve.bn_aggr(lmv[:, u, j, :], lst[:, u, j, :])
                m.then_inc(var, 1)

            def normed(u, bufs, src, to):
                _, lmv, _, lrs = bufs
                for j in range(QT):
                    m = dve.tensor_scalar(to[:, u, j * F:(j + 1) * F], src(j), lmv[:, u, j, 0:1], lrs[:, u, j:j + 1],
                                          ALU.subtract, ALU.mult)
                return m

            def prep_stats(q, u):
                stats(Chain(dve, prep_step, q, 1), u, prep_norm, lambda j: h[:, bass.ds(q * QF + j * F, F)], var_p)

            def prep_xn(q, u):
                dve.wait_ge(xt_done, q + 1)
                dve.wait_ge(rstd_p, q + 1)
                apart(dve)
                normed(u, prep_norm, lambda j: h[:, bass.ds(q * QF + j * F, F)], xn).then_inc(xn_ready, 1)

            def prep_vg(q, u):
                dve.wait_ge(av_done, q * NH + NH)
                for b in range(2):
                    dve.wait_ge(vg_done, q * 2 + b + 1 + 4)
                    src = (p_b, p_a)[b][0:HALF, :].rearrange("t (j n) -> t j n", j=2)
                    dve.tensor_tensor(vg[:, u, 2 * b:2 * b + 2, :], src,
                                      bvg[:, :].unsqueeze(1).to_broadcast([HALF, 2, 2 * F]), ALU.add).then_inc(v_added, 1)

            def decaying(q, n):
                dve.wait_ge(av_done, q * NH + n + 29)
                dve.wait_ge(s_done, q * NH + n + 1 + 32)
                dve.tensor_tensor(probs[:, n % 4, :], p_s[n % 2][0:HALF, 0:W], decay[:, HEAD[n], :], ALU.mult).then_inc(decayed, 1)

            def finish(ch, q, u, t):
                dve.wait_ge(av_done, q * NH + NH + 32)
                dve.wait_ge(silu_done, q + 1)
                ch.link(dve.tensor_tensor(gated[:, :], p_o[u][0:HALF, :], silu[:, u, :], ALU.mult))
                dve.wait_ge(h3_out[u], t * 16 + 16)
                apart(dve)
                dve.tensor_tensor(h3[:, u, :], gated[:, :], h[:, bass.ds(q * QF, QF)], ALU.add).then_inc(h3_done, 1)
                dve.wait_ge(h3_done, q + 1 + 2)
                stats(ch, u, route_norm, lambda j: h3[:, u, j * F:(j + 1) * F], var_r)

            def route_xn(q, u):
                dve.wait_ge(xr_done, q + 1)
                dve.wait_ge(rstd_r, q + 1)
                normed(u, route_norm, lambda j: h3[:, u, j * F:(j + 1) * F], xr).then_inc(xr_ready, 1)

            def over_e(r):
                return r4[:, r, :].unsqueeze(2).to_broadcast([HALF, QT, E])

            def over_j(c):
                return c[:, :].unsqueeze(1).to_broadcast([HALF, QT, E])

            def logits(ch, q):
                dve.wait_ge(lg_done, q + 1 + 1)
                ch.link(dve.tensor_tensor(lg[:, :, :], p_l[0:HALF, 0:QT * E].rearrange("t (j e) -> t j e", j=QT), over_j(bg1), ALU.add))
                ch.link(dve.tensor_reduce(r4[:, 0, :], lg[:, :, :], AX.X, ALU.max))
                dve.tensor_tensor(lg[:, :, :], lg[:, :, :], over_e(0), ALU.subtract).then_inc(z_ready, 1)

            def choice(ch, q, u):
                dve.wait_ge(ez_done, q + 1)
                dve.tensor_reduce(r4[:, 1, :], ez[:, :, :], AX.X, ALU.add)
                ch.link(dve.tensor_reduce(r4[:, 2, :], ez[:, :, :], AX.X, ALU.max))
                dve.reciprocal(r4[:, 3, :], r4[:, 1, :])
                ch.link(dve.tensor_tensor(eq[:, :, :], ez[:, :, :], over_e(2), ALU.is_equal))
                dve.tensor_tensor(r4[:, 4, :], r4[:, 2, :], r4[:, 3, :], ALU.mult)
                ch.link(dve.tensor_tensor(eq[:, :, :], eq[:, :, :], over_j(prio), ALU.mult))
                ch.link(dve.tensor_reduce(r4[:, 5, :], eq[:, :, :], AX.X, ALU.max))
                dve.tensor_tensor(hot[:, :, :], eq[:, :, :], over_e(5), ALU.is_equal).then_inc(hot_ready, 1)
                dve.wait_ge(xs_free, q + 1)
                dve.tensor_tensor(xs[:, u, :].rearrange("t (j f) -> t j f", j=QT), xr[:, u, :].rearrange("t (j f) -> t j f", j=QT),
                                  r4[:, 4, :].unsqueeze(2).to_broadcast([HALF, QT, F]), ALU.mult)

            def places(ch, q, u):
                dve.wait_ge(pre_done, q + 1)
                pl = p_l[0:HALF, QT * E:(2 * QT + 1) * E]
                ch.link(dve.tensor_tensor(pz[:, :, :], pl[:, 0:QT * E].rearrange("t (j e) -> t j e", j=QT), over_j(base), ALU.add))
                dve.tensor_tensor(base[:, :], pl[:, QT * E:(QT + 1) * E], base[:, :], ALU.add)
                ch.link(dve.tensor_tensor(pz[:, :, :], pz[:, :, :], hot[:, :, :], ALU.mult))
                ch.link(dve.tensor_reduce(r4[:, 0, :], pz[:, :, :], AX.X, ALU.add))
                dve.tensor_copy(idx[:, u, :], r4[:, 0, :]).then_inc(idx_done, 1)

            ROUTE_LINKS = 11

            def quad(q, u, t, prep, route):
                if route:
                    ch = Chain(dve, route_step, q - 1, ROUTE_LINKS)
                    finish(ch, q - 1, 1 - u, t - 1 if u == 0 else t)
                if prep:
                    prep_stats(q + 1, 1 - u)
                for n in range(NH):
                    decaying(q, n)
                    if prep and n == 2:
                        prep_xn(q + 1, 1 - u)
                    if route and n == 2:
                        route_xn(q - 1, 1 - u)
                    if route and n == 10:
                        logits(ch, q - 1)
                    if route and n == 12:
                        choice(ch, q - 1, 1 - u)
                    if prep and n == 13:
                        prep_vg(q + 1, 1 - u)
                if route:
                    places(ch, q - 1, 1 - u)
                    assert ch.n == ROUTE_LINKS

            prep_stats(0, 0)
            prep_xn(0, 0)
            prep_vg(0, 0)
            quad(0, 0, 0, True, False)
            quad(1, 1, 0, True, True)
            with dve.Fori(1, NQ // 2 - 1) as t:
                quad(t * 2, 0, t, True, True)
                quad(t * 2 + 1, 1, t, True, True)
            quad(NQ - 2, 0, NQ // 2 - 1, True, True)
            quad(NQ - 1, 1, NQ // 2 - 1, False, True)
            ch = Chain(dve, route_step, NQ - 1, ROUTE_LINKS)
            finish(ch, NQ - 1, 1, NQ // 2 - 1)
            route_xn(NQ - 1, 1)
            logits(ch, NQ - 1)
            choice(ch, NQ - 1, 1)
            places(ch, NQ - 1, 1)


def plan_tiles(nc, k, d, base, tab, xs_dram, h3_dram):
    ctx = ExitStack()
    with ctx:
        zeros = k.sb(ctx, "zeros", [128, RB // 128 * F])
        v = k.sb(ctx, "v_h", [1, 10, E])
        vi = k.sb(ctx, "vi_h", [1, 3, E], I32)
        kk = k.sb(ctx, "kk", [1, NK, E])
        a = k.sb(ctx, "a_h", [1, NK, E])
        ind = k.sb(ctx, "ind", [1, NK, E])
        val = k.sb(ctx, "val", [1, 2, NK, E])
        tf = k.sb(ctx, "tf", [1, 3, NK])
        consts = k.sem("consts_h")
        zero_set = k.sem("zero_set")
        ends_ready = k.sem("ends_ready")
        zero_out = k.sem("zero_out")
        step = k.sem("step_h")
        block = ctx.enter_context(nc.Block())

        @block.gpsimd
        def _(pool):
            pool.memset(zeros[:, :], 0.0).then_inc(zero_set, 1)

        def rows(ap):
            return ap.rearrange("(p r) f -> p (r f)", p=128)

        @block.sync
        def _(sp):
            sp.dma_start(kk[:, :, :], d["kk"]).then_inc(consts, 16)
            sp.dma_start(v[:, 8, :], d["region"]).then_inc(consts, 16)
            sp.dma_start(v[:, 9, :], d["number"]).then_inc(consts, 16)
            sp.wait_ge(zero_set, 1)
            sp.dma_start(rows(h3_dram[TOK:TOK + RB, :]), zeros[:, :]).then_inc(zero_out, 16)
            sp.dma_start(rows(xs_dram[DUMMY_IN:DUMMY_IN + RB, :]), zeros[:, :]).then_inc(zero_out, 16)
            sp.wait_ge(ends_ready, 1)
            for e in range(E):
                row = sp.value_load(vi[0:1, 0, e:e + 1], min_val=e * REG, max_val=e * REG + TOK)
                sp.dma_start(rows(xs_dram[bass.ds(row, RB), :]), zeros[:, :]).then_inc(zero_out, 16)
            sp.wait_ge(zero_out, 16 * (E + 2))

        @block.vector
        def _(dve):
            ch = Chain(dve, step)
            count, tiles, off, first, ones, last, region, number = (v[:, r, :] for r in (0, 1, 2, 3, 4, 5, 8, 9))
            ch.link(dve.memset(ones, 1.0))
            dve.wait_ge(consts, 48)
            dve.tensor_copy(vi[:, 0, :], base[0:1, :]).then_inc(ends_ready, 1)
            ch.link(dve.tensor_tensor(count, base[0:1, :], region, ALU.subtract))
            ch.link(dve.tensor_scalar(tiles, count, float(RB - 1), None, ALU.add))
            ch.link(dve.tensor_copy(vi[:, 1, :], tiles))
            ch.link(dve.tensor_scalar(vi[:, 2, :], vi[:, 1, :], RB.bit_length() - 1, None, ALU.logical_shift_right))
            ch.link(dve.tensor_copy(tiles, vi[:, 2, :]))
            ch.link(dve.tensor_tensor_scan(off, ones, count, 0.0, ALU.mult, ALU.add))
            ch.link(dve.tensor_tensor(off, off, count, ALU.subtract))
            ch.link(dve.tensor_tensor_scan(last, ones, tiles, 0.0, ALU.mult, ALU.add))
            ch.link(dve.tensor_tensor(first, last, tiles, ALU.subtract))

            def wide(r):
                return r.unsqueeze(1).to_broadcast([1, NK, E])

            ch.link(dve.tensor_tensor(a[:, :, :], kk[:, :, :], wide(last), ALU.is_lt))
            ch.link(dve.tensor_tensor(ind[:, :, :], kk[:, :, :], wide(first), ALU.is_ge))
            ch.link(dve.tensor_tensor(ind[:, :, :], ind[:, :, :], a[:, :, :], ALU.mult))
            ch.link(dve.tensor_tensor(a[:, :, :], kk[:, :, :], wide(first), ALU.subtract))
            ch.link(dve.tensor_scalar(a[:, :, :], a[:, :, :], float(RB), None, ALU.mult))
            for r, (start, none) in enumerate(((region, DUMMY_IN), (off, DUMMY_OUT))):
                ch.link(dve.tensor_tensor(val[:, r, :, :], a[:, :, :], wide(start), ALU.add))
                ch.link(dve.tensor_scalar(val[:, r, :, :], val[:, r, :, :], -float(none), None, ALU.add))
                ch.link(dve.tensor_tensor(val[:, r, :, :], val[:, r, :, :], ind[:, :, :], ALU.mult))
                ch.link(dve.tensor_reduce(tf[:, r, :], val[:, r, :, :], AX.X, ALU.add))
                ch.link(dve.tensor_scalar(tf[:, r, :], tf[:, r, :], float(none), None, ALU.add))
            ch.link(dve.tensor_tensor(a[:, :, :], ind[:, :, :], wide(number), ALU.mult))
            ch.link(dve.tensor_reduce(tf[:, 2, :], a[:, :, :], AX.X, ALU.add))
            ch.link(dve.tensor_copy(tab[:, :, :], tf[:, :, :]))


def mixture1(nc, k, d, ident, tab, xs_dram, h3_dram, out):
    ctx = ExitStack()
    with ctx:
        CH = F1 // F
        RP = RB // 128
        RING = 4
        TURNS = (NK - RING) // RING
        w1 = k.sb(ctx, "w1_1", [F, E * F1])
        w2 = k.sb(ctx, "w2_1", [F, E * CH * F])
        b1 = k.sb(ctx, "b1_1", [F, E * CH])
        b2 = k.sb(ctx, "b2_1", [128, E * F])
        w1e = k.sb(ctx, "w1e", [F, 2, F1])
        b1e = k.sb(ctx, "b1e", [F, 2, CH])
        xs = k.sb(ctx, "xs_i", [128, RING, RP, F])
        xt = k.sb(ctx, "xt_i", [F, 2, RB])
        h3 = k.sb(ctx, "h3_i", [128, RING, RP, F])
        hid = k.sb(ctx, "hid_i", [F, 2, CH, RB])
        y = k.sb(ctx, "y_i", [128, 2, RP, F])
        res = k.sb(ctx, "res", [128, RING, RP, F])
        p_x = [k.ps(ctx, f"p_xi{u}") for u in range(2)]
        p_u = [[k.ps(ctx, f"p_ui{u}{r}") for r in range(2)] for u in range(2)]
        p_y = [k.ps(ctx, f"p_yi{u}") for u in range(2)]
        w_in = k.sem("w_in_i")
        w2_in = k.sem("w2_in_i")
        w1e_copied = k.sem("w1e_copied")
        xs_in = [k.sem(f"xs_in{u}") for u in range(RING)]
        h3_in = [k.sem(f"h3_in{u}") for u in range(RING)]
        stored = k.sem("stored")
        x_done = k.sem("x_done")
        x_copied = k.sem("x_copied")
        up_done = k.sem("up_done")
        relu_done = k.sem("relu_done_i")
        y_done = k.sem("y_done_i")
        y_step = k.sem("y_step")
        res_done = k.sem("res_done")
        block = ctx.enter_context(nc.Block())

        @block.sync
        def _(sp):
            sp.dma_start(w1[:, :], d["w1_1"]).then_inc(w_in, 16)
            sp.dma_start(b1[:, :], d["b1_1"]).then_inc(w_in, 16)

            def load_x(t, u):
                row = sp.value_load(tab[0:1, 0, bass.ds(t, 1)], min_val=0, max_val=DUMMY_IN)
                sp.wait_ge(x_done, t + 1)
                sp.dma_start(xs[:, u, :, :], xs_dram[bass.ds(row, RB), :].rearrange("(p r) f -> p r f", r=RP)).then_inc(xs_in[u], 16)

            def load_h(t, u):
                row = sp.value_load(tab[0:1, 1, bass.ds(t, 1)], min_val=0, max_val=DUMMY_OUT)
                sp.wait_ge(res_done, t + 1)
                sp.dma_start(h3[:, u, :, :], h3_dram[bass.ds(row, RB), :].rearrange("(p r) f -> p r f", r=RP)).then_inc(h3_in[u], 16)

            def store(t, u):
                row = sp.value_load(tab[0:1, 1, bass.ds(t, 1)], min_val=0, max_val=DUMMY_OUT)
                sp.wait_ge(res_done, t + 1 + RING)
                sp.wait_ge(stored, t * 16 + 32)
                sp.dma_start(out[bass.ds(row, RB), :].rearrange("(p r) f -> p r f", r=RP), res[:, u, :, :]).then_inc(stored, 16)

            for u in range(RING):
                load_x(u, u)
                load_h(u, u)
            sp.dma_start(w2[:, :], d["w2_1"]).then_inc(w2_in, 16)
            sp.dma_start(b2[:, :], bass.AP(d["b2_1"].tensor, 0, [[0, 128], [1, E * F]])).then_inc(w2_in, 16)

            def turn(t, u, more):
                if more:
                    load_x(t + RING, u)
                    load_h(t + RING, u)
                store(t, u)

            with sp.Fori(0, TURNS) as i:
                for u in range(RING):
                    turn(i * RING + u, u, True)
            for t in range(TURNS * RING, NK):
                turn(t, t % RING, t + RING < NK)
            sp.wait_ge(stored, NK * 16 + 32)

        @block.gpsimd
        def _(pool):
            pool.wait_ge(w_in, 32)

            def weights(t, u):
                e = pool.value_load(tab[0:1, 2, bass.ds(t, 1)], min_val=0, max_val=E - 1)
                pool.wait_ge(up_done, t * 2 + 2)
                pool.wait_ge(relu_done, t * 2 + 2)
                apart(pool)
                pool.tensor_copy(b1e[:, u, :], b1[:, bass.ds(e * CH, CH)])
                pool.tensor_copy(w1e[:, u, :], w1[:, bass.ds(e * F1, F1)]).then_inc(w1e_copied, 1)

            with pool.Fori(0, NK // 2) as i:
                for u in range(2):
                    weights(i * 2 + u, u)

        @block.tensor
        def _(pe):
            def transpose_x(t, r4, turn):
                u = r4 % 2
                pe.wait_ge(xs_in[r4], turn * 16 + 16)
                pe.wait_ge(x_copied, t + 1)
                for r in range(RP):
                    m = pe.transpose(p_x[u][:, r * 128:(r + 1) * 128], xs[:, r4, r, :], ident[:, :])
                m.then_inc(x_done, 1)

            def first(t, u):
                pe.wait_ge(w1e_copied, t + 1)
                pe.wait_ge(x_copied, t + 1 + 2)
                for c in range(CH):
                    if c % 2 == 0:
                        pe.wait_ge(relu_done, t * 2 + c // 2 + 1)
                    m = pe.matmul(p_u[u][c // 2][:, c % 2 * RB:(c % 2 + 1) * RB], w1e[:, u, c * F:(c + 1) * F], xt[:, u, :],
                                  start=True, stop=True)
                    if c % 2:
                        m.then_inc(up_done, 1)

            def second(t, u):
                e = pe.value_load(tab[0:1, 2, bass.ds(t, 1)], min_val=0, max_val=E - 1)
                pe.wait_ge(relu_done, t * 2 + 2 + 4)
                pe.wait_ge(res_done, t + RING - 1)
                for r in range(RP):
                    for c in range(CH):
                        m = pe.matmul(p_y[u][:, r * F:(r + 1) * F], hid[:, u, c, r * 128:(r + 1) * 128],
                                      w2[:, bass.ds(e * (CH * F) + c * F, F)], start=(c == 0), stop=(c == CH - 1))
                m.then_inc(y_done, 1)

            def turn(t, u, i):
                first(t, u % 2)
                transpose_x(t + 1, (u + 1) % RING, i + (u + 1) // RING)
                second(t - 1, (u + 1) % 2)

            transpose_x(0, 0, 0)
            first(0, 0)
            transpose_x(1, 1, 0)
            pe.wait_ge(w2_in, 32)
            for t in range(1, RING):
                turn(t, t, 0)
            with pe.Fori(1, TURNS) as i:
                for u in range(RING):
                    turn(i * RING + u, u, i)
            for t in range(TURNS * RING, NK - 1):
                turn(t, t % RING, t // RING)
            first(NK - 1, 1)
            second(NK - 2, 0)
            second(NK - 1, 1)

        @block.scalar
        def _(act):
            act.sem_inc(x_copied, 2)
            act.sem_inc(stored, 32)
            act.sem_inc(relu_done, 4)
            act.sem_inc(x_done, RING)
            with act.Fori(0, NK // 2) as i:
                for u in range(2):
                    t = i * 2 + u
                    act.wait_ge(y_done, t + 1)
                    for c in range(CH):
                        if c % 2 == 0:
                            act.wait_ge(up_done, t * 2 + c // 2 + 1 + 4)
                        m = act.activation(hid[:, u, c, :], p_u[u][c // 2][:, c % 2 * RB:(c % 2 + 1) * RB], ACT.Relu,
                                           bias=b1e[:, u, c:c + 1])
                        if c % 2:
                            m.then_inc(relu_done, 1)

        @block.vector
        def _(dve):
            dve.sem_inc(up_done, 4)
            dve.sem_inc(y_done, 2)
            dve.sem_inc(res_done, RING)

            def copy_x(t, u):
                dve.wait_ge(up_done, t * 2 + 2)
                dve.wait_ge(x_done, t + 1 + RING)
                dve.tensor_copy(xt[:, u, :], p_x[u][:, 0:RB]).then_inc(x_copied, 1)

            def result(t, r4, turn):
                u = r4 % 2
                e = dve.value_load(tab[0:1, 2, bass.ds(t, 1)], min_val=0, max_val=E - 1)
                dve.wait_ge(y_done, t + 1 + 2)
                apart(dve)
                ch = Chain(dve, y_step, t, 1)
                ch.link(dve.tensor_tensor(y[:, u, :, :], p_y[u][:, 0:RB].rearrange("p (r f) -> p r f", r=RP),
                                          b2[:, bass.ds(e * F, F)].unsqueeze(1).to_broadcast([128, RP, F]), ALU.add))
                dve.wait_ge(h3_in[r4], turn * 16 + 16)
                if not (isinstance(t, int) and t < RING - 2):
                    dve.wait_ge(stored, (t - RING + 1) * 16 + 32)
                dve.tensor_tensor(res[:, r4, :, :], y[:, u, :, :], h3[:, r4, :, :], ALU.add).then_inc(res_done, 1)

            copy_x(0, 0)
            copy_x(1, 1)
            dve.wait_ge(w2_in, 32)

            def turn(t, u, i):
                if not (isinstance(t, int) and t + 2 >= NK):
                    copy_x(t + 2, u % 2)
                result(t, u, i)

            for u in range(RING):
                turn(u, u, 0)
            with dve.Fori(1, TURNS) as i:
                for u in range(RING):
                    turn(i * RING + u, u, i)
            for t in range(TURNS * RING, NK):
                turn(t, t % RING, t // RING)


def audio_tower(nc, d, out):
    top = ExitStack()
    with top:
        k = Tools(nc, top)
        h0_dram = nc.dram_tensor("h0_dram", [HALF, NT * F], FP32)
        att_dram = nc.dram_tensor("att_dram", [NG, HALF, 2, B * CG], FP32)
        filt_dram = nc.dram_tensor("filt_dram", [2, STAGES, F, PAD], FP32)

        ident = k.sb(top, "ident", [128, 128])
        small = k.sb(top, "small", [128, 8])
        bn = k.sb(top, "bn", [128, 2])
        front = ExitStack()
        with front:
            fm = k.sb(front, "fm", [F, TOK])
            fm_rev = k.sb(front, "fm_rev", [F, TOK])
            tdnn(nc, k, d, ident, small, bn, fm, filt_dram)
            first_norm(nc, k, d, ident, bn, fm, fm_rev, h0_dram)
            convolutions(nc, k, d, fm, fm_rev, filt_dram, att_dram)
        h = k.sb(top, "h", [HALF, NT * F])
        middle = ExitStack()
        with middle:
            xf = k.sb(middle, "xf", [F, TOK])
            s_tok = k.sb(middle, "s_tok", [HALF, 2, B, E])
            g_tok = k.sb(middle, "g_tok", [HALF, 2, B, E])
            attach_norm(nc, k, d, ident, h0_dram, att_dram, h, xf, s_tok)
            choose(nc, k, d, ident, h, s_tok, g_tok)
            mixture0(nc, k, d, h, xf, g_tok)
        xs_dram = nc.dram_tensor("xs_dram", [DUMMY_IN + RB, F], FP32)
        h3_dram = nc.dram_tensor("h3_dram", [TOK + RB, F], FP32)
        base = k.sb(top, "base", [HALF, E])
        tab = k.sb(top, "tab", [1, 3, NK], I32)
        retain_and_route(nc, k, d, ident, small, h, base, xs_dram, h3_dram)
        plan_tiles(nc, k, d, base, tab, xs_dram, h3_dram)
        mixture1(nc, k, d, ident, tab, xs_dram, h3_dram, out)


def constants():
    import numpy as np

    half = F // 2
    freqs = np.float32(10000.0) ** (-np.arange(half, dtype=np.float32) / np.float32(half))
    phi = np.arange(L, dtype=np.float32)[:, None] * freqs.astype(np.float32)[None, :]
    pe = np.concatenate([np.sin(phi), np.cos(phi)], axis=-1).astype(np.float32)
    gamma = 1.0 - 2.0 ** (-5.0 - np.arange(HEADS, dtype=np.float64))
    decay = np.zeros((HALF, HEADS, 3 * HALF), np.float32)
    for first, j0, width in ((0, 0, HALF), (HALF, HALF, L)):
        rel = (np.arange(HALF)[:, None] + j0) - np.arange(width)[None, :]
        for n in range(HEADS):
            decay[:, n, first:first + width] = np.where(rel >= 0, gamma[n] ** np.maximum(rel, 0), 0.0) / np.sqrt(HD)
    even = (np.arange(F) // HD % 2 == 0).astype(np.float32)
    more = {"decay": decay, "even": even, "before": np.triu(np.ones((HALF, HALF), np.float32), 1),
            "prio": (E - np.arange(E, dtype=np.float32))[None, :], "region": (REG * np.arange(E, dtype=np.float32))[None, :],
            "number": np.arange(E, dtype=np.float32)[None, :],
            "kk": np.repeat(np.arange(NK, dtype=np.float32), E).reshape(1, NK, E)}
    return {**more, "ident": np.eye(128, dtype=np.float32), "flip": np.eye(HALF, dtype=np.float32)[::-1].copy(), "pe_t": np.ascontiguousarray(pe.T)}


def kernel(**inputs):
    import numpy as np
    import concourse.bacc as bacc
    from concourse.bass_utils import run_bass_kernel_spmd

    a = {n: np.asarray(v) for n, v in inputs.items()}
    rows = constants()
    rows["x"] = a["x"].reshape(-1)
    rows["tok_w"] = np.concatenate([a["L0_tok_W"].T, a["L0_tok_b"][None, :]], axis=0)
    even = rows.pop("even")
    rows["small"] = np.stack([a["L0_tok_gamma"], a["L0_tok_beta"], even, (even == 0).astype(np.float32), a["L1_attn_bq"],
                              a["L1_attn_bk"], np.zeros(F, np.float32), np.zeros(F, np.float32)], axis=1)
    rows["wq"] = a["L1_attn_wq"].T
    rows["wk"] = a["L1_attn_wk"].T
    rows["wvg"] = np.concatenate([a["L1_attn_wv"].T, a["L1_attn_wg"].T], axis=1)
    rows["bvg"] = np.concatenate([a["L1_attn_bv"], a["L1_attn_bg"]])[None, :]
    rows["wg1"] = a["L1_ffn_Wg"]
    rows["bg1"] = a["L1_ffn_bg"][None, :]
    rows["w1_1"] = a["L1_ffn_W1"].transpose(1, 0, 2).reshape(F, E * F1)
    rows["b1_1"] = a["L1_ffn_b1"].reshape(E * F1 // F, F).T
    rows["w2_1"] = a["L1_ffn_W2"].reshape(E * F1 // F, F, F).transpose(1, 0, 2).reshape(F, E * F1)
    rows["b2_1"] = a["L1_ffn_b2"].reshape(1, E * F)
    rows["w_filt"] = a["L0_attn_W_filt"].reshape(F, F * STAGES)
    rows["w_proj"] = a["L0_attn_W_proj"].reshape(F, NG, CG, 2, 2).transpose(0, 1, 4, 3, 2).reshape(F, NG, 2, 2 * CG)
    rows["wg0"] = a["L0_ffn_Wg"]
    rows["b2_0"] = a["L0_ffn_b2"]
    rows["w1_0"] = a["L0_ffn_W1"].transpose(1, 0, 2)
    rows["b1_0"] = a["L0_ffn_b1"].reshape(E, F0 // F, F).transpose(2, 0, 1)
    rows["w2_0"] = a["L0_ffn_W2"].reshape(E, F0 // F, F, F).transpose(2, 0, 1, 3)
    rows = {n: np.ascontiguousarray(v) for n, v in rows.items()}

    nc = bacc.Bacc("TRN2", target_bir_lowering=False, num_devices=1)
    d = {n: nc.dram_tensor(f"in_{n}", v.shape, mybir.dt.from_np(v.dtype), kind="ExternalInput").ap()
         for n, v in rows.items()}
    out = nc.dram_tensor("out", (TOK + RB, F), FP32, kind="ExternalOutput").ap()
    audio_tower(nc, d, out)
    r = run_bass_kernel_spmd(nc, [{f"in_{n}": v for n, v in rows.items()}], core_ids=[0])
    return r.results[0]["out"][:TOK].reshape(B, L, F)
```

```python
from contextlib import ExitStack

import concourse.bass as bass
from concourse import mybir

FP32 = mybir.dt.float32
BF16 = mybir.dt.bfloat16
I32 = mybir.dt.int32
ALU = mybir.AluOpType
ACT = mybir.ActivationFunctionType
AX = mybir.AxisListType

B, T_IN, D_IN = 64, 256, 23
CTX = 5
L = T_IN - CTX + 1
HALF = L // 2
NT = 2 * B
TOK = B * L
F = 128
QT = 4
QN = QT * HALF
QF = QT * F
NQ = NT // QT
PATCH = CTX * D_IN
EPS = 1e-5
STAGES = 3
PAD = 3 * HALF
E = 8
TOPK = L * 2 // E
F0 = 256
F1 = 512
HEADS = 8
HD = F // HEADS
CG = 32
NG = F // CG
QC = 4
NS = CG // QC
RB = 256
REG = TOK + RB
DUMMY_IN = E * REG
DUMMY_OUT = TOK
NK = (TOK + E * (RB - 1)) // RB
NK += NK % 2
TR = 6


def apart(eng):
    eng.nop(nofuse=True)


class Chain:

    def __init__(self, eng, sem, at=0, per=0, base=0):
        self.eng, self.sem, self.n, self.start = eng, sem, 0, at * per + base

    def sig(self, ins):
        ins.then_inc(self.sem, 1)
        self.n += 1

    def wait(self):
        self.eng.wait_ge(self.sem, self.start + self.n)

    def link(self, ins):
        self.sig(ins)
        self.wait()


class Tools:
    def __init__(self, nc, top):
        self.nc, self.top = nc, top

    def sem(self, name):
        return self.top.enter_context(self.nc.semaphore(name))

    def sb(self, ctx, name, shape, dt=FP32):
        return ctx.enter_context(self.nc.sbuf_tensor(name, list(shape), dt))

    def ps(self, ctx, name, dt=FP32):
        return ctx.enter_context(self.nc.psum_tensor(name, [128, 2048 // (4 if dt == FP32 else 2)], dt))


def tdnn(nc, k, d, ident, small, bn, fm, filt_dram):
    ctx = ExitStack()
    with ctx:
        U = 2
        tok_w = k.sb(ctx, "tok_w", [PATCH + 1, F])
        patch = k.sb(ctx, "patch", [HALF, U, QT, PATCH + 1])
        patch_t = k.sb(ctx, "patch_t", [PATCH + 1, U, QN])
        stats = k.sb(ctx, "stats", [F, NQ * 6])
        mv = k.sb(ctx, "mv", [F, 2])
        rs = k.sb(ctx, "rs", [F, 4])
        nhalf = k.sb(ctx, "nhalf", [F, 1])
        pe_t = k.sb(ctx, "pe_t", [F, L])
        w_filt = k.sb(ctx, "w_filt", [F, F * STAGES])
        filt = k.sb(ctx, "filt", [F, 2, STAGES, PAD])
        p_win = [k.ps(ctx, f"p_win{u}") for u in range(U)]
        p_y = [k.ps(ctx, f"p_y{u}") for u in range(U)]
        p_filt = [k.ps(ctx, f"p_filt{s}") for s in range(STAGES)]

        consts = k.sem("consts")
        win_in = [k.sem(f"win_in{u}") for u in range(U)]
        ones_set = k.sem("ones_set")
        win_t = k.sem("win_t")
        win_copied = k.sem("win_copied")
        y_done = k.sem("y_done")
        relu_done = k.sem("relu_done")
        bn_step = k.sem("bn_step")
        rstd_done = k.sem("rstd_done")
        nhalf_set = k.sem("nhalf_set")
        filt_pe = k.sem("filt_pe")
        filt_zero = k.sem("filt_zero")
        filt_copied = k.sem("filt_copied")
        filt_out = k.sem("filt_out")
        block = ctx.enter_context(nc.Block())

        @block.sync
        def _(sp):
            sp.dma_start(tok_w[:, :], d["tok_w"]).then_inc(consts, 16)
            sp.dma_start(ident[:, :], d["ident"]).then_inc(consts, 16)
            sp.dma_start(small[:, :], d["small"]).then_inc(consts, 16)
            sp.dma_start(pe_t[:, :], d["pe_t"]).then_inc(consts, 16)
            sp.dma_start(w_filt[:, :], d["w_filt"]).then_inc(consts, 16)
            sp.wait_ge(ones_set, U)
            with sp.Fori(0, NQ // U) as i:
                for u in range(U):
                    sp.wait_ge(win_copied, i * U + u + 1)
                    for b in range(2):
                        at = d["x"][bass.ds((i * U + u) * (2 * T_IN * D_IN) + b * T_IN * D_IN, 1)]
                        src = bass.AP(at.tensor, at.offset, [[D_IN, HALF], [HALF * D_IN, 2], [1, PATCH]])
                        sp.dma_start(patch[:, u, 2 * b:2 * b + 2, 0:PATCH], src).then_inc(win_in[u], 16)
            sp.wait_ge(filt_zero, 1)
            sp.wait_ge(filt_copied, 2 * STAGES)
            sp.dma_start(filt_dram.ap().rearrange("r s c t -> c r s t"), filt[:, :, :, :]).then_inc(filt_out, 16)
            sp.wait_ge(filt_out, 16)

        @block.tensor
        def _(pe):
            pe.wait_ge(consts, 80)
            for s in range(STAGES):
                wf = w_filt[:, :].rearrange("p (c s) -> p s c", s=STAGES)[:, s, :]
                pe.matmul(p_filt[s][:, 0:L], wf, pe_t[:, :], start=True, stop=True).then_inc(filt_pe, 1)
            with pe.Fori(0, NQ // U) as i:
                for u in range(U):
                    pe.wait_ge(win_in[u], i * 32 + 32)
                    pe.wait_ge(win_copied, i * U + u + 1)
                    for j in range(QT):
                        m = pe.transpose(p_win[u][0:PATCH + 1, j * HALF:(j + 1) * HALF], patch[:, u, j, :],
                                         ident[0:HALF, 0:HALF])
                    m.then_inc(win_t, 1)
                for u in range(U):
                    pe.wait_ge(win_copied, i * U + u + 1 + U)
                    pe.wait_ge(relu_done, i * U + u + 1)
                    pe.matmul(p_y[u][:, 0:QN], tok_w[:, :], patch_t[:, u, :], start=True, stop=True).then_inc(y_done, 1)

        @block.scalar
        def _(act):
            act.sem_inc(win_copied, U)
            act.sem_inc(relu_done, U)
            for s in range(STAGES):
                act.wait_ge(filt_pe, s + 1)
                act.activation(filt[:, 0, s, HALF:HALF + L], p_filt[s][:, 0:L], ACT.Copy).then_inc(filt_copied, 1)
                act.activation(filt[:, 1, s, 0:L], p_filt[s][:, L - 1::-1], ACT.Copy).then_inc(filt_copied, 1)
            with act.Fori(0, NQ // U) as i:
                for u in range(U):
                    act.wait_ge(win_t, i * U + u + 1)
                    act.activation(patch_t[:, u, :], p_win[u][0:PATCH + 1, 0:QN], ACT.Copy).then_inc(win_copied, 1)
                for u in range(U):
                    act.wait_ge(y_done, i * U + u + 1)
                    apart(act)
                    act.activation(fm[:, bass.ds((i * U + u) * QN, QN)], p_y[u][:, 0:QN], ACT.Relu).then_inc(relu_done, 1)

        @block.gpsimd
        def _(pool):
            pool.memset(nhalf[:, :], -0.5).then_inc(nhalf_set, 1)
            pool.memset(filt[:, 0, :, 0:HALF], 0.0).then_inc(nhalf_set, 1)
            pool.memset(filt[:, 1, :, L:PAD], 0.0).then_inc(filt_zero, 1)
            pool.wait_ge(nhalf_set, 2)
            pool.wait_ge(bn_step, 2)
            pool.tensor_tensor(out=rs[:, 1:2], in0=rs[:, 0:1], in1=nhalf[:, :], op=ALU.pow).then_inc(rstd_done, 1)

        @block.vector
        def _(dve):
            for u in range(U):
                dve.memset(patch[:, u, :, PATCH:PATCH + 1], 1.0).then_inc(ones_set, 1)
            with dve.Fori(0, NQ) as i:
                dve.wait_ge(relu_done, i + 1 + U)
                dve.bn_stats(stats[:, bass.ds(i * 6, 6)], fm[:, bass.ds(i * QN, QN)]).then_inc(ones_set, 1)
            dve.wait_ge(ones_set, U + NQ)
            ch = Chain(dve, bn_step)
            ch.link(dve.bn_aggr(mv[:, :], stats[:, :]))
            ch.sig(dve.tensor_scalar(rs[:, 0:1], mv[:, 1:2], EPS, None, ALU.add))
            dve.wait_ge(consts, 80)
            dve.wait_ge(rstd_done, 1)
            ch.link(dve.tensor_tensor(bn[:, 0:1], small[:, 0:1], rs[:, 1:2], ALU.mult))
            ch.link(dve.tensor_tensor(rs[:, 2:3], mv[:, 0:1], bn[:, 0:1], ALU.mult))
            ch.link(dve.tensor_tensor(bn[:, 1:2], small[:, 1:2], rs[:, 2:3], ALU.subtract))


def first_norm(nc, k, d, ident, bn, fm, fm_rev, h0_dram):
    ctx = ExitStack()
    with ctx:
        U = 4
        hn = k.sb(ctx, "hn", [F, U, QN])
        ht = k.sb(ctx, "ht", [HALF, U, QF])
        xn = k.sb(ctx, "xn", [HALF, U, QF])
        lst = k.sb(ctx, "lst", [HALF, U, QT, 6])
        lmv = k.sb(ctx, "lmv", [HALF, U, QT, 2])
        lve = k.sb(ctx, "lve", [HALF, U, QT])
        lrs = k.sb(ctx, "lrs", [HALF, U, QT])
        nhalf = k.sb(ctx, "nhalf_b", [HALF, QT])
        p_h = [k.ps(ctx, f"p_h{u}") for u in range(U)]
        p_x = [k.ps(ctx, f"p_x{u}") for u in range(U)]

        hn_ready = k.sem("hn_ready")
        h_done = k.sem("h_done")
        ht_copied = k.sem("ht_copied")
        h0_out = [k.sem(f"h0_out{u}") for u in range(U)]
        var_done = k.sem("var_done")
        rstd_done = k.sem("rstd_done_b")
        pool_step = k.sem("pool_step_b")
        dve_step = k.sem("dve_step_b")
        xn_ready = k.sem("xn_ready")
        xt_done = k.sem("xt_done")
        fm_copied = k.sem("fm_copied")
        rev_copied = k.sem("rev_copied")
        block = ctx.enter_context(nc.Block())

        @block.sync
        def _(sp):
            with sp.Fori(0, NQ // U) as i:
                for u in range(U):
                    sp.wait_ge(ht_copied, i * U + u + 1 + U)
                    sp.dma_start(h0_dram[:, bass.ds((i * U + u) * QF, QF)], ht[:, u, :]).then_inc(h0_out[u], 16)
            for u in range(U):
                sp.wait_ge(h0_out[u], 16 * (NQ // U + 1))

        @block.tensor
        def _(pe):
            with pe.Fori(0, NQ // U) as i:
                for u in range(U):
                    pe.wait_ge(hn_ready, i * U + u + 1)
                    pe.wait_ge(ht_copied, i * U + u + 1)
                    for j in range(QT):
                        m = pe.transpose(p_h[u][0:HALF, j * F:(j + 1) * F], hn[:, u, j * HALF:(j + 1) * HALF], ident[:, :])
                    m.then_inc(h_done, 1)
                for u in range(U):
                    pe.wait_ge(xn_ready, i * U + u + 1)
                    pe.wait_ge(rev_copied, i * U + u + 1)
                    for j in range(QT):
                        m = pe.transpose(p_x[u][:, j * HALF:(j + 1) * HALF], xn[:, u, j * F:(j + 1) * F],
                                         ident[0:HALF, 0:HALF])
                    m.then_inc(xt_done, 1)

        @block.scalar
        def _(act):
            act.sem_inc(ht_copied, U)
            for u in range(U):
                act.sem_inc(h0_out[u], 16)
            with act.Fori(0, NQ // U) as i:
                for u in range(U):
                    act.activation(hn[:, u, :], fm[:, bass.ds((i * U + u) * QN, QN)], ACT.Identity,
                                   bias=bn[:, 1:2], scale=bn[:, 0:1]).then_inc(hn_ready, 1)
                for u in range(U):
                    act.wait_ge(h_done, i * U + u + 1)
                    act.wait_ge(h0_out[u], i * 16 + 16)
                    act.activation(ht[:, u, :], p_h[u][0:HALF, :], ACT.Copy).then_inc(ht_copied, 1)
                for u in range(U):
                    act.wait_ge(xt_done, i * U + u + 1)
                    apart(act)
                    act.activation(fm[:, bass.ds((i * U + u) * QN, QN)], p_x[u][:, 0:QN], ACT.Copy).then_inc(fm_copied, 1)

        @block.gpsimd
        def _(pool):
            ch = Chain(pool, pool_step)
            ch.link(pool.memset(nhalf[:, :], -0.5))
            with pool.Fori(0, NQ // U) as i:
                for u in range(U):
                    pool.wait_ge(var_done, i * U + u + 1)
                    apart(pool)
                    pc = Chain(pool, pool_step, i, U, 1 + u)
                    pc.link(pool.tensor_scalar(lve[:, u, :], lmv[:, u, :, 1], EPS, None, ALU.add))
                    pool.tensor_tensor(out=lrs[:, u, :], in0=lve[:, u, :], in1=nhalf[:, :], op=ALU.pow).then_inc(rstd_done, 1)

        @block.vector
        def _(dve):
            dve.sem_inc(rev_copied, U)
            with dve.Fori(0, NQ // U) as i:
                ch = Chain(dve, dve_step, i, U)
                for u in range(U):
                    dve.wait_ge(ht_copied, i * U + u + 1 + U)
                    for j in range(QT):
                        m = dve.bn_stats(lst[:, u, j, :], ht[:, u, j * F:(j + 1) * F])
                    ch.link(m)
                    apart(dve)
                    for j in range(QT):
                        m = dve.bn_aggr(lmv[:, u, j, :], lst[:, u, j, :])
                    m.then_inc(var_done, 1)
                for u in range(U):
                    dve.wait_ge(rstd_done, i * U + u + 1)
                    for j in range(QT):
                        m = dve.tensor_scalar(xn[:, u, j * F:(j + 1) * F], ht[:, u, j * F:(j + 1) * F],
                                              lmv[:, u, j, 0:1], lrs[:, u, j:j + 1], ALU.subtract, ALU.mult)
                    m.then_inc(xn_ready, 1)
                for u in range(U):
                    dve.wait_ge(fm_copied, i * U + u + 1)
                    rev = fm_rev[:, bass.ds((i * U + u) * QN, QN)].rearrange("p (j t) -> p j t", j=QT)
                    src = p_x[u][:, 0:QN].rearrange("p (j t) -> p j t", j=QT)[:, :, ::-1]
                    dve.tensor_copy(rev, src).then_inc(rev_copied, 1)


def convolutions(nc, k, d, fm, fm_rev, filt_dram, att_dram):
    ctx = ExitStack()
    with ctx:
        w_proj = k.sb(ctx, "w_proj", [F, NG, 2, 2 * CG])
        x_buf = k.sb(ctx, "x_buf", [HALF, B + 8 * CG * B])
        x = x_buf[:, B:].rearrange("t (o h p n) -> t o h p n", o=2, h=2, p=2)
        x_blocks = x_buf[:, :].rearrange("t (k b) -> t k b", b=B)
        toep = k.sb(ctx, "toep", [HALF, TR, 2, L])
        p_p = [k.ps(ctx, f"p_p{r}") for r in range(4)]
        p_c = [k.ps(ctx, f"p_c{r}") for r in range(4)]
        NB = 4
        BANKS = (B // NB) * 2 * 2
        STEPS = STAGES * NS
        TILES = 2 * STEPS

        w_in = k.sem("w_in")
        zeros_set = k.sem("zeros_set")
        toep_in = [k.sem(f"toep_in{r}") for r in range(TR)]
        proj_done = k.sem("proj_done")
        proj_copied = k.sem("proj_copied")
        conv_done = k.sem("conv_done")
        prod_done = k.sem("prod_done")
        att_out = k.sem("att_out")
        att_stored = k.sem("att_stored")
        block = ctx.enter_context(nc.Block())

        def banks():
            for o in (1, 0):
                for bg in range(B // NB):
                    for half in range(2):
                        yield o, bg, half

        def place(s):
            return s % 2, s // 2

        @block.sync
        def _(sp):
            sp.dma_start(w_proj[:, :, :, :], d["w_proj"]).then_inc(w_in, 16)
            with sp.Fori(0, NG) as g:
                for m in range(TILES):
                    s, c = m // (2 * NS), (m % (2 * NS)) * 2
                    kind, first = ((1, 0), (0, 1), (1, 0))[s]
                    at = filt_dram.ap().rearrange("r s c t -> (r s c t)")[
                        bass.ds(g * (CG * PAD) + ((kind * STAGES + s) * F + c) * PAD + first, 1)]
                    src = bass.AP(at.tensor, at.offset, [[1, HALF], [PAD, 2], [1, L]])
                    sp.wait_ge(conv_done, g * TILES + m + 1)
                    sp.dma_start(toep[:, m % TR, :, :], src).then_inc(toep_in[m % TR], 16)

        @block.tensor
        def _(pe):
            pe.wait_ge(w_in, 16)
            pe.wait_ge(zeros_set, 1)
            with pe.Fori(0, NG) as g:
                for n, (o, bg, half) in enumerate(banks()):
                    pe.wait_ge(proj_copied, g * BANKS + n + 1)
                    src = fm_rev if o else fm
                    for b in range(NB):
                        tile = 2 * (bg * NB + b) + half
                        m = pe.matmul(p_p[n % 4][0:HALF, b * 4 * CG:(b + 1) * 4 * CG], src[:, tile * HALF:(tile + 1) * HALF],
                                      w_proj[:, bass.ds(g, 1), :, :], start=True, stop=True)
                    m.then_inc(proj_done, 1)
                pe.wait_ge(proj_copied, g * BANKS + BANKS + 4)
                for n in range(STEPS):
                    s, q = n // NS, n % NS
                    o, p = place(s)
                    pe.wait_ge(prod_done, g * STEPS + n + 1)
                    for t in range(2):
                        r = 2 * n + t
                        pe.wait_ge(toep_in[r % TR], g * (16 * TILES // TR) + 16 * (r // TR) + 16)
                        for c in range(2):
                            ch = q * QC + 2 * t + c
                            tt = toep[:, r % TR, c, :]
                            near, far = (tt[:, HALF:L], tt[:, 0:HALF]) if s % 2 == 0 else (tt[:, 0:HALF], tt[:, HALF:L])
                            to = p_c[n % 4][0:HALF, (2 * t + c) * 2 * B:(2 * t + c + 1) * 2 * B]
                            y0 = 1 + (o * 4 + p) * CG + ch
                            pe.matmul(to, near, x[:, o, :, p, ch * B:(ch + 1) * B], start=True, stop=False)
                            m = pe.matmul(to, far, x_blocks[:, 0:y0 + 1:y0, :], start=False, stop=True)
                        m.then_inc(conv_done, 1)

        @block.scalar
        def _(act):
            act.sem_inc(proj_copied, 4)
            with act.Fori(0, NG) as g:
                for n, (o, bg, half) in enumerate(banks()):
                    if n == 0:
                        act.wait_ge(prod_done, g * STEPS + 4)
                    if n == BANKS // 2:
                        act.wait_ge(att_stored, g + 1)
                    act.wait_ge(proj_done, g * BANKS + n + 1)
                    dst = x[:, o, half, :, :].rearrange("t p (c b) -> t (p c) b", b=B)[:, :, bg * NB:(bg + 1) * NB]
                    src = p_p[n % 4][0:HALF, :].rearrange("t (b o k) -> t k b o", b=NB, o=2)[:, :, :, o]
                    act.activation(dst, src, ACT.Copy).then_inc(proj_copied, 1)

        @block.gpsimd
        def _(pool):
            pool.sem_inc(att_stored, 1)
            with pool.Fori(0, NG) as g:
                pool.wait_ge(prod_done, g * STEPS + STEPS + 4)
                pool.dma_start(att_dram[bass.ds(g, 1), :, :, :].rearrange("o t h n -> (o t) h n"),
                               x[:, 0, :, 0, :]).then_inc(att_out, 16)
                pool.wait_ge(att_out, g * 16 + 16)
                pool.sem_inc(att_stored, 1)

        @block.vector
        def _(dve):
            dve.memset(x_buf[:, 0:B], 0.0).then_inc(zeros_set, 1)
            dve.sem_inc(conv_done, TR)
            dve.sem_inc(prod_done, 4)
            with dve.Fori(0, NG) as g:
                for n in range(STEPS):
                    s, q = n // NS, n % NS
                    o, p = place(s + 1)
                    dve.wait_ge(conv_done, g * TILES + 2 * n + 2 + TR)
                    nxt = x[:, o, :, p, q * QC * B:(q + 1) * QC * B]
                    y = p_c[n % 4][0:HALF, :].rearrange("t (c h b) -> t h c b", c=QC, h=2)
                    if s < STAGES - 1:
                        nxt = nxt.rearrange("t h (c b) -> t h c b", c=QC)
                        dve.tensor_tensor(nxt, y, nxt, ALU.mult).then_inc(prod_done, 1)
                    else:
                        for half in range(2):
                            dst = x[:, 0, half, 0, :].rearrange("t (b c) -> t c b", b=B)[:, q * QC:(q + 1) * QC, :]
                            m = dve.tensor_tensor(dst, y[:, half, :, :],
                                                  nxt[:, half, :].rearrange("t (c b) -> t c b", c=QC), ALU.mult)
                        m.then_inc(prod_done, 1)


def attach_norm(nc, k, d, ident, h0_dram, att_dram, h, xf, s_tok):
    ctx = ExitStack()
    with ctx:
        U = 4
        flip = k.sb(ctx, "flip", [HALF, HALF])
        wg0 = k.sb(ctx, "wg0", [F, E])
        h0 = k.sb(ctx, "h0", [HALF, U, QF])
        att = k.sb(ctx, "att", [HALF, U, NG, 2, 2 * CG])
        xn = k.sb(ctx, "xn_d", [HALF, U, QF])
        xt = k.sb(ctx, "xt_d", [F, U, QN])
        lst = k.sb(ctx, "lst_d", [HALF, U, QT, 6])
        lmv = k.sb(ctx, "lmv_d", [HALF, U, QT, 2])
        lve = k.sb(ctx, "lve_d", [HALF, U, QT])
        lrs = k.sb(ctx, "lrs_d", [HALF, U, QT])
        nhalf = k.sb(ctx, "nhalf_d", [HALF, QT])
        p_f = [k.ps(ctx, f"p_f{r}") for r in range(2)]
        p_x = [k.ps(ctx, f"p_xd{u}") for u in range(U)]
        p_l = [k.ps(ctx, f"p_l{r}") for r in range(2)]

        consts = k.sem("consts_d")
        quad_in = [k.sem(f"quad_in{u}") for u in range(U)]
        flipped = k.sem("flipped")
        joined = k.sem("joined")
        var_done = k.sem("var_done_d")
        pool_step = k.sem("pool_step_d")
        dve_step = k.sem("dve_step_d")
        rstd_done = k.sem("rstd_done_d")
        xn_ready = k.sem("xn_ready_d")
        xt_done = k.sem("xt_done_d")
        xt_copied = k.sem("xt_copied_d")
        xf_copied = k.sem("xf_copied")
        log_done = k.sem("log_done")
        log_copied = k.sem("log_copied")
        block = ctx.enter_context(nc.Block())

        @block.sync
        def _(sp):
            sp.dma_start(flip[:, :], d["flip"]).then_inc(consts, 16)
            sp.dma_start(wg0[:, :], d["wg0"]).then_inc(consts, 16)
            with sp.Fori(0, NQ // U) as i:
                for u in range(U):
                    sp.wait_ge(joined, i * U + u + 1)
                    sp.dma_start(h0[:, u, :], h0_dram[:, bass.ds((i * U + u) * QF, QF)]).then_inc(quad_in[u], 16)
                    for g in range(NG):
                        sp.dma_start(att[:, u, g, :, :],
                                     att_dram[g, :, :, bass.ds((i * U + u) * 2 * CG, 2 * CG)]).then_inc(quad_in[u], 16)

        @block.tensor
        def _(pe):
            pe.wait_ge(consts, 32)
            with pe.Fori(0, NQ // U) as i:
                for u in range(U):
                    n = i * U + u
                    pe.wait_ge(quad_in[u], i * 80 + 80)
                    pe.wait_ge(joined, n + 3)
                    for j in range(QT):
                        b, half = j // 2, j % 2
                        m = pe.matmul(p_f[u % 2][0:HALF, j * F:(j + 1) * F], flip[:, :],
                                      att[:, u, :, half, b * CG:(b + 1) * CG], start=True, stop=True)
                    m.then_inc(flipped, 1)
                for u in range(U):
                    n = i * U + u
                    pe.wait_ge(xn_ready, n + 1)
                    pe.wait_ge(xt_copied, n + 1)
                    for j in range(QT):
                        m = pe.transpose(p_x[u][:, j * HALF:(j + 1) * HALF], xn[:, u, j * F:(j + 1) * F],
                                         ident[0:HALF, 0:HALF])
                    m.then_inc(xt_done, 1)
                for u in range(U):
                    n = i * U + u
                    pe.wait_ge(xt_copied, n + 1 + U)
                    pe.wait_ge(log_copied, n + 3)
                    for j in range(QT):
                        m = pe.matmul(p_l[u % 2][0:HALF, j * E:(j + 1) * E], xt[:, u, j * HALF:(j + 1) * HALF],
                                      wg0[:, :], start=True, stop=True)
                    m.then_inc(log_done, 1)

        @block.scalar
        def _(act):
            act.sem_inc(xt_copied, U)
            with act.Fori(0, NQ // U) as i:
                for u in range(U):
                    n = i * U + u
                    act.wait_ge(log_copied, n + 1)
                    act.wait_ge(xf_copied, n + 1)
                    act.wait_ge(xt_done, n + 1)
                    act.activation(xt[:, u, :], p_x[u][:, 0:QN], ACT.Copy).then_inc(xt_copied, 1)

        @block.gpsimd
        def _(pool):
            ch = Chain(pool, pool_step)
            pool.sem_inc(xf_copied, U)
            ch.link(pool.memset(nhalf[:, :], -0.5))
            with pool.Fori(0, NQ // U) as i:
                pc = Chain(pool, pool_step, i, U, 1)
                for u in range(U):
                    pool.wait_ge(var_done, i * U + u + 1)
                    apart(pool)
                    pc.link(pool.tensor_scalar(lve[:, u, :], lmv[:, u, :, 1], EPS, None, ALU.add))
                    pool.tensor_tensor(out=lrs[:, u, :], in0=lve[:, u, :], in1=nhalf[:, :], op=ALU.pow).then_inc(rstd_done, 1)
                for u in range(U):
                    n = i * U + u
                    pool.wait_ge(xt_copied, n + 1 + U)
                    apart(pool)
                    pool.tensor_copy(xf[:, bass.ds(n * QN, QN)], xt[:, u, :]).then_inc(xf_copied, 1)

        @block.vector
        def _(dve):
            dve.sem_inc(joined, U)
            dve.sem_inc(log_copied, U)
            with dve.Fori(0, NQ // U) as i:
                ch = Chain(dve, dve_step, i, U)
                for u in range(U):
                    n = i * U + u
                    dve.wait_ge(flipped, n + 1)
                    apart(dve)
                    dve.tensor_tensor(h[:, bass.ds(n * QF, QF)], p_f[u % 2][0:HALF, :], h0[:, u, :], ALU.add).then_inc(joined, 1)
                    dve.wait_ge(joined, n + 1 + U)
                    apart(dve)
                    for j in range(QT):
                        m = dve.bn_stats(lst[:, u, j, :], h[:, bass.ds(n * QF + j * F, F)])
                    ch.link(m)
                    apart(dve)
                    for j in range(QT):
                        m = dve.bn_aggr(lmv[:, u, j, :], lst[:, u, j, :])
                    m.then_inc(var_done, 1)
                for u in range(U):
                    n = i * U + u
                    dve.wait_ge(rstd_done, n + 1)
                    apart(dve)
                    for j in range(QT):
                        m = dve.tensor_scalar(xn[:, u, j * F:(j + 1) * F], h[:, bass.ds(n * QF + j * F, F)],
                                              lmv[:, u, j, 0:1], lrs[:, u, j:j + 1], ALU.subtract, ALU.mult)
                    m.then_inc(xn_ready, 1)
                for u in range(U):
                    n = i * U + u
                    dve.wait_ge(log_done, n + 1)
                    apart(dve)
                    src = p_l[u % 2][0:HALF, 0:QT * E].rearrange("t (b h e) -> t h b e", b=2, h=2)
                    dve.tensor_copy(s_tok[:, :, bass.ds(n * 2, 2), :], src).then_inc(log_copied, 1)


def choose(nc, k, d, ident, h, s_tok, g_tok):
    ctx = ExitStack()
    with ctx:
        BG = 16
        NBG = B // BG
        mx = k.sb(ctx, "mx", [HALF, NT])
        st = k.sb(ctx, "st", [128, NBG, L])
        work = k.sb(ctx, "work", [128, NBG, L])
        m8 = k.sb(ctx, "m8", [128, NBG, 8])
        above = k.sb(ctx, "above", [128, NBG, L])
        equal = k.sb(ctx, "equal", [128, NBG, L])
        rank = k.sb(ctx, "rank", [128, NBG, L])
        gate = k.sb(ctx, "gate", [128, NBG, L])
        ones = k.sb(ctx, "ones_e", [128, L])
        count = k.sb(ctx, "count", [128, NBG])
        room = k.sb(ctx, "room", [128, NBG])
        b2d = k.sb(ctx, "b2d", [128, BG * F])
        p_s = [k.ps(ctx, f"p_s{r}") for r in range(2)]
        p_g = [k.ps(ctx, f"p_g{r}") for r in range(2)]
        p_b = [k.ps(ctx, f"p_b{r}") for r in range(4)]

        dve_step = k.sem("dve_step_e")
        shifted = k.sem("shifted")
        exps = k.sem("exps")
        probs = k.sem("probs")
        s_t = k.sem("s_t")
        gates = k.sem("gates")
        g_t = k.sem("g_t")
        b2_zero = k.sem("b2_zero")
        b2_in = k.sem("b2_in")
        b2_done = k.sem("b2_done")
        b2_added = k.sem("b2_added")
        block = ctx.enter_context(nc.Block())
        s_flat = s_tok[:, :, :, :].rearrange("t h b e -> t (h b) e")

        @block.sync
        def _(sp):
            sp.wait_ge(b2_zero, 1)
            for b in range(BG):
                sp.dma_start(b2d[b * E:(b + 1) * E, b * F:(b + 1) * F], d["b2_0"]).then_inc(b2_in, 16)
            sp.wait_ge(b2_in, 16 * BG)

        @block.gpsimd
        def _(pool):
            pool.memset(b2d[:, :], 0.0).then_inc(b2_zero, 1)

        @block.scalar
        def _(act):
            act.wait_ge(shifted, 1)
            act.activation(s_flat, s_flat, ACT.Exp).then_inc(exps, 1)

        @block.tensor
        def _(pe):
            pe.wait_ge(probs, 1)
            for g in range(NBG):
                for half in range(2):
                    col = (g % 2) * L + half * HALF
                    m = pe.transpose(p_s[g // 2][:, col:col + HALF],
                                     s_tok[:, half, g * BG:(g + 1) * BG, :].rearrange("t b e -> t (b e)"),
                                     ident[0:HALF, 0:HALF])
                if g % 2:
                    m.then_inc(s_t, 1)
            pe.wait_ge(gates, NBG)
            for half in range(2):
                for g in range(NBG):
                    m = pe.transpose(p_g[half][0:HALF, g * 128:(g + 1) * 128], gate[:, g, half * HALF:(half + 1) * HALF],
                                     ident[:, :])
                m.then_inc(g_t, 1)
            pe.wait_ge(b2_in, 16 * BG)
            for n in range(2 * NBG * 4):
                g, half, sub = n // 8, n // 4 % 2, n % 4
                if n >= 4:
                    pe.wait_ge(b2_added, n - 3)
                pe.matmul(p_b[n % 4][0:HALF, :], gate[:, g, half * HALF:(half + 1) * HALF],
                          b2d[:, sub * 4 * F:(sub + 1) * 4 * F], start=True, stop=True).then_inc(b2_done, 1)

        @block.vector
        def _(dve):
            ch = Chain(dve, dve_step)
            ch.link(dve.tensor_reduce(mx[:, :], s_flat, AX.X, ALU.max))
            dve.tensor_tensor(s_flat, s_flat, mx[:, :].unsqueeze(2).to_broadcast([HALF, NT, E]), ALU.subtract).then_inc(shifted, 1)
            dve.wait_ge(exps, 1)
            ch.link(dve.tensor_reduce(mx[:, :], s_flat, AX.X, ALU.add))
            ch.link(dve.reciprocal(mx[:, :], mx[:, :]))
            dve.tensor_tensor(s_flat, s_flat, mx[:, :].unsqueeze(2).to_broadcast([HALF, NT, E]), ALU.mult).then_inc(probs, 1)
            ch.link(dve.memset(ones[:, :], 1.0))
            for r in range(NBG // 2):
                dve.wait_ge(s_t, r + 1)
                ch.link(dve.tensor_copy(st[:, 2 * r:2 * r + 2, :], p_s[r][:, 0:2 * L].rearrange("p (g t) -> p g t", g=2)))
            rounds = (TOPK + 7) // 8
            for r in range(rounds):
                for g in range(NBG):
                    m = dve.max(m8[:, g, :], (st if r == 0 else work)[:, g, :])
                ch.link(m)
                if r < rounds - 1:
                    for g in range(NBG):
                        m = dve.match_replace(work[:, g, :], m8[:, g, :], (st if r == 0 else work)[:, g, :], -1.0)
                    ch.link(m)
            at = TOPK - 1 - 8 * (rounds - 1)
            for g in range(NBG):
                kth = m8[:, g, at:at + 1]
                dve.tensor_scalar(above[:, g, :], st[:, g, :], kth, None, ALU.is_gt, ALU.add, accum_out=count[:, g:g + 1])
                m = dve.tensor_scalar(equal[:, g, :], st[:, g, :], kth, None, ALU.is_equal)
            ch.link(m)
            ch.link(dve.tensor_scalar(room[:, :], count[:, :], -1.0, float(TOPK), ALU.mult, ALU.add))
            for g in range(NBG):
                m = dve.tensor_tensor_scan(rank[:, g, :], ones[:, :], equal[:, g, :], 0.0, ALU.mult, ALU.add)
            ch.link(m)
            for g in range(NBG):
                m = dve.scalar_tensor_tensor(work[:, g, :], rank[:, g, :], room[:, g:g + 1], equal[:, g, :], ALU.is_le, ALU.mult)
            ch.link(m)
            ch.link(dve.tensor_tensor(above[:, :, :], above[:, :, :], work[:, :, :], ALU.add))
            dve.tensor_tensor(gate[:, :, :], above[:, :, :], st[:, :, :], ALU.mult).then_inc(gates, NBG)
            for half in range(2):
                dve.wait_ge(g_t, half + 1)
                dve.tensor_copy(g_tok[:, half, :, :].rearrange("t b e -> t (b e)"), p_g[half][0:HALF, :])
            for n in range(2 * NBG * 4):
                g, half, sub = n // 8, n // 4 % 2, n % 4
                tiles = h[:, :].rearrange("t (b h f) -> t h b f", h=2, f=F)[:, half, g * BG + sub * 4:g * BG + sub * 4 + 4, :]
                dve.wait_ge(b2_done, n + 1)
                dve.tensor_tensor(tiles, p_b[n % 4][0:HALF, :].rearrange("t (b f) -> t b f", b=4), tiles, ALU.add).then_inc(b2_added, 1)
            dve.wait_ge(b2_added, 2 * NBG * 4)


def mixture0(nc, k, d, h, xf, g_tok):
    ctx = ExitStack()
    with ctx:
        CH = F0 // F
        w1 = k.sb(ctx, "w1_0", [F, E, F0])
        w2 = k.sb(ctx, "w2_0", [F, E, CH, F])
        b1 = k.sb(ctx, "b1_0", [F, E, CH])
        hid = k.sb(ctx, "hid", [F, 4, CH, QN])
        gq = k.sb(ctx, "gq", [HALF, 2, 2, E])
        acc = k.sb(ctx, "acc", [HALF, QF])
        p_1 = [[k.ps(ctx, f"p_1{r}{c}") for c in range(CH)] for r in range(2)]
        p_2 = [k.ps(ctx, f"p_2{r}") for r in range(4)]

        w_in = k.sem("w_in_f")
        w1_done = k.sem("w1_done")
        gelu_done = k.sem("gelu_done")
        w2_done = k.sem("w2_done")
        acc_done = k.sem("acc_done")
        gq_copied = k.sem("gq_copied")
        block = ctx.enter_context(nc.Block())

        @block.sync
        def _(sp):
            sp.dma_start(w1[:, :, :], d["w1_0"]).then_inc(w_in, 16)
            sp.dma_start(b1[:, :, :], d["b1_0"]).then_inc(w_in, 16)
            sp.dma_start(w2[:, :, :, :], d["w2_0"]).then_inc(w_in, 16)

        @block.tensor
        def _(pe):
            pe.wait_ge(w_in, 48)

            def down(n, e):
                pe.wait_ge(gelu_done, n * 2 + 2 + 4)
                pe.wait_ge(acc_done, n + 1)
                for j in range(QT):
                    for c in range(CH):
                        m = pe.matmul(p_2[e % 4][0:HALF, j * F:(j + 1) * F], hid[:, e % 4, c, j * HALF:(j + 1) * HALF],
                                      w2[:, e, c, :], start=(c == 0), stop=(c == CH - 1))
                m.then_inc(w2_done, 1)

            with pe.Fori(0, NQ) as i:
                for e in range(E):
                    n = i * E + e
                    pe.wait_ge(gelu_done, n * 2 + 2)
                    for c in range(CH):
                        pe.matmul(p_1[e % 2][c][:, 0:QN], w1[:, e, c * F:(c + 1) * F], xf[:, bass.ds(i * QN, QN)],
                                  start=True, stop=True).then_inc(w1_done, 1)
                    if e:
                        down(n - 1, e - 1)
                down(i * E + E - 1, E - 1)

        @block.scalar
        def _(act):
            act.sem_inc(gelu_done, 4)
            act.wait_ge(w_in, 48)
            with act.Fori(0, NQ) as i:
                for e in range(E):
                    n = i * E + e
                    act.wait_ge(w2_done, n + 1)
                    for c in range(CH):
                        act.wait_ge(w1_done, n * 2 + c + 1)
                        act.activation(hid[:, e % 4, c, :], p_1[e % 2][c][:, 0:QN], ACT.Gelu,
                                       bias=b1[:, e, c:c + 1]).then_inc(gelu_done, 1)

        @block.vector
        def _(dve):
            dve.sem_inc(w2_done, 4)
            dve.sem_inc(acc_done, 4)
            with dve.Fori(0, NQ) as i:
                dve.wait_ge(acc_done, i * E + 4)
                apart(dve)
                dve.tensor_copy(gq[:, :, :, :], g_tok[:, :, bass.ds(i * 2, 2), :]).then_inc(gq_copied, 1)
                dve.wait_ge(gq_copied, i + 1)
                for e in range(E):
                    n = i * E + e
                    dve.wait_ge(acc_done, n + 4)
                    dve.wait_ge(w2_done, n + 1 + 4)
                    apart(dve)
                    for j in range(QT):
                        at = bass.ds(i * QF + j * F, F)
                        a = acc[:, j * F:(j + 1) * F]
                        m = dve.scalar_tensor_tensor(h[:, at] if e == E - 1 else a, p_2[e % 4][0:HALF, j * F:(j + 1) * F],
                                                     gq[:, j % 2, j // 2, e:e + 1], h[:, at] if e == 0 else a,
                                                     ALU.mult, ALU.add)
                    m.then_inc(acc_done, 1)


def retain_and_route(nc, k, d, ident, small, h, base, xs_dram, h3_dram):
    ctx = ExitStack()
    with ctx:
        HG = 4
        STEP = [(b, half, g) for b in range(2) for half in (1, 0) for g in range(HEADS // HG)]
        NH = len(STEP)
        WL = 96
        wq = k.sb(ctx, "wq", [F, F])
        wk = k.sb(ctx, "wk", [F, F])
        wvg = k.sb(ctx, "wvg", [F, 2 * F])
        bvg = k.sb(ctx, "bvg", [HALF, 2 * F])
        wg1 = k.sb(ctx, "wg1", [F, WL])
        bg1 = k.sb(ctx, "bg1", [HALF, E])
        prio = k.sb(ctx, "prio", [HALF, E])
        before_f = k.sb(ctx, "before_f", [HALF, HALF])
        before = k.sb(ctx, "before", [HALF, HALF], BF16)
        ones = k.sb(ctx, "ones_g", [HALF, HALF], BF16)
        decay = k.sb(ctx, "decay", [HALF, HEADS, HALF])
        decay_i = k.sb(ctx, "decay_i", [F, HALF])
        decay_j = k.sb(ctx, "decay_j", [HALF, F])
        same = k.sb(ctx, "same", [F, F])
        bk_row = k.sb(ctx, "bk_row", [HALF, F])
        nhalf = k.sb(ctx, "nhalf_g", [HALF, QT])

        def norm_buffers(name):
            return (k.sb(ctx, "lst_" + name, [HALF, 2, QT, 6]), k.sb(ctx, "lmv_" + name, [HALF, 2, QT, 2]),
                    k.sb(ctx, "lve_" + name, [HALF, 2, QT]), k.sb(ctx, "lrs_" + name, [HALF, 2, QT]))

        prep_norm = norm_buffers("p")
        route_norm = norm_buffers("r")
        xn = k.sb(ctx, "xn_g", [HALF, 2, QF])
        xt = k.sb(ctx, "xt_g", [F, 2, QN])
        qm = k.sb(ctx, "qm", [F, 2, HEADS, QN])
        kt = k.sb(ctx, "kt", [F, 2, QN])
        q_first = k.sb(ctx, "q_first", [F, 2, HALF])
        q_decay = k.sb(ctx, "q_decay", [F, 2, 2, HALF])
        k_sum = k.sb(ctx, "k_sum", [HALF, 2, F])
        k_decay = k.sb(ctx, "k_decay", [HALF, 2, F])
        state = k.sb(ctx, "state", [F, 2, F])
        vp = k.sb(ctx, "vp", [HALF, 2, QT, HEADS, F])
        gate = k.sb(ctx, "gate_g", [HALF, QF])
        silu = k.sb(ctx, "silu", [HALF, 2, QF])
        probs = k.sb(ctx, "probs_g", [HALF, 4, QN])
        gated = k.sb(ctx, "gated", [HALF, QF])
        h3 = k.sb(ctx, "h3", [HALF, 2, QF])
        xr = k.sb(ctx, "xr", [HALF, 2, QF])
        xrt = k.sb(ctx, "xrt", [F, QN])
        xs = k.sb(ctx, "xs", [HALF, 2, QF])
        lg = k.sb(ctx, "lg", [HALF, QT, E])
        ez = k.sb(ctx, "ez", [HALF, QT, E])
        eq = k.sb(ctx, "eq", [HALF, QT, E])
        hot = k.sb(ctx, "hot", [HALF, QT, E], BF16)
        pz = k.sb(ctx, "pz", [HALF, QT, E])
        r4 = k.sb(ctx, "r4", [HALF, 6, QT])
        idx = k.sb(ctx, "idx", [HALF, 2, QT], I32)
        p_a = k.ps(ctx, "p_a")
        p_b = k.ps(ctx, "p_bq")
        p_s = [k.ps(ctx, f"p_sc{r}") for r in range(2)]
        p_o = [k.ps(ctx, f"p_o{u}") for u in range(2)]
        p_r = k.ps(ctx, "p_r")
        p_l = k.ps(ctx, "p_lr")

        consts = k.sem("consts_g")
        set_up = k.sem("set_up")
        wg1_cleared = k.sem("wg1_cleared")
        prep_step = k.sem("prep_step")
        route_step = k.sem("route_step")
        k_step = k.sem("k_step")
        pool_prep = k.sem("pool_prep")
        pool_route = k.sem("pool_route")
        var_p = k.sem("var_p")
        var_r = k.sem("var_r")
        rstd_p = k.sem("rstd_p")
        rstd_r = k.sem("rstd_r")
        xn_ready = k.sem("xn_ready_g")
        xt_done = k.sem("xt_done_g")
        xt_copied = k.sem("xt_copied_g")
        q_done = k.sem("q_done")
        q_copied = k.sem("q_copied")
        k_done = k.sem("k_done")
        k_copied = k.sem("k_copied")
        vg_done = k.sem("vg_done")
        v_added = k.sem("v_added")
        k_tok_done = k.sem("k_tok_done")
        k_decayed = k.sem("k_decayed")
        q_decayed = k.sem("q_decayed")
        state_done = k.sem("state_done")
        state_copied = k.sem("state_copied")
        silu_done = k.sem("silu_done")
        s_done = k.sem("s_done")
        decayed = k.sem("decayed")
        av_done = k.sem("av_done")
        h3_done = k.sem("h3_done")
        h3_out = [k.sem(f"h3_out{u}") for u in range(2)]
        xr_ready = k.sem("xr_ready")
        xr_done = k.sem("xr_done")
        xr_copied = k.sem("xr_copied")
        lg_done = k.sem("lg_done")
        z_ready = k.sem("z_ready")
        ez_done = k.sem("ez_done")
        hot_ready = k.sem("hot_ready")
        pre_done = k.sem("pre_done")
        idx_done = k.sem("idx_done")
        sent = [k.sem(f"sent{u}") for u in range(2)]
        xs_free = k.sem("xs_free")
        block = ctx.enter_context(nc.Block())

        @block.sync
        def _(sp):
            for name, to in (("wq", wq), ("wk", wk), ("wvg", wvg), ("before", before_f), ("decay_i", decay_i), ("decay_j", decay_j), ("same", same)):
                sp.dma_start(to[:, :], d[name]).then_inc(consts, 16)
            sp.dma_start(decay[:, :, :], d["decay"]).then_inc(consts, 16)
            sp.wait_ge(wg1_cleared, 1)
            sp.dma_start(wg1[:, 0:E], d["wg1"]).then_inc(consts, 16)
            for name, to, n in (("bvg", bvg, 2 * F), ("bg1", bg1, E), ("prio", prio, E), ("bk", bk_row, F), ("region", base, E)):
                sp.dma_start(to[:, :], bass.AP(d[name].tensor, 0, [[0, HALF], [1, n]])).then_inc(consts, 16)

            def store(q, u):
                sp.wait_ge(h3_done, q + 1 + 2)
                dst = h3_dram[bass.ds(q * QN, QN), :].rearrange("(j t) f -> t j f", j=QT)
                sp.dma_start(dst, h3[:, u, :].rearrange("t (j f) -> t j f", j=QT)).then_inc(h3_out[u], 16)

            with sp.Fori(0, NQ // 2) as j:
                for u in range(2):
                    store(j * 2 + u, u)
            for u in range(2):
                sp.wait_ge(h3_out[u], 16 * (NQ // 2 + 1))

        @block.tensor
        def _(pe):
            pe.wait_ge(consts, 224)
            pe.wait_ge(set_up, 5)

            def prep_x(q, u):
                pe.wait_ge(xn_ready, q + 1)
                pe.wait_ge(state_copied, q + 1)
                for j in range(QT):
                    m = pe.transpose(p_a[:, j * HALF:(j + 1) * HALF], xn[:, u, j * F:(j + 1) * F], ident[0:HALF, 0:HALF])
                m.then_inc(xt_done, 1)

            def prep_q(q, u):
                pe.wait_ge(xt_copied, q + 1)
                pe.matmul(p_b[:, 0:QN], wq[:, :], xt[:, u, :], start=True, stop=True).then_inc(q_done, 1)

            def prep_k(q, u):
                pe.matmul(p_a[:, 0:QN], wk[:, :], xt[:, u, :], start=True, stop=True).then_inc(k_done, 1)

            def prep_v(q, u):
                pe.wait_ge(q_copied, q + 1)
                for b in range(2):
                    if b:
                        pe.wait_ge(k_copied, q + 1)
                    for half in range(2):
                        j = 2 * b + half
                        m = pe.matmul((p_b, p_a)[b][0:HALF, half * 2 * F:(half + 1) * 2 * F],
                                      xt[:, u, j * HALF:(j + 1) * HALF], wvg[:, :], start=True, stop=True)
                    m.then_inc(vg_done, 1)

            def scores(q, u, n):
                if n == 0:
                    pe.wait_ge(q_copied, q + 1)
                    pe.wait_ge(k_copied, q + 1)
                pe.wait_ge(decayed, q * NH + n + 1)
                b, half, g = STEP[n]
                tile = slice((2 * b + half) * HALF, (2 * b + half + 1) * HALF)
                pe.matmul(p_s[n % 2][0:HALF, 0:QN], kt[:, u, tile], qm[:, u, g * HG:(g + 1) * HG, tile],
                          start=True, stop=True).then_inc(s_done, 1)

            def prep_k_tokens(q, u):
                pe.wait_ge(v_added, q * 2 + 1 + 2)
                for b in range(2):
                    m = pe.matmul(p_b[0:HALF, b * F:(b + 1) * F], xt[:, u, (2 * b + 1) * HALF:(2 * b + 2) * HALF], wk[:, :],
                                  start=True, stop=True)
                m.then_inc(k_tok_done, 1)

            def prep_state(q, u):
                pe.wait_ge(v_added, q * 2 + 2 + 2)
                pe.wait_ge(k_decayed, q + 1)
                for b in range(2):
                    m = pe.matmul(p_a[:, b * F:(b + 1) * F], k_decay[:, b, :], vp[:, u, 2 * b + 1, :, 0:HD], start=True, stop=True)
                m.then_inc(state_done, 1)

            def values(q, u, n):
                if n == 0:
                    pe.wait_ge(h3_done, q + 1)
                    pe.wait_ge(v_added, q * 2 + 2 + 2)
                pe.wait_ge(decayed, q * NH + n + 1 + 2)
                b, half, g = STEP[n]
                first, last = g == 0, g == HEADS // HG - 1
                flat = vp[:, u, 2 * b + half, :, :].rearrange("t h x -> t (h x)")
                to = p_o[u][0:HALF, (2 * b + half) * F:(2 * b + half + 1) * F]
                for c in range(HG):
                    head = g * HG + c
                    at = head * (F - HD)
                    m = pe.matmul(to, probs[:, n % 4, c * HALF:(c + 1) * HALF], flat[:, at:at + F],
                                  start=(first and c == 0), stop=(last and half == 1 and c == HG - 1))
                if last and half == 0:
                    pe.wait_ge(q_decayed, q + 1 + 1)
                    pe.wait_ge(state_copied, q + 1 + 1)
                    m = pe.matmul(to, q_decay[:, u, b, :], state[:, b, :], start=False, stop=True)
                m.then_inc(av_done, 1)

            def route_x(q, u):
                pe.wait_ge(xr_ready, q + 1)
                pe.wait_ge(xr_copied, q + 1)
                for j in range(QT):
                    m = pe.transpose(p_r[:, j * HALF:(j + 1) * HALF], xr[:, u, j * F:(j + 1) * F], ident[0:HALF, 0:HALF])
                m.then_inc(xr_done, 1)

            def route_logits(q):
                pe.wait_ge(xr_copied, q + 2)
                pe.wait_ge(idx_done, q + 1)
                for j in range(QT):
                    m = pe.matmul(p_l[0:HALF, j * WL:(j + 1) * WL], xrt[:, j * HALF:(j + 1) * HALF], wg1[:, :],
                                  start=True, stop=True)
                m.then_inc(lg_done, 1)

            def route_places(q):
                pe.wait_ge(hot_ready, q + 1)
                for j in range(QT + 1):
                    to = p_l[0:HALF, QT * WL + j * E:QT * WL + (j + 1) * E]
                    if j < QT:
                        m = pe.matmul(to, before[:, :], hot[:, j, :], start=True, stop=(j == 0))
                    for i in range(j):
                        m = pe.matmul(to, ones[:, :], hot[:, i, :], start=(j == QT and i == 0), stop=(i == j - 1))
                m.then_inc(pre_done, 1)

            def quad(q, u, prep, route, place):
                for n in range(NH):
                    scores(q, u, n)
                    if n:
                        values(q, u, n - 1)
                    if n == 0:
                        prep_state(q, u)
                    if place and n == 1:
                        route_places(q - 2)
                    if prep and n == 2:
                        prep_x(q + 1, 1 - u)
                    if prep and n == 3:
                        prep_q(q + 1, 1 - u)
                        prep_k(q + 1, 1 - u)
                    if prep and n == 6:
                        prep_v(q + 1, 1 - u)
                    if route and n == 6:
                        route_x(q - 1, 1 - u)
                    if route and n == 7:
                        route_logits(q - 1)
                if prep:
                    prep_k_tokens(q + 1, 1 - u)
                values(q, u, NH - 1)

            prep_x(0, 0)
            prep_q(0, 0)
            prep_k(0, 0)
            prep_v(0, 0)
            prep_k_tokens(0, 0)
            quad(0, 0, True, False, False)
            quad(1, 1, True, True, False)
            for q in (2, 3):
                quad(q, q % 2, True, True, True)
            with pe.Fori(2, NQ // 2 - 1) as t:
                for u in range(2):
                    quad(t * 2 + u, u, True, True, True)
            quad(NQ - 2, 0, True, True, True)
            quad(NQ - 1, 1, False, True, True)
            route_places(NQ - 2)
            route_x(NQ - 1, 1)
            route_logits(NQ - 1)
            route_places(NQ - 1)

        @block.scalar
        def _(act):
            act.sem_inc(xr_copied, 1)
            for u in range(2):
                act.sem_inc(h3_out[u], 16)
            act.wait_ge(set_up, 5)

            def prep_x(q, u):
                act.wait_ge(k_tok_done, q + 1)
                act.wait_ge(xt_done, q + 1 + 2)
                act.activation(xt[:, u, :], p_a[:, 0:QN], ACT.Copy).then_inc(xt_copied, 1)

            def prep_q(q, u):
                act.wait_ge(s_done, q * NH + NH)
                act.wait_ge(q_done, q + 1)
                for head in range(HEADS):
                    rows, odd = slice(head // 2 * 32, head // 2 * 32 + 32), head % 2
                    act.activation(qm[rows, u, head, :], p_b[rows, 0:QN], ACT.Identity, bias=small[rows, 6 + odd:7 + odd],
                                       scale=small[rows, 2 + odd:3 + odd])
                act.wait_ge(q_decayed, q + 1)
                act.activation(q_first[:, :, :], p_b[:, 0:QN].rearrange("f (b o t) -> f b o t", b=2, o=2)[:, :, 0, :],
                               ACT.Identity, bias=small[:, 4:5]).then_inc(q_copied, 1)

            def prep_k(q, u):
                act.wait_ge(s_done, q * NH + NH)
                act.wait_ge(k_done, q + 1)
                act.activation(kt[:, u, :], p_a[:, 0:QN], ACT.Identity, bias=small[:, 5:6]).then_inc(k_copied, 1)

            def prep_silu(q, u):
                act.wait_ge(h3_done, q + 1)
                act.wait_ge(v_added, q * 2 + 2 + 2)
                act.activation(silu[:, u, :], gate[:, :], ACT.Silu).then_inc(silu_done, 1)

            def route_x(q):
                act.wait_ge(lg_done, q + 1)
                act.wait_ge(xr_done, q + 1 + 2)
                act.activation(xrt[:, :], p_r[:, 0:QN], ACT.Copy).then_inc(xr_copied, 1)

            def route_exp(q):
                act.wait_ge(z_ready, q + 1)
                act.activation(ez[:, :, :], lg[:, :, :], ACT.Exp).then_inc(ez_done, 1)

            def quad(q, u, prep, route):
                if prep:
                    prep_x(q + 1, 1 - u)
                    prep_q(q + 1, 1 - u)
                    prep_k(q + 1, 1 - u)
                if route:
                    route_x(q - 1)
                    route_exp(q - 1)
                if prep:
                    prep_silu(q + 1, 1 - u)

            prep_x(0, 0)
            prep_q(0, 0)
            prep_k(0, 0)
            prep_silu(0, 0)
            quad(0, 0, True, False)
            for q in (1, 2, 3):
                quad(q, q % 2, True, True)
            with act.Fori(2, NQ // 2 - 1) as t:
                for u in range(2):
                    quad(t * 2 + u, u, True, True)
            quad(NQ - 2, 0, True, True)
            quad(NQ - 1, 1, False, True)
            route_x(NQ - 1)
            route_exp(NQ - 1)

        @block.gpsimd
        def _(pool):
            pool.memset(nhalf[:, :], -0.5)
            pool.memset(vp[:, :, :, :, :], 0.0).then_inc(set_up, 1)
            pool.wait_ge(set_up, 5)

            def rstd(q, u, var, bufs, step, done):
                _, lmv, lve, lrs = bufs
                pool.wait_ge(var, q + 1)
                apart(pool)
                ch = Chain(pool, step, q, 1)
                ch.link(pool.tensor_scalar(lve[:, u, :], lmv[:, u, :, 1], EPS, None, ALU.add))
                pool.tensor_tensor(out=lrs[:, u, :], in0=lve[:, u, :], in1=nhalf[:, :], op=ALU.pow).then_inc(done, 1)

            def send(q, u, t):
                if not (isinstance(q, int) and q == 0):
                    pool.wait_ge(sent[1 - u], (t + u) * 64)
                    pool.sem_inc(xs_free, 1)
                pool.wait_ge(idx_done, q + 2)
                apart(pool)
                for j in range(QT):
                    pool.indirect_dma_start(xs_dram[:, :], bass.IndirectOffsetOnAxis(ap=idx[:, u, j:j + 1], axis=0),
                                            xs[:, u, j * F:(j + 1) * F], None).then_inc(sent[u], 16)

            def quad(q, u, t, prep, route, place):
                if prep:
                    rstd(q + 1, 1 - u, var_p, prep_norm, pool_prep, rstd_p)
                if route:
                    rstd(q - 1, 1 - u, var_r, route_norm, pool_route, rstd_r)
                if place:
                    send(q - 2, u, t - 1)

            rstd(0, 0, var_p, prep_norm, pool_prep, rstd_p)
            quad(0, 0, 0, True, False, False)
            quad(1, 1, 0, True, True, False)
            for q in (2, 3):
                quad(q, q % 2, 1, True, True, True)
            with pool.Fori(2, NQ // 2 - 1) as t:
                for u in range(2):
                    quad(t * 2 + u, u, t, True, True, True)
            quad(NQ - 2, 0, NQ // 2 - 1, True, True, True)
            quad(NQ - 1, 1, NQ // 2 - 1, False, True, True)
            send(NQ - 2, 0, NQ // 2 - 1)
            rstd(NQ - 1, 1, var_r, route_norm, pool_route, rstd_r)
            send(NQ - 1, 1, NQ // 2 - 1)
            for u in range(2):
                pool.wait_ge(sent[u], 64 * (NQ // 2))

        @block.vector
        def _(dve):
            for s, n in ((xt_done, 2), (vg_done, 4), (v_added, 2), (s_done, 2 * NH), (decayed, 2), (av_done, 2 * NH),
                         (h3_done, 2), (xr_done, 2), (lg_done, 1), (silu_done, 1), (idx_done, 1), (k_tok_done, 2),
                         (q_decayed, 1), (state_done, 1), (state_copied, 1), (xs_free, 2)):
                dve.sem_inc(s, n)
            dve.memset(wg1[:, :], 0.0).then_inc(wg1_cleared, 1)
            dve.memset(qm[:, :, :, :], 0.0).then_inc(set_up, 1)
            dve.wait_ge(consts, 224)
            dve.tensor_copy(before[:, :], before_f[:, :])
            dve.memset(ones[:, :], 1.0).then_inc(set_up, 1)
            dve.tensor_tensor(small[:, 6:7], small[:, 4:5], small[:, 2:3], ALU.mult).then_inc(set_up, 1)
            dve.tensor_tensor(small[:, 7:8], small[:, 4:5], small[:, 3:4], ALU.mult).then_inc(set_up, 1)

            def stats(ch, u, bufs, src, var):
                lst, lmv, _, _ = bufs
                for j in range(QT):
                    m = dve.bn_stats(lst[:, u, j, :], src(j))
                ch.link(m)
                apart(dve)
                for j in range(QT):
                    m = dve.bn_aggr(lmv[:, u, j, :], lst[:, u, j, :])
                m.then_inc(var, 1)

            def normed(u, bufs, src, to):
                _, lmv, _, lrs = bufs
                for j in range(QT):
                    m = dve.tensor_scalar(to[:, u, j * F:(j + 1) * F], src(j), lmv[:, u, j, 0:1], lrs[:, u, j:j + 1],
                                          ALU.subtract, ALU.mult)
                return m

            def prep_stats(q, u):
                stats(Chain(dve, prep_step, q, 1), u, prep_norm, lambda j: h[:, bass.ds(q * QF + j * F, F)], var_p)

            def prep_xn(q, u):
                dve.wait_ge(xt_done, q + 1)
                dve.wait_ge(rstd_p, q + 1)
                apart(dve)
                normed(u, prep_norm, lambda j: h[:, bass.ds(q * QF + j * F, F)], xn).then_inc(xn_ready, 1)

            def prep_vg(q, u):
                dve.wait_ge(av_done, q * NH + NH)
                dve.wait_ge(silu_done, q + 1)
                for b in range(2):
                    dve.wait_ge(vg_done, q * 2 + b + 1 + 4)
                    src = (p_b, p_a)[b][0:HALF, :].rearrange("t (j n) -> t j n", j=2)
                    for half in range(2):
                        dve.tensor_tensor(vp[:, u, 2 * b + half, :, 0:HD], src[:, half, 0:F].rearrange("t (h x) -> t h x", h=HEADS),
                                          bvg[:, 0:F].rearrange("t (h x) -> t h x", h=HEADS), ALU.add)
                    dve.tensor_tensor(gate[:, b * 2 * F:(b + 1) * 2 * F].rearrange("t (j f) -> t j f", j=2), src[:, :, F:2 * F],
                                      bvg[:, F:2 * F].unsqueeze(1).to_broadcast([HALF, 2, F]), ALU.add).then_inc(v_added, 1)

            def prep_q_decay(q, u):
                dve.wait_ge(av_done, q * NH + NH)
                dve.wait_ge(q_copied, q + 1)
                dve.tensor_tensor(q_decay[:, u, :, :], q_first[:, :, :], decay_i[:, :].unsqueeze(1).to_broadcast([F, 2, HALF]),
                                  ALU.mult).then_inc(q_decayed, 1)

            def prep_k_decay(q):
                ch = Chain(dve, k_step, q, 1)
                dve.wait_ge(k_tok_done, q + 1 + 2)
                ch.link(dve.tensor_tensor(k_sum[:, :, :], p_b[0:HALF, 0:2 * F].rearrange("t (b f) -> t b f", b=2),
                                          bk_row[:, :].unsqueeze(1).to_broadcast([HALF, 2, F]), ALU.add))
                dve.wait_ge(state_done, q + 1)
                dve.tensor_tensor(k_decay[:, :, :], k_sum[:, :, :], decay_j[:, :].unsqueeze(1).to_broadcast([HALF, 2, F]),
                                  ALU.mult).then_inc(k_decayed, 1)

            def keep_state(q):
                dve.wait_ge(av_done, q * NH + 2 * NH)
                dve.wait_ge(state_done, q + 1 + 1)
                dve.tensor_tensor(state[:, :, :], p_a[:, 0:2 * F].rearrange("p (b f) -> p b f", b=2),
                                  same[:, :].unsqueeze(1).to_broadcast([F, 2, F]), ALU.mult).then_inc(state_copied, 1)

            def decaying(q, n):
                g = STEP[n][2]
                dve.wait_ge(av_done, q * NH + n - 3 + 2 * NH)
                dve.wait_ge(s_done, q * NH + n + 1 + 2 * NH)
                dve.tensor_tensor(probs[:, n % 4, :], p_s[n % 2][0:HALF, 0:QN],
                                  decay[:, g * HG:(g + 1) * HG, :].rearrange("t h x -> t (h x)"), ALU.mult).then_inc(decayed, 1)

            def finish(ch, q, u, t):
                dve.wait_ge(av_done, q * NH + NH + 2 * NH)
                dve.wait_ge(silu_done, q + 1 + 1)
                ch.link(dve.tensor_tensor(gated[:, :], p_o[u][0:HALF, :], silu[:, u, :], ALU.mult))
                dve.wait_ge(h3_out[u], t * 16 + 16)
                apart(dve)
                dve.tensor_tensor(h3[:, u, :], gated[:, :], h[:, bass.ds(q * QF, QF)], ALU.add).then_inc(h3_done, 1)

            def route_stats(ch, q, u):
                dve.wait_ge(h3_done, q + 1 + 2)
                stats(ch, u, route_norm, lambda j: h3[:, u, j * F:(j + 1) * F], var_r)

            def route_xn(q, u):
                dve.wait_ge(xr_done, q + 1)
                dve.wait_ge(rstd_r, q + 1)
                normed(u, route_norm, lambda j: h3[:, u, j * F:(j + 1) * F], xr).then_inc(xr_ready, 1)

            def over_e(r):
                return r4[:, r, :].unsqueeze(2).to_broadcast([HALF, QT, E])

            def over_j(c):
                return c[:, :].unsqueeze(1).to_broadcast([HALF, QT, E])

            def logits(ch, q):
                dve.wait_ge(lg_done, q + 1 + 1)
                ch.link(dve.tensor_tensor(lg[:, :, :], p_l[0:HALF, 0:QT * WL].rearrange("t (j e) -> t j e", j=QT)[:, :, 0:E], over_j(bg1), ALU.add))
                ch.link(dve.tensor_reduce(r4[:, 0, :], lg[:, :, :], AX.X, ALU.max))
                dve.tensor_tensor(lg[:, :, :], lg[:, :, :], over_e(0), ALU.subtract).then_inc(z_ready, 1)

            def choice(ch, q, u):
                dve.wait_ge(ez_done, q + 1)
                dve.tensor_reduce(r4[:, 1, :], ez[:, :, :], AX.X, ALU.add)
                ch.link(dve.tensor_reduce(r4[:, 2, :], ez[:, :, :], AX.X, ALU.max))
                dve.reciprocal(r4[:, 3, :], r4[:, 1, :])
                ch.link(dve.tensor_tensor(eq[:, :, :], ez[:, :, :], over_e(2), ALU.is_equal))
                dve.tensor_tensor(r4[:, 4, :], r4[:, 2, :], r4[:, 3, :], ALU.mult)
                ch.link(dve.tensor_tensor(eq[:, :, :], eq[:, :, :], over_j(prio), ALU.mult))
                ch.link(dve.tensor_reduce(r4[:, 5, :], eq[:, :, :], AX.X, ALU.max))
                dve.tensor_tensor(hot[:, :, :], eq[:, :, :], over_e(5), ALU.is_equal).then_inc(hot_ready, 1)

            def rows(q, u):
                dve.wait_ge(xs_free, q + 1)
                dve.tensor_tensor(xs[:, u, :].rearrange("t (j f) -> t j f", j=QT), xr[:, u, :].rearrange("t (j f) -> t j f", j=QT),
                                  r4[:, 4, :].unsqueeze(2).to_broadcast([HALF, QT, F]), ALU.mult)

            def places(ch, q, u):
                dve.wait_ge(pre_done, q + 1)
                pl = p_l[0:HALF, QT * WL:QT * WL + (QT + 1) * E]
                ch.link(dve.tensor_tensor(pz[:, :, :], pl[:, 0:QT * E].rearrange("t (j e) -> t j e", j=QT), over_j(base), ALU.add))
                dve.tensor_tensor(base[:, :], pl[:, QT * E:(QT + 1) * E], base[:, :], ALU.add)
                ch.link(dve.tensor_tensor(pz[:, :, :], pz[:, :, :], hot[:, :, :], ALU.mult))
                ch.link(dve.tensor_reduce(r4[:, 0, :], pz[:, :, :], AX.X, ALU.add))
                dve.tensor_copy(idx[:, u, :], r4[:, 0, :]).then_inc(idx_done, 1)

            ROUTE_LINKS, PLACE_LINKS = 11, 3

            def place(q, u):
                ch = Chain(dve, route_step, q, ROUTE_LINKS, ROUTE_LINKS - PLACE_LINKS)
                places(ch, q, u)
                assert ch.n == PLACE_LINKS

            def quad(q, u, t, prep, route, placing):
                if route:
                    ch = Chain(dve, route_step, q - 1, ROUTE_LINKS)
                for n in range(NH):
                    decaying(q, n)
                    if prep and n == 0:
                        prep_stats(q + 1, 1 - u)
                    if n == 1:
                        keep_state(q)
                    if placing and n == 2:
                        place(q - 2, u)
                    if prep and n == 1:
                        prep_xn(q + 1, 1 - u)
                    if route and n == 2:
                        finish(ch, q - 1, 1 - u, t - 1 if u == 0 else t)
                    if route and n == 3:
                        route_stats(ch, q - 1, 1 - u)
                    if route and n == 4:
                        route_xn(q - 1, 1 - u)
                    if prep and n == 5:
                        prep_q_decay(q + 1, 1 - u)
                    if prep and n == 6:
                        prep_vg(q + 1, 1 - u)
                if prep:
                    prep_k_decay(q + 1)
                if route:
                    logits(ch, q - 1)
                    choice(ch, q - 1, 1 - u)
                    rows(q - 1, 1 - u)
                    assert ch.n == ROUTE_LINKS - PLACE_LINKS

            prep_stats(0, 0)
            prep_xn(0, 0)
            prep_q_decay(0, 0)
            prep_vg(0, 0)
            prep_k_decay(0)
            quad(0, 0, 0, True, False, False)
            quad(1, 1, 0, True, True, False)
            for q in (2, 3):
                quad(q, q % 2, 1, True, True, True)
            with dve.Fori(2, NQ // 2 - 1) as t:
                for u in range(2):
                    quad(t * 2 + u, u, t, True, True, True)
            quad(NQ - 2, 0, NQ // 2 - 1, True, True, True)
            quad(NQ - 1, 1, NQ // 2 - 1, False, True, True)
            place(NQ - 2, 0)
            ch = Chain(dve, route_step, NQ - 1, ROUTE_LINKS)
            finish(ch, NQ - 1, 1, NQ // 2 - 1)
            route_stats(ch, NQ - 1, 1)
            route_xn(NQ - 1, 1)
            logits(ch, NQ - 1)
            choice(ch, NQ - 1, 1)
            rows(NQ - 1, 1)
            place(NQ - 1, 1)


def plan_tiles(nc, k, d, base, tab, xs_dram, h3_dram):
    ctx = ExitStack()
    with ctx:
        zeros = k.sb(ctx, "zeros", [128, RB // 128 * F])
        v = k.sb(ctx, "v_h", [1, 10, E])
        vi = k.sb(ctx, "vi_h", [1, 3, E], I32)
        kk = k.sb(ctx, "kk", [1, NK, E])
        a = k.sb(ctx, "a_h", [1, NK, E])
        ind = k.sb(ctx, "ind", [1, NK, E])
        val = k.sb(ctx, "val", [1, 2, NK, E])
        tf = k.sb(ctx, "tf", [1, 3, NK])
        consts = k.sem("consts_h")
        zero_set = k.sem("zero_set")
        ends_ready = k.sem("ends_ready")
        zero_out = k.sem("zero_out")
        step = k.sem("step_h")
        block = ctx.enter_context(nc.Block())

        @block.gpsimd
        def _(pool):
            pool.memset(zeros[:, :], 0.0).then_inc(zero_set, 1)

        def rows(ap):
            return ap.rearrange("(p r) f -> p (r f)", p=128)

        @block.sync
        def _(sp):
            sp.dma_start(kk[:, :, :], d["kk"]).then_inc(consts, 16)
            sp.dma_start(v[:, 8, :], d["region"]).then_inc(consts, 16)
            sp.dma_start(v[:, 9, :], d["number"]).then_inc(consts, 16)
            sp.wait_ge(zero_set, 1)
            sp.dma_start(rows(h3_dram[TOK:TOK + RB, :]), zeros[:, :]).then_inc(zero_out, 16)
            sp.dma_start(rows(xs_dram[DUMMY_IN:DUMMY_IN + RB, :]), zeros[:, :]).then_inc(zero_out, 16)
            sp.wait_ge(ends_ready, 1)
            for e in range(E):
                row = sp.value_load(vi[0:1, 0, e:e + 1], min_val=e * REG, max_val=e * REG + TOK)
                sp.dma_start(rows(xs_dram[bass.ds(row, RB), :]), zeros[:, :]).then_inc(zero_out, 16)
            sp.wait_ge(zero_out, 16 * (E + 2))

        @block.vector
        def _(dve):
            ch = Chain(dve, step)
            count, tiles, off, first, ones, last, region, number = (v[:, r, :] for r in (0, 1, 2, 3, 4, 5, 8, 9))
            ch.link(dve.memset(ones, 1.0))
            dve.wait_ge(consts, 48)
            dve.tensor_copy(vi[:, 0, :], base[0:1, :]).then_inc(ends_ready, 1)
            ch.link(dve.tensor_tensor(count, base[0:1, :], region, ALU.subtract))
            ch.link(dve.tensor_scalar(tiles, count, float(RB - 1), None, ALU.add))
            ch.link(dve.tensor_copy(vi[:, 1, :], tiles))
            ch.link(dve.tensor_scalar(vi[:, 2, :], vi[:, 1, :], RB.bit_length() - 1, None, ALU.logical_shift_right))
            ch.link(dve.tensor_copy(tiles, vi[:, 2, :]))
            ch.link(dve.tensor_tensor_scan(off, ones, count, 0.0, ALU.mult, ALU.add))
            ch.link(dve.tensor_tensor(off, off, count, ALU.subtract))
            ch.link(dve.tensor_tensor_scan(last, ones, tiles, 0.0, ALU.mult, ALU.add))
            ch.link(dve.tensor_tensor(first, last, tiles, ALU.subtract))

            def wide(r):
                return r.unsqueeze(1).to_broadcast([1, NK, E])

            ch.link(dve.tensor_tensor(a[:, :, :], kk[:, :, :], wide(last), ALU.is_lt))
            ch.link(dve.tensor_tensor(ind[:, :, :], kk[:, :, :], wide(first), ALU.is_ge))
            ch.link(dve.tensor_tensor(ind[:, :, :], ind[:, :, :], a[:, :, :], ALU.mult))
            ch.link(dve.tensor_tensor(a[:, :, :], kk[:, :, :], wide(first), ALU.subtract))
            ch.link(dve.tensor_scalar(a[:, :, :], a[:, :, :], float(RB), None, ALU.mult))
            for r, (start, none) in enumerate(((region, DUMMY_IN), (off, DUMMY_OUT))):
                ch.link(dve.tensor_tensor(val[:, r, :, :], a[:, :, :], wide(start), ALU.add))
                ch.link(dve.tensor_scalar(val[:, r, :, :], val[:, r, :, :], -float(none), None, ALU.add))
                ch.link(dve.tensor_tensor(val[:, r, :, :], val[:, r, :, :], ind[:, :, :], ALU.mult))
                ch.link(dve.tensor_reduce(tf[:, r, :], val[:, r, :, :], AX.X, ALU.add))
                ch.link(dve.tensor_scalar(tf[:, r, :], tf[:, r, :], float(none), None, ALU.add))
            ch.link(dve.tensor_tensor(a[:, :, :], ind[:, :, :], wide(number), ALU.mult))
            ch.link(dve.tensor_reduce(tf[:, 2, :], a[:, :, :], AX.X, ALU.add))
            ch.link(dve.tensor_copy(tab[:, :, :], tf[:, :, :]))


def mixture1(nc, k, d, ident, tab, xs_dram, h3_dram, out):
    ctx = ExitStack()
    with ctx:
        CH = F1 // F
        RP = RB // 128
        RING = 4
        TURNS = (NK - RING) // RING
        w1 = k.sb(ctx, "w1_1", [F, E * F1])
        w2 = k.sb(ctx, "w2_1", [F, E * CH * F])
        b1 = k.sb(ctx, "b1_1", [F, E * CH])
        b2 = k.sb(ctx, "b2_1", [128, E * F])
        w1e = k.sb(ctx, "w1e", [F, 2, F1])
        b1e = k.sb(ctx, "b1e", [F, 2, CH])
        xs = k.sb(ctx, "xs_i", [128, RING, RP, F])
        xt = k.sb(ctx, "xt_i", [F, 2, RB])
        h3 = k.sb(ctx, "h3_i", [128, RING, RP, F])
        hid = k.sb(ctx, "hid_i", [F, 2, CH, RB])
        y = k.sb(ctx, "y_i", [128, 2, RP, F])
        res = k.sb(ctx, "res", [128, RING, RP, F])
        p_x = [k.ps(ctx, f"p_xi{u}") for u in range(2)]
        p_u = [[k.ps(ctx, f"p_ui{u}{r}") for r in range(2)] for u in range(2)]
        p_y = [k.ps(ctx, f"p_yi{u}") for u in range(2)]
        w_in = k.sem("w_in_i")
        w2_in = k.sem("w2_in_i")
        w1e_copied = k.sem("w1e_copied")
        xs_in = [k.sem(f"xs_in{u}") for u in range(RING)]
        h3_in = [k.sem(f"h3_in{u}") for u in range(RING)]
        stored = k.sem("stored")
        x_done = k.sem("x_done")
        x_copied = k.sem("x_copied")
        up_done = k.sem("up_done")
        relu_done = k.sem("relu_done_i")
        y_done = k.sem("y_done_i")
        y_step = k.sem("y_step")
        res_done = k.sem("res_done")
        block = ctx.enter_context(nc.Block())

        @block.sync
        def _(sp):
            sp.dma_start(w1[:, :], d["w1_1"]).then_inc(w_in, 16)
            sp.dma_start(b1[:, :], d["b1_1"]).then_inc(w_in, 16)

            def load_x(t, u):
                row = sp.value_load(tab[0:1, 0, bass.ds(t, 1)], min_val=0, max_val=DUMMY_IN)
                sp.wait_ge(x_done, t + 1)
                sp.dma_start(xs[:, u, :, :], xs_dram[bass.ds(row, RB), :].rearrange("(p r) f -> p r f", r=RP)).then_inc(xs_in[u], 16)

            def load_h(t, u):
                row = sp.value_load(tab[0:1, 1, bass.ds(t, 1)], min_val=0, max_val=DUMMY_OUT)
                sp.wait_ge(res_done, t + 1)
                sp.dma_start(h3[:, u, :, :], h3_dram[bass.ds(row, RB), :].rearrange("(p r) f -> p r f", r=RP)).then_inc(h3_in[u], 16)

            def store(t, u):
                row = sp.value_load(tab[0:1, 1, bass.ds(t, 1)], min_val=0, max_val=DUMMY_OUT)
                sp.wait_ge(res_done, t + 1 + RING)
                sp.wait_ge(stored, t * 16 + 32)
                sp.dma_start(out[bass.ds(row, RB), :].rearrange("(p r) f -> p r f", r=RP), res[:, u, :, :]).then_inc(stored, 16)

            for u in range(RING):
                load_x(u, u)
                load_h(u, u)
            sp.dma_start(w2[:, :], d["w2_1"]).then_inc(w2_in, 16)
            sp.dma_start(b2[:, :], bass.AP(d["b2_1"].tensor, 0, [[0, 128], [1, E * F]])).then_inc(w2_in, 16)

            def turn(t, u, more):
                if more:
                    load_x(t + RING, u)
                    load_h(t + RING, u)
                store(t, u)

            with sp.Fori(0, TURNS) as i:
                for u in range(RING):
                    turn(i * RING + u, u, True)
            for t in range(TURNS * RING, NK):
                turn(t, t % RING, t + RING < NK)
            sp.wait_ge(stored, NK * 16 + 32)

        @block.gpsimd
        def _(pool):
            pool.wait_ge(w_in, 32)

            def weights(t, u):
                e = pool.value_load(tab[0:1, 2, bass.ds(t, 1)], min_val=0, max_val=E - 1)
                pool.wait_ge(up_done, t * 2 + 2)
                pool.wait_ge(relu_done, t * 2 + 2)
                apart(pool)
                pool.tensor_copy(b1e[:, u, :], b1[:, bass.ds(e * CH, CH)])
                pool.tensor_copy(w1e[:, u, :], w1[:, bass.ds(e * F1, F1)]).then_inc(w1e_copied, 1)

            with pool.Fori(0, NK // 2) as i:
                for u in range(2):
                    weights(i * 2 + u, u)

        @block.tensor
        def _(pe):
            def transpose_x(t, r4, turn):
                u = r4 % 2
                pe.wait_ge(xs_in[r4], turn * 16 + 16)
                pe.wait_ge(x_copied, t + 1)
                for r in range(RP):
                    m = pe.transpose(p_x[u][:, r * 128:(r + 1) * 128], xs[:, r4, r, :], ident[:, :])
                m.then_inc(x_done, 1)

            def first(t, u):
                pe.wait_ge(w1e_copied, t + 1)
                pe.wait_ge(x_copied, t + 1 + 2)
                for c in range(CH):
                    if c % 2 == 0:
                        pe.wait_ge(relu_done, t * 2 + c // 2 + 1)
                    m = pe.matmul(p_u[u][c // 2][:, c % 2 * RB:(c % 2 + 1) * RB], w1e[:, u, c * F:(c + 1) * F], xt[:, u, :],
                                  start=True, stop=True)
                    if c % 2:
                        m.then_inc(up_done, 1)

            def second(t, u):
                e = pe.value_load(tab[0:1, 2, bass.ds(t, 1)], min_val=0, max_val=E - 1)
                pe.wait_ge(relu_done, t * 2 + 2 + 4)
                pe.wait_ge(res_done, t + RING - 1)
                for r in range(RP):
                    for c in range(CH):
                        m = pe.matmul(p_y[u][:, r * F:(r + 1) * F], hid[:, u, c, r * 128:(r + 1) * 128],
                                      w2[:, bass.ds(e * (CH * F) + c * F, F)], start=(c == 0), stop=(c == CH - 1))
                m.then_inc(y_done, 1)

            def turn(t, u, i):
                first(t, u % 2)
                transpose_x(t + 1, (u + 1) % RING, i + (u + 1) // RING)
                second(t - 1, (u + 1) % 2)

            transpose_x(0, 0, 0)
            first(0, 0)
            transpose_x(1, 1, 0)
            pe.wait_ge(w2_in, 32)
            for t in range(1, RING):
                turn(t, t, 0)
            with pe.Fori(1, TURNS) as i:
                for u in range(RING):
                    turn(i * RING + u, u, i)
            for t in range(TURNS * RING, NK - 1):
                turn(t, t % RING, t // RING)
            first(NK - 1, 1)
            second(NK - 2, 0)
            second(NK - 1, 1)

        @block.scalar
        def _(act):
            act.sem_inc(x_copied, 2)
            act.sem_inc(stored, 32)
            act.sem_inc(relu_done, 4)
            act.sem_inc(x_done, RING)
            with act.Fori(0, NK // 2) as i:
                for u in range(2):
                    t = i * 2 + u
                    act.wait_ge(y_done, t + 1)
                    for c in range(CH):
                        if c % 2 == 0:
                            act.wait_ge(up_done, t * 2 + c // 2 + 1 + 4)
                        m = act.activation(hid[:, u, c, :], p_u[u][c // 2][:, c % 2 * RB:(c % 2 + 1) * RB], ACT.Relu,
                                           bias=b1e[:, u, c:c + 1])
                        if c % 2:
                            m.then_inc(relu_done, 1)

        @block.vector
        def _(dve):
            dve.sem_inc(up_done, 4)
            dve.sem_inc(y_done, 2)
            dve.sem_inc(res_done, RING)

            def copy_x(t, u):
                dve.wait_ge(up_done, t * 2 + 2)
                dve.wait_ge(x_done, t + 1 + RING)
                dve.tensor_copy(xt[:, u, :], p_x[u][:, 0:RB]).then_inc(x_copied, 1)

            def result(t, r4, turn):
                u = r4 % 2
                e = dve.value_load(tab[0:1, 2, bass.ds(t, 1)], min_val=0, max_val=E - 1)
                dve.wait_ge(y_done, t + 1 + 2)
                apart(dve)
                ch = Chain(dve, y_step, t, 1)
                ch.link(dve.tensor_tensor(y[:, u, :, :], p_y[u][:, 0:RB].rearrange("p (r f) -> p r f", r=RP),
                                          b2[:, bass.ds(e * F, F)].unsqueeze(1).to_broadcast([128, RP, F]), ALU.add))
                dve.wait_ge(h3_in[r4], turn * 16 + 16)
                if not (isinstance(t, int) and t < RING - 2):
                    dve.wait_ge(stored, (t - RING + 1) * 16 + 32)
                dve.tensor_tensor(res[:, r4, :, :], y[:, u, :, :], h3[:, r4, :, :], ALU.add).then_inc(res_done, 1)

            copy_x(0, 0)
            copy_x(1, 1)
            dve.wait_ge(w2_in, 32)

            def turn(t, u, i):
                if not (isinstance(t, int) and t + 2 >= NK):
                    copy_x(t + 2, u % 2)
                result(t, u, i)

            for u in range(RING):
                turn(u, u, 0)
            with dve.Fori(1, TURNS) as i:
                for u in range(RING):
                    turn(i * RING + u, u, i)
            for t in range(TURNS * RING, NK):
                turn(t, t % RING, t // RING)


def audio_tower(nc, d, out):
    top = ExitStack()
    with top:
        k = Tools(nc, top)
        h0_dram = nc.dram_tensor("h0_dram", [HALF, NT * F], FP32)
        att_dram = nc.dram_tensor("att_dram", [NG, HALF, 2, B * CG], FP32)
        filt_dram = nc.dram_tensor("filt_dram", [2, STAGES, F, PAD], FP32)

        ident = k.sb(top, "ident", [128, 128])
        small = k.sb(top, "small", [128, 8])
        bn = k.sb(top, "bn", [128, 2])
        front = ExitStack()
        with front:
            fm = k.sb(front, "fm", [F, TOK])
            fm_rev = k.sb(front, "fm_rev", [F, TOK])
            tdnn(nc, k, d, ident, small, bn, fm, filt_dram)
            first_norm(nc, k, d, ident, bn, fm, fm_rev, h0_dram)
            convolutions(nc, k, d, fm, fm_rev, filt_dram, att_dram)
        h = k.sb(top, "h", [HALF, NT * F])
        middle = ExitStack()
        with middle:
            xf = k.sb(middle, "xf", [F, TOK])
            s_tok = k.sb(middle, "s_tok", [HALF, 2, B, E])
            g_tok = k.sb(middle, "g_tok", [HALF, 2, B, E])
            attach_norm(nc, k, d, ident, h0_dram, att_dram, h, xf, s_tok)
            choose(nc, k, d, ident, h, s_tok, g_tok)
            mixture0(nc, k, d, h, xf, g_tok)
        xs_dram = nc.dram_tensor("xs_dram", [DUMMY_IN + RB, F], FP32)
        h3_dram = nc.dram_tensor("h3_dram", [TOK + RB, F], FP32)
        base = k.sb(top, "base", [HALF, E])
        tab = k.sb(top, "tab", [1, 3, NK], I32)
        retain_and_route(nc, k, d, ident, small, h, base, xs_dram, h3_dram)
        plan_tiles(nc, k, d, base, tab, xs_dram, h3_dram)
        mixture1(nc, k, d, ident, tab, xs_dram, h3_dram, out)


def constants():
    import numpy as np

    half = F // 2
    freqs = np.float32(10000.0) ** (-np.arange(half, dtype=np.float32) / np.float32(half))
    phi = np.arange(L, dtype=np.float32)[:, None] * freqs.astype(np.float32)[None, :]
    pe = np.concatenate([np.sin(phi), np.cos(phi)], axis=-1).astype(np.float32)
    gamma = 1.0 - 2.0 ** (-5.0 - np.arange(HEADS, dtype=np.float64))
    rel = np.arange(HALF)[:, None, None] - np.arange(HALF)
    decay = (np.where(rel >= 0, gamma[:, None] ** np.maximum(rel, 0), 0.0) / np.sqrt(HD)).astype(np.float32)
    head = np.arange(F) // HD
    decay_i = (gamma[head][:, None] ** (HALF - np.arange(HALF))).astype(np.float32)
    decay_j = (gamma[head][None, :] ** np.arange(HALF)[:, None] / np.sqrt(HD)).astype(np.float32)
    same = (head[:, None] == head[None, :]).astype(np.float32)
    even = (np.arange(F) // HD % 2 == 0).astype(np.float32)
    more = {"decay": decay, "decay_i": decay_i, "decay_j": decay_j, "same": same, "even": even, "before": np.triu(np.ones((HALF, HALF), np.float32), 1),
            "prio": (E - np.arange(E, dtype=np.float32))[None, :], "region": (REG * np.arange(E, dtype=np.float32))[None, :],
            "number": np.arange(E, dtype=np.float32)[None, :],
            "kk": np.repeat(np.arange(NK, dtype=np.float32), E).reshape(1, NK, E)}
    return {**more, "ident": np.eye(128, dtype=np.float32), "flip": np.eye(HALF, dtype=np.float32)[::-1].copy(), "pe_t": np.ascontiguousarray(pe.T)}


def kernel(**inputs):
    import numpy as np
    import concourse.bacc as bacc
    from concourse.bass_utils import run_bass_kernel_spmd

    a = {n: np.asarray(v) for n, v in inputs.items()}
    rows = constants()
    rows["x"] = a["x"].reshape(-1)
    rows["tok_w"] = np.concatenate([a["L0_tok_W"].T, a["L0_tok_b"][None, :]], axis=0)
    even = rows.pop("even")
    rows["small"] = np.stack([a["L0_tok_gamma"], a["L0_tok_beta"], even, (even == 0).astype(np.float32), a["L1_attn_bq"],
                              a["L1_attn_bk"], np.zeros(F, np.float32), np.zeros(F, np.float32)], axis=1)
    rows["bk"] = a["L1_attn_bk"][None, :]
    rows["wq"] = a["L1_attn_wq"].T
    rows["wk"] = a["L1_attn_wk"].T
    rows["wvg"] = np.concatenate([a["L1_attn_wv"].T, a["L1_attn_wg"].T], axis=1)
    rows["bvg"] = np.concatenate([a["L1_attn_bv"], a["L1_attn_bg"]])[None, :]
    rows["wg1"] = a["L1_ffn_Wg"]
    rows["bg1"] = a["L1_ffn_bg"][None, :]
    rows["w1_1"] = a["L1_ffn_W1"].transpose(1, 0, 2).reshape(F, E * F1)
    rows["b1_1"] = a["L1_ffn_b1"].reshape(E * F1 // F, F).T
    rows["w2_1"] = a["L1_ffn_W2"].reshape(E * F1 // F, F, F).transpose(1, 0, 2).reshape(F, E * F1)
    rows["b2_1"] = a["L1_ffn_b2"].reshape(1, E * F)
    rows["w_filt"] = a["L0_attn_W_filt"].reshape(F, F * STAGES)
    rows["w_proj"] = a["L0_attn_W_proj"].reshape(F, NG, CG, 2, 2).transpose(0, 1, 4, 3, 2).reshape(F, NG, 2, 2 * CG)
    rows["wg0"] = a["L0_ffn_Wg"]
    rows["b2_0"] = a["L0_ffn_b2"]
    rows["w1_0"] = a["L0_ffn_W1"].transpose(1, 0, 2)
    rows["b1_0"] = a["L0_ffn_b1"].reshape(E, F0 // F, F).transpose(2, 0, 1)
    rows["w2_0"] = a["L0_ffn_W2"].reshape(E, F0 // F, F, F).transpose(2, 0, 1, 3)
    rows = {n: np.ascontiguousarray(v) for n, v in rows.items()}

    nc = bacc.Bacc("TRN2", target_bir_lowering=False, num_devices=1)
    d = {n: nc.dram_tensor(f"in_{n}", v.shape, mybir.dt.from_np(v.dtype), kind="ExternalInput").ap()
         for n, v in rows.items()}
    out = nc.dram_tensor("out", (TOK + RB, F), FP32, kind="ExternalOutput").ap()
    audio_tower(nc, d, out)
    r = run_bass_kernel_spmd(nc, [{f"in_{n}": v for n, v in rows.items()}], core_ids=[0])
    return r.results[0]["out"][:TOK].reshape(B, L, F)
```

```python
from contextlib import ExitStack

import concourse.bass as bass
from concourse import mybir

FP32 = mybir.dt.float32
BF16 = mybir.dt.bfloat16
I32 = mybir.dt.int32
ALU = mybir.AluOpType
ACT = mybir.ActivationFunctionType
AX = mybir.AxisListType

B, T_IN, D_IN = 64, 256, 23
CTX = 5
L = T_IN - CTX + 1
HALF = L // 2
NT = 2 * B
TOK = B * L
F = 128
QT = 4
QN = QT * HALF
QF = QT * F
NQ = NT // QT
PATCH = CTX * D_IN
EPS = 1e-5
STAGES = 3
PAD = 3 * HALF
E = 8
TOPK = L * 2 // E
F0 = 256
F1 = 512
HEADS = 8
HD = F // HEADS
CG = 32
NG = F // CG
QC = 4
NS = CG // QC
RB = 256
REG = TOK + RB
DUMMY_IN = E * REG
DUMMY_OUT = TOK
NK = (TOK + E * (RB - 1)) // RB
NK += NK % 2
TR = 6


def apart(eng):
    eng.nop(nofuse=True)


class Chain:

    def __init__(self, eng, sem, at=0, per=0, base=0):
        self.eng, self.sem, self.n, self.start = eng, sem, 0, at * per + base

    def sig(self, ins):
        ins.then_inc(self.sem, 1)
        self.n += 1

    def wait(self):
        self.eng.wait_ge(self.sem, self.start + self.n)

    def link(self, ins):
        self.sig(ins)
        self.wait()


def staggered(eng, ring, steps):
    def peeled(n):
        for lag, step in steps:
            if 0 <= n - lag < NQ:
                step(n - lag, (n - lag) % ring, (n - lag) // ring)

    for n in range(ring):
        peeled(n)
    with eng.Fori(1, NQ // ring) as i:
        for v in range(ring):
            for lag, step in steps:
                step(i * ring + (v - lag), (v - lag) % ring, i + (v - lag) // ring)
    for n in range(NQ, NQ + max(lag for lag, _ in steps)):
        peeled(n)


class Tools:
    def __init__(self, nc, top):
        self.nc, self.top = nc, top

    def sem(self, name):
        return self.top.enter_context(self.nc.semaphore(name))

    def sb(self, ctx, name, shape, dt=FP32):
        return ctx.enter_context(self.nc.sbuf_tensor(name, list(shape), dt))

    def ps(self, ctx, name, dt=FP32):
        return ctx.enter_context(self.nc.psum_tensor(name, [128, 2048 // (4 if dt == FP32 else 2)], dt))


def tdnn(nc, k, d, ident, small, bn, fm, filt_dram):
    ctx = ExitStack()
    with ctx:
        U = 4
        tok_w = k.sb(ctx, "tok_w", [PATCH + 1, F])
        patch = k.sb(ctx, "patch", [HALF, U, QT, PATCH + 1])
        patch_t = k.sb(ctx, "patch_t", [PATCH + 1, U, QN])
        stats = k.sb(ctx, "stats", [F, NQ * 6])
        mv = k.sb(ctx, "mv", [F, 2])
        rs = k.sb(ctx, "rs", [F, 4])
        nhalf = k.sb(ctx, "nhalf", [F, 1])
        pe_t = k.sb(ctx, "pe_t", [F, L])
        w_filt = k.sb(ctx, "w_filt", [F, F * STAGES])
        filt = k.sb(ctx, "filt", [F, 2, STAGES, PAD])
        p_win = [k.ps(ctx, f"p_win{r}") for r in range(2)]
        p_y = [k.ps(ctx, f"p_y{r}") for r in range(2)]
        p_filt = [k.ps(ctx, f"p_filt{s}") for s in range(STAGES)]

        consts = k.sem("consts")
        win_in = [k.sem(f"win_in{u}") for u in range(U)]
        ones_set = k.sem("ones_set")
        win_t = k.sem("win_t")
        win_copied = k.sem("win_copied")
        y_done = k.sem("y_done")
        relu_done = k.sem("relu_done")
        bn_step = k.sem("bn_step")
        rstd_done = k.sem("rstd_done")
        nhalf_set = k.sem("nhalf_set")
        filt_pe = k.sem("filt_pe")
        filt_zero = k.sem("filt_zero")
        filt_copied = k.sem("filt_copied")
        filt_out = k.sem("filt_out")
        block = ctx.enter_context(nc.Block())

        @block.sync
        def _(sp):
            sp.dma_start(tok_w[:, :], d["tok_w"]).then_inc(consts, 16)
            sp.dma_start(ident[:, :], d["ident"]).then_inc(consts, 16)
            sp.dma_start(small[:, :], d["small"]).then_inc(consts, 16)
            sp.dma_start(pe_t[:, :], d["pe_t"]).then_inc(consts, 16)
            sp.dma_start(w_filt[:, :], d["w_filt"]).then_inc(consts, 16)
            sp.wait_ge(ones_set, U)
            with sp.Fori(0, NQ // U) as i:
                for u in range(U):
                    sp.wait_ge(win_copied, i * U + u + 1)
                    for b in range(2):
                        at = d["x"][bass.ds((i * U + u) * (2 * T_IN * D_IN) + b * T_IN * D_IN, 1)]
                        src = bass.AP(at.tensor, at.offset, [[D_IN, HALF], [HALF * D_IN, 2], [1, PATCH]])
                        sp.dma_start(patch[:, u, 2 * b:2 * b + 2, 0:PATCH], src).then_inc(win_in[u], 16)
            sp.wait_ge(filt_zero, 1)
            sp.wait_ge(filt_copied, 2 * STAGES)
            sp.dma_start(filt_dram.ap().rearrange("r s c t -> c r s t"), filt[:, :, :, :]).then_inc(filt_out, 16)
            sp.wait_ge(filt_out, 16)

        @block.tensor
        def _(pe):
            pe.wait_ge(consts, 80)
            for s in range(STAGES):
                wf = w_filt[:, :].rearrange("p (c s) -> p s c", s=STAGES)[:, s, :]
                pe.matmul(p_filt[s][:, 0:L], wf, pe_t[:, :], start=True, stop=True).then_inc(filt_pe, 1)

            def windows(n, u, i):
                pe.wait_ge(win_in[u], i * 32 + 32)
                pe.wait_ge(win_copied, n + U - 1)
                for j in range(QT):
                    m = pe.transpose(p_win[u % 2][0:PATCH + 1, j * HALF:(j + 1) * HALF], patch[:, u, j, :],
                                     ident[0:HALF, 0:HALF])
                m.then_inc(win_t, 1)

            def linear(n, u, i):
                pe.wait_ge(win_copied, n + 1 + U)
                pe.wait_ge(relu_done, n + U - 1)
                pe.matmul(p_y[u % 2][:, 0:QN], tok_w[:, :], patch_t[:, u, :], start=True, stop=True).then_inc(y_done, 1)

            staggered(pe, U, ((0, windows), (1, linear)))

        @block.scalar
        def _(act):
            act.sem_inc(win_copied, U)
            act.sem_inc(relu_done, U)
            for s in range(STAGES):
                act.wait_ge(filt_pe, s + 1)
                act.activation(filt[:, 0, s, HALF:HALF + L], p_filt[s][:, 0:L], ACT.Copy).then_inc(filt_copied, 1)
                act.activation(filt[:, 1, s, 0:L], p_filt[s][:, L - 1::-1], ACT.Copy).then_inc(filt_copied, 1)

            def copy_windows(n, u, i):
                act.wait_ge(win_t, n + 1)
                act.activation(patch_t[:, u, :], p_win[u % 2][0:PATCH + 1, 0:QN], ACT.Copy).then_inc(win_copied, 1)

            def relu(n, u, i):
                act.wait_ge(y_done, n + 1)
                apart(act)
                act.activation(fm[:, bass.ds(n * QN, QN)], p_y[u % 2][:, 0:QN], ACT.Relu).then_inc(relu_done, 1)

            staggered(act, U, ((0, copy_windows), (1, relu)))

        @block.gpsimd
        def _(pool):
            pool.memset(nhalf[:, :], -0.5).then_inc(nhalf_set, 1)
            pool.memset(filt[:, 0, :, 0:HALF], 0.0).then_inc(nhalf_set, 1)
            pool.memset(filt[:, 1, :, L:PAD], 0.0).then_inc(filt_zero, 1)
            pool.wait_ge(nhalf_set, 2)
            pool.wait_ge(bn_step, 2)
            pool.tensor_tensor(out=rs[:, 1:2], in0=rs[:, 0:1], in1=nhalf[:, :], op=ALU.pow).then_inc(rstd_done, 1)

        @block.vector
        def _(dve):
            for u in range(U):
                dve.memset(patch[:, u, :, PATCH:PATCH + 1], 1.0).then_inc(ones_set, 1)
            with dve.Fori(0, NQ) as i:
                dve.wait_ge(relu_done, i + 1 + U)
                dve.bn_stats(stats[:, bass.ds(i * 6, 6)], fm[:, bass.ds(i * QN, QN)]).then_inc(ones_set, 1)
            dve.wait_ge(ones_set, U + NQ)
            ch = Chain(dve, bn_step)
            ch.link(dve.bn_aggr(mv[:, :], stats[:, :]))
            ch.sig(dve.tensor_scalar(rs[:, 0:1], mv[:, 1:2], EPS, None, ALU.add))
            dve.wait_ge(consts, 80)
            dve.wait_ge(rstd_done, 1)
            ch.link(dve.tensor_tensor(bn[:, 0:1], small[:, 0:1], rs[:, 1:2], ALU.mult))
            ch.link(dve.tensor_tensor(rs[:, 2:3], mv[:, 0:1], bn[:, 0:1], ALU.mult))
            ch.link(dve.tensor_tensor(bn[:, 1:2], small[:, 1:2], rs[:, 2:3], ALU.subtract))


def first_norm(nc, k, d, ident, bn, fm, fm_rev, h0_dram):
    ctx = ExitStack()
    with ctx:
        U = 4
        hn = k.sb(ctx, "hn", [F, U, QN])
        ht = k.sb(ctx, "ht", [HALF, U, QF])
        xn = k.sb(ctx, "xn", [HALF, U, QF])
        lst = k.sb(ctx, "lst", [HALF, U, QT, 6])
        lmv = k.sb(ctx, "lmv", [HALF, U, QT, 2])
        lve = k.sb(ctx, "lve", [HALF, U, QT])
        lrs = k.sb(ctx, "lrs", [HALF, U, QT])
        nhalf = k.sb(ctx, "nhalf_b", [HALF, QT])
        p_h = [k.ps(ctx, f"p_h{u}") for u in range(U)]
        p_x = [k.ps(ctx, f"p_x{u}") for u in range(U)]

        hn_ready = k.sem("hn_ready")
        h_done = k.sem("h_done")
        ht_copied = k.sem("ht_copied")
        h0_out = [k.sem(f"h0_out{u}") for u in range(U)]
        var_done = k.sem("var_done")
        rstd_done = k.sem("rstd_done_b")
        pool_step = k.sem("pool_step_b")
        dve_step = k.sem("dve_step_b")
        xn_ready = k.sem("xn_ready")
        xt_done = k.sem("xt_done")
        fm_copied = k.sem("fm_copied")
        block = ctx.enter_context(nc.Block())

        @block.sync
        def _(sp):
            with sp.Fori(0, NQ // U) as i:
                for u in range(U):
                    sp.wait_ge(ht_copied, i * U + u + 1 + U)
                    sp.dma_start(h0_dram[:, bass.ds((i * U + u) * QF, QF)], ht[:, u, :]).then_inc(h0_out[u], 16)
            for u in range(U):
                sp.wait_ge(h0_out[u], 16 * (NQ // U + 1))

        @block.tensor
        def _(pe):
            def to_tokens(n, u, i):
                pe.wait_ge(hn_ready, n + 1)
                pe.wait_ge(ht_copied, n + 1)
                for j in range(QT):
                    m = pe.transpose(p_h[u][0:HALF, j * F:(j + 1) * F], hn[:, u, j * HALF:(j + 1) * HALF], ident[:, :])
                m.then_inc(h_done, 1)

            def to_features(n, u, i):
                pe.wait_ge(xn_ready, n + 1)
                pe.wait_ge(fm_copied, n + 1)
                for j in range(QT):
                    m = pe.transpose(p_x[u][:, j * HALF:(j + 1) * HALF], xn[:, u, j * F:(j + 1) * F],
                                     ident[0:HALF, 0:HALF])
                m.then_inc(xt_done, 1)

            staggered(pe, U, ((0, to_tokens), (3, to_features)))

        @block.scalar
        def _(act):
            act.sem_inc(ht_copied, U)
            for u in range(U):
                act.sem_inc(h0_out[u], 16)

            def batch_norm(n, u, i):
                act.activation(hn[:, u, :], fm[:, bass.ds(n * QN, QN)], ACT.Identity,
                               bias=bn[:, 1:2], scale=bn[:, 0:1]).then_inc(hn_ready, 1)

            def copy_tokens(n, u, i):
                act.wait_ge(h_done, n + 1)
                act.wait_ge(h0_out[u], i * 16 + 16)
                act.activation(ht[:, u, :], p_h[u][0:HALF, :], ACT.Copy).then_inc(ht_copied, 1)

            def copy_features(n, u, i):
                act.wait_ge(xt_done, n + 1)
                apart(act)
                act.activation(fm[:, bass.ds(n * QN, QN)], p_x[u][:, 0:QN], ACT.Copy)
                rev = fm_rev[:, bass.ds(n * QN, QN)].rearrange("p (j t) -> p j t", j=QT)
                src = p_x[u][:, 0:QN].rearrange("p (j t) -> p j t", j=QT)[:, :, ::-1]
                act.activation(rev, src, ACT.Copy).then_inc(fm_copied, 1)

            staggered(act, U, ((1, copy_tokens), (0, batch_norm), (4, copy_features)))

        @block.gpsimd
        def _(pool):
            ch = Chain(pool, pool_step)
            ch.link(pool.memset(nhalf[:, :], -0.5))
            with pool.Fori(0, NQ // U) as i:
                for u in range(U):
                    pool.wait_ge(var_done, i * U + u + 1)
                    apart(pool)
                    pc = Chain(pool, pool_step, i, U, 1 + u)
                    pc.link(pool.tensor_scalar(lve[:, u, :], lmv[:, u, :, 1], EPS, None, ALU.add))
                    pool.tensor_tensor(out=lrs[:, u, :], in0=lve[:, u, :], in1=nhalf[:, :], op=ALU.pow).then_inc(rstd_done, 1)

        @block.vector
        def _(dve):
            dve.sem_inc(fm_copied, U)

            def token_stats(n, u, i):
                dve.wait_ge(ht_copied, n + 1 + U)
                for j in range(QT):
                    m = dve.bn_stats(lst[:, u, j, :], ht[:, u, j * F:(j + 1) * F])
                Chain(dve, dve_step, n, 1).link(m)
                apart(dve)
                for j in range(QT):
                    m = dve.bn_aggr(lmv[:, u, j, :], lst[:, u, j, :])
                m.then_inc(var_done, 1)

            def normed(n, u, i):
                dve.wait_ge(fm_copied, n + 1)
                dve.wait_ge(rstd_done, n + 1)
                for j in range(QT):
                    m = dve.tensor_scalar(xn[:, u, j * F:(j + 1) * F], ht[:, u, j * F:(j + 1) * F],
                                          lmv[:, u, j, 0:1], lrs[:, u, j:j + 1], ALU.subtract, ALU.mult)
                m.then_inc(xn_ready, 1)

            staggered(dve, U, ((1, token_stats), (2, normed)))


def convolutions(nc, k, d, fm, fm_rev, filt_dram, att_dram):
    ctx = ExitStack()
    with ctx:
        w_proj = k.sb(ctx, "w_proj", [F, NG, 2, 2 * CG])
        x_buf = k.sb(ctx, "x_buf", [HALF, B + 8 * CG * B])
        x = x_buf[:, B:].rearrange("t (o h p n) -> t o h p n", o=2, h=2, p=2)
        x_blocks = x_buf[:, :].rearrange("t (k b) -> t k b", b=B)
        toep = k.sb(ctx, "toep", [HALF, TR, 2, L])
        p_p = [k.ps(ctx, f"p_p{r}") for r in range(4)]
        p_c = [k.ps(ctx, f"p_c{r}") for r in range(4)]
        NB = 4
        BANKS = (B // NB) * 2 * 2
        STEPS = STAGES * NS
        TILES = 2 * STEPS

        w_in = k.sem("w_in")
        zeros_set = k.sem("zeros_set")
        toep_in = [k.sem(f"toep_in{r}") for r in range(TR)]
        proj_done = k.sem("proj_done")
        proj_copied = k.sem("proj_copied")
        conv_done = k.sem("conv_done")
        prod_done = k.sem("prod_done")
        att_out = k.sem("att_out")
        att_stored = k.sem("att_stored")
        block = ctx.enter_context(nc.Block())

        def banks():
            for o in (1, 0):
                for bg in range(B // NB):
                    for half in range(2):
                        yield o, bg, half

        def place(s):
            return s % 2, s // 2

        @block.sync
        def _(sp):
            sp.dma_start(w_proj[:, :, :, :], d["w_proj"]).then_inc(w_in, 16)
            with sp.Fori(0, NG) as g:
                for m in range(TILES):
                    s, c = m // (2 * NS), (m % (2 * NS)) * 2
                    kind, first = ((1, 0), (0, 1), (1, 0))[s]
                    at = filt_dram.ap().rearrange("r s c t -> (r s c t)")[
                        bass.ds(g * (CG * PAD) + ((kind * STAGES + s) * F + c) * PAD + first, 1)]
                    src = bass.AP(at.tensor, at.offset, [[1, HALF], [PAD, 2], [1, L]])
                    sp.wait_ge(conv_done, g * TILES + m + 1)
                    sp.dma_start(toep[:, m % TR, :, :], src).then_inc(toep_in[m % TR], 16)

        @block.tensor
        def _(pe):
            pe.wait_ge(w_in, 16)
            pe.wait_ge(zeros_set, 1)
            with pe.Fori(0, NG) as g:
                for n, (o, bg, half) in enumerate(banks()):
                    pe.wait_ge(proj_copied, g * BANKS + n + 1)
                    src = fm_rev if o else fm
                    for b in range(NB):
                        tile = 2 * (bg * NB + b) + half
                        m = pe.matmul(p_p[n % 4][0:HALF, b * 4 * CG:(b + 1) * 4 * CG], src[:, tile * HALF:(tile + 1) * HALF],
                                      w_proj[:, bass.ds(g, 1), :, :], start=True, stop=True)
                    m.then_inc(proj_done, 1)
                pe.wait_ge(proj_copied, g * BANKS + BANKS + 4)
                for n in range(STEPS):
                    s, q = n // NS, n % NS
                    o, p = place(s)
                    pe.wait_ge(prod_done, g * STEPS + n + 1)
                    for t in range(2):
                        r = 2 * n + t
                        pe.wait_ge(toep_in[r % TR], g * (16 * TILES // TR) + 16 * (r // TR) + 16)
                        for c in range(2):
                            ch = q * QC + 2 * t + c
                            tt = toep[:, r % TR, c, :]
                            near, far = (tt[:, HALF:L], tt[:, 0:HALF]) if s % 2 == 0 else (tt[:, 0:HALF], tt[:, HALF:L])
                            to = p_c[n % 4][0:HALF, (2 * t + c) * 2 * B:(2 * t + c + 1) * 2 * B]
                            y0 = 1 + (o * 4 + p) * CG + ch
                            pe.matmul(to, near, x[:, o, :, p, ch * B:(ch + 1) * B], start=True, stop=False)
                            m = pe.matmul(to, far, x_blocks[:, 0:y0 + 1:y0, :], start=False, stop=True)
                        m.then_inc(conv_done, 1)

        @block.scalar
        def _(act):
            act.sem_inc(proj_copied, 4)
            with act.Fori(0, NG) as g:
                for n, (o, bg, half) in enumerate(banks()):
                    if n == 0:
                        act.wait_ge(prod_done, g * STEPS + 4)
                    if n == BANKS // 2:
                        act.wait_ge(att_stored, g + 1)
                    act.wait_ge(proj_done, g * BANKS + n + 1)
                    dst = x[:, o, half, :, :].rearrange("t p (c b) -> t (p c) b", b=B)[:, :, bg * NB:(bg + 1) * NB]
                    src = p_p[n % 4][0:HALF, :].rearrange("t (b o k) -> t k b o", b=NB, o=2)[:, :, :, o]
                    act.activation(dst, src, ACT.Copy).then_inc(proj_copied, 1)

        @block.gpsimd
        def _(pool):
            pool.sem_inc(att_stored, 1)
            with pool.Fori(0, NG) as g:
                pool.wait_ge(prod_done, g * STEPS + STEPS + 4)
                pool.dma_start(att_dram[bass.ds(g, 1), :, :, :].rearrange("o t h n -> (o t) h n"),
                               x[:, 0, :, 0, :]).then_inc(att_out, 16)
                pool.wait_ge(att_out, g * 16 + 16)
                pool.sem_inc(att_stored, 1)

        @block.vector
        def _(dve):
            dve.memset(x_buf[:, 0:B], 0.0).then_inc(zeros_set, 1)
            dve.sem_inc(conv_done, TR)
            dve.sem_inc(prod_done, 4)
            with dve.Fori(0, NG) as g:
                for n in range(STEPS):
                    s, q = n // NS, n % NS
                    o, p = place(s + 1)
                    dve.wait_ge(conv_done, g * TILES + 2 * n + 2 + TR)
                    nxt = x[:, o, :, p, q * QC * B:(q + 1) * QC * B]
                    y = p_c[n % 4][0:HALF, :].rearrange("t (c h b) -> t h c b", c=QC, h=2)
                    if s < STAGES - 1:
                        nxt = nxt.rearrange("t h (c b) -> t h c b", c=QC)
                        dve.tensor_tensor(nxt, y, nxt, ALU.mult).then_inc(prod_done, 1)
                    else:
                        for half in range(2):
                            dst = x[:, 0, half, 0, :].rearrange("t (b c) -> t c b", b=B)[:, q * QC:(q + 1) * QC, :]
                            m = dve.tensor_tensor(dst, y[:, half, :, :],
                                                  nxt[:, half, :].rearrange("t (c b) -> t c b", c=QC), ALU.mult)
                        m.then_inc(prod_done, 1)


def attach_norm(nc, k, d, ident, h0_dram, att_dram, h, xf, s_tok):
    ctx = ExitStack()
    with ctx:
        U = 4
        WL = 96
        flip = k.sb(ctx, "flip", [HALF, HALF])
        wg0 = k.sb(ctx, "wg0", [F, WL])
        h0 = k.sb(ctx, "h0", [HALF, U // 2, 2 * QF])
        att = k.sb(ctx, "att", [HALF, U // 2, NG, 2, 4 * CG])
        xn = k.sb(ctx, "xn_d", [HALF, U, QF])
        xt = k.sb(ctx, "xt_d", [F, U, QN])
        lst = k.sb(ctx, "lst_d", [HALF, U, QT, 6])
        lmv = k.sb(ctx, "lmv_d", [HALF, U, QT, 2])
        lve = k.sb(ctx, "lve_d", [HALF, U, QT])
        lrs = k.sb(ctx, "lrs_d", [HALF, U, QT])
        lmr = k.sb(ctx, "lmr_d", [HALF, U, QT])
        lbi = k.sb(ctx, "lbi_d", [HALF, U, QT])
        nhalf = k.sb(ctx, "nhalf_d", [HALF, QT])
        p_f = [k.ps(ctx, f"p_f{u}") for u in range(U)]
        p_x = [k.ps(ctx, f"p_xd{r}") for r in range(2)]
        p_l = [k.ps(ctx, f"p_l{r}") for r in range(2)]

        consts = k.sem("consts_d")
        wg0_cleared = k.sem("wg0_cleared")
        pair_in = [k.sem(f"pair_in{v}") for v in range(U // 2)]
        flipped = k.sem("flipped")
        joined = k.sem("joined")
        var_done = k.sem("var_done_d")
        pool_step = k.sem("pool_step_d")
        dve_step = k.sem("dve_step_d")
        rstd_done = k.sem("rstd_done_d")
        xn_ready = k.sem("xn_ready_d")
        xt_done = k.sem("xt_done_d")
        xt_copied = k.sem("xt_copied_d")
        log_done = k.sem("log_done")
        log_copied = k.sem("log_copied")
        block = ctx.enter_context(nc.Block())

        @block.sync
        def _(sp):
            sp.dma_start(flip[:, :], d["flip"]).then_inc(consts, 16)
            sp.wait_ge(wg0_cleared, 1)
            sp.dma_start(wg0[:, 0:E], d["wg0"]).then_inc(consts, 16)
            with sp.Fori(0, NQ // U) as i:
                for v in range(U // 2):
                    n = i * U + 2 * v
                    sp.wait_ge(joined, n + 2)
                    sp.dma_start(h0[:, v, :], h0_dram[:, bass.ds(n * QF, 2 * QF)]).then_inc(pair_in[v], 16)
                    for g in range(NG):
                        sp.dma_start(att[:, v, g, :, :], att_dram[g, :, :, bass.ds(n * 2 * CG, 4 * CG)]).then_inc(pair_in[v], 16)

        @block.tensor
        def _(pe):
            pe.wait_ge(consts, 32)

            def turning(n, u, i):
                pe.wait_ge(pair_in[u // 2], i * 80 + 80)
                pe.wait_ge(joined, n + 1)
                for j in range(QT):
                    b, half = j // 2, j % 2
                    m = pe.matmul(p_f[u][0:HALF, j * F:(j + 1) * F], flip[:, :],
                                  att[:, u // 2, :, half, (u % 2 * 2 + b) * CG:(u % 2 * 2 + b + 1) * CG], start=True, stop=True)
                m.then_inc(flipped, 1)

            def back(n, u, i):
                pe.wait_ge(xn_ready, n + 1)
                pe.wait_ge(xt_copied, n + U - 1)
                for j in range(QT):
                    m = pe.transpose(p_x[u % 2][:, j * HALF:(j + 1) * HALF], xn[:, u, j * F:(j + 1) * F],
                                     ident[0:HALF, 0:HALF])
                m.then_inc(xt_done, 1)

            def logits(n, u, i):
                pe.wait_ge(xt_copied, n + 1 + U)
                pe.wait_ge(log_copied, n + 3)
                for j in range(QT):
                    m = pe.matmul(p_l[u % 2][0:HALF, j * WL:(j + 1) * WL], xt[:, u, j * HALF:(j + 1) * HALF],
                                  wg0[:, :], start=True, stop=True)
                m.then_inc(log_done, 1)

            staggered(pe, U, ((0, turning), (3, back), (4, logits)))

        @block.scalar
        def _(act):
            act.sem_inc(xt_copied, U)

            def normed(n, u, i):
                act.wait_ge(rstd_done, n + 1)
                apart(act)
                for j in range(QT):
                    m = act.activation(xn[:, u, j * F:(j + 1) * F], h[:, bass.ds(n * QF + j * F, F)], ACT.Identity,
                                       bias=lbi[:, u, j:j + 1], scale=lrs[:, u, j:j + 1])
                m.then_inc(xn_ready, 1)

            def copy_features(n, u, i):
                act.wait_ge(log_copied, n + 1)
                act.wait_ge(xt_done, n + 1)
                apart(act)
                act.activation(xf[:, bass.ds(n * QN, QN)], p_x[u % 2][:, 0:QN], ACT.Copy)
                act.activation(xt[:, u, :], p_x[u % 2][:, 0:QN], ACT.Copy).then_inc(xt_copied, 1)

            staggered(act, U, ((3, copy_features), (1, normed)))

        @block.gpsimd
        def _(pool):
            ch = Chain(pool, pool_step)
            ch.link(pool.memset(nhalf[:, :], -0.5))

            def rstd(n, u, i):
                pool.wait_ge(var_done, n + 1)
                apart(pool)
                pc = Chain(pool, pool_step, n, 3, 1)
                pc.link(pool.tensor_scalar(lve[:, u, :], lmv[:, u, :, 1], EPS, None, ALU.add))
                pc.link(pool.tensor_tensor(out=lrs[:, u, :], in0=lve[:, u, :], in1=nhalf[:, :], op=ALU.pow))
                pc.link(pool.tensor_tensor(out=lmr[:, u, :], in0=lmv[:, u, :, 0], in1=lrs[:, u, :], op=ALU.mult))
                apart(pool)
                pool.tensor_scalar(lbi[:, u, :], lmr[:, u, :], -1.0, None, ALU.mult).then_inc(rstd_done, 1)

            staggered(pool, U, ((0, rstd),))

        @block.vector
        def _(dve):
            dve.memset(wg0[:, :], 0.0).then_inc(wg0_cleared, 1)
            dve.sem_inc(joined, U)
            dve.sem_inc(log_copied, U)

            def join(n, u, i):
                dve.wait_ge(flipped, n + 1)
                apart(dve)
                dve.tensor_tensor(h[:, bass.ds(n * QF, QF)], p_f[u][0:HALF, :], h0[:, u // 2, u % 2 * QF:(u % 2 + 1) * QF], ALU.add).then_inc(joined, 1)
                dve.wait_ge(joined, n + 1 + U)
                apart(dve)
                for j in range(QT):
                    m = dve.bn_stats(lst[:, u, j, :], h[:, bass.ds(n * QF + j * F, F)])
                Chain(dve, dve_step, n, 1).link(m)
                apart(dve)
                for j in range(QT):
                    m = dve.bn_aggr(lmv[:, u, j, :], lst[:, u, j, :])
                m.then_inc(var_done, 1)

            def keep_logits(n, u, i):
                dve.wait_ge(log_done, n + 1)
                apart(dve)
                src = p_l[u % 2][0:HALF, 0:QT * WL].rearrange("t (b h e) -> t h b e", b=2, h=2)[:, :, :, 0:E]
                dve.tensor_copy(s_tok[:, :, bass.ds(n * 2, 2), :], src).then_inc(log_copied, 1)

            staggered(dve, U, ((0, join), (4, keep_logits)))


def choose(nc, k, d, ident, h, s_tok, g_tok, weights0):
    ctx = ExitStack()
    with ctx:
        BG = 16
        NBG = B // BG
        mx = k.sb(ctx, "mx", [HALF, NT])
        st = k.sb(ctx, "st", [128, NBG, L])
        work = k.sb(ctx, "work", [128, NBG, L])
        m8 = k.sb(ctx, "m8", [128, NBG, 8])
        above = k.sb(ctx, "above", [128, NBG, L])
        equal = k.sb(ctx, "equal", [128, NBG, L])
        rank = k.sb(ctx, "rank", [128, NBG, L])
        gate = k.sb(ctx, "gate", [128, NBG, L])
        ones = k.sb(ctx, "ones_e", [128, L])
        count = k.sb(ctx, "count", [128, NBG])
        room = k.sb(ctx, "room", [128, NBG])
        b2d = k.sb(ctx, "b2d", [128, BG * F])
        p_s = [k.ps(ctx, f"p_s{r}") for r in range(2)]
        p_g = [k.ps(ctx, f"p_g{r}") for r in range(2)]
        p_b = [k.ps(ctx, f"p_b{r}") for r in range(4)]

        dve_step = k.sem("dve_step_e")
        shifted = k.sem("shifted")
        exps = k.sem("exps")
        probs = k.sem("probs")
        s_t = k.sem("s_t")
        gates = k.sem("gates")
        g_t = k.sem("g_t")
        b2_zero = k.sem("b2_zero")
        b2_in = k.sem("b2_in")
        w_in = k.sem("w_in_f")
        b2_done = k.sem("b2_done")
        b2_added = k.sem("b2_added")
        block = ctx.enter_context(nc.Block())
        s_flat = s_tok[:, :, :, :].rearrange("t h b e -> t (h b) e")

        @block.sync
        def _(sp):
            sp.wait_ge(b2_zero, 1)
            for b in range(BG):
                sp.dma_start(b2d[b * E:(b + 1) * E, b * F:(b + 1) * F], d["b2_0"]).then_inc(b2_in, 16)
            for name, to in zip(("w1_0", "b1_0", "w2_0"), weights0):
                sp.dma_start(to, d[name]).then_inc(w_in, 16)
            sp.wait_ge(b2_in, 16 * BG)
            sp.wait_ge(w_in, 48)

        @block.gpsimd
        def _(pool):
            pool.memset(b2d[:, :], 0.0).then_inc(b2_zero, 1)

        @block.scalar
        def _(act):
            act.wait_ge(shifted, 1)
            act.activation(s_flat, s_flat, ACT.Exp).then_inc(exps, 1)

        @block.tensor
        def _(pe):
            pe.wait_ge(probs, 1)
            for g in range(NBG):
                for half in range(2):
                    col = (g % 2) * L + half * HALF
                    m = pe.transpose(p_s[g // 2][:, col:col + HALF],
                                     s_tok[:, half, g * BG:(g + 1) * BG, :].rearrange("t b e -> t (b e)"),
                                     ident[0:HALF, 0:HALF])
                if g % 2:
                    m.then_inc(s_t, 1)
            pe.wait_ge(gates, NBG)
            for half in range(2):
                for g in range(NBG):
                    m = pe.transpose(p_g[half][0:HALF, g * 128:(g + 1) * 128], gate[:, g, half * HALF:(half + 1) * HALF],
                                     ident[:, :])
                m.then_inc(g_t, 1)
            pe.wait_ge(b2_in, 16 * BG)
            for n in range(2 * NBG * 4):
                g, half, sub = n // 8, n // 4 % 2, n % 4
                if n >= 4:
                    pe.wait_ge(b2_added, n - 3)
                pe.matmul(p_b[n % 4][0:HALF, :], gate[:, g, half * HALF:(half + 1) * HALF],
                          b2d[:, sub * 4 * F:(sub + 1) * 4 * F], start=True, stop=True).then_inc(b2_done, 1)

        @block.vector
        def _(dve):
            ch = Chain(dve, dve_step)
            ch.link(dve.tensor_reduce(mx[:, :], s_flat, AX.X, ALU.max))
            dve.tensor_tensor(s_flat, s_flat, mx[:, :].unsqueeze(2).to_broadcast([HALF, NT, E]), ALU.subtract).then_inc(shifted, 1)
            dve.wait_ge(exps, 1)
            ch.link(dve.tensor_reduce(mx[:, :], s_flat, AX.X, ALU.add))
            ch.link(dve.reciprocal(mx[:, :], mx[:, :]))
            dve.tensor_tensor(s_flat, s_flat, mx[:, :].unsqueeze(2).to_broadcast([HALF, NT, E]), ALU.mult).then_inc(probs, 1)
            ch.link(dve.memset(ones[:, :], 1.0))
            for r in range(NBG // 2):
                dve.wait_ge(s_t, r + 1)
                ch.link(dve.tensor_copy(st[:, 2 * r:2 * r + 2, :], p_s[r][:, 0:2 * L].rearrange("p (g t) -> p g t", g=2)))
            rounds = (TOPK + 7) // 8
            for r in range(rounds):
                for g in range(NBG):
                    m = dve.max(m8[:, g, :], (st if r == 0 else work)[:, g, :])
                ch.link(m)
                if r < rounds - 1:
                    for g in range(NBG):
                        m = dve.match_replace(work[:, g, :], m8[:, g, :], (st if r == 0 else work)[:, g, :], -1.0)
                    ch.link(m)
            at = TOPK - 1 - 8 * (rounds - 1)
            for g in range(NBG):
                kth = m8[:, g, at:at + 1]
                dve.tensor_scalar(above[:, g, :], st[:, g, :], kth, None, ALU.is_gt, ALU.add, accum_out=count[:, g:g + 1])
                m = dve.tensor_scalar(equal[:, g, :], st[:, g, :], kth, None, ALU.is_equal)
            ch.link(m)
            ch.link(dve.tensor_scalar(room[:, :], count[:, :], -1.0, float(TOPK), ALU.mult, ALU.add))
            for g in range(NBG):
                m = dve.tensor_tensor_scan(rank[:, g, :], ones[:, :], equal[:, g, :], 0.0, ALU.mult, ALU.add)
            ch.link(m)
            for g in range(NBG):
                m = dve.scalar_tensor_tensor(work[:, g, :], rank[:, g, :], room[:, g:g + 1], equal[:, g, :], ALU.is_le, ALU.mult)
            ch.link(m)
            ch.link(dve.tensor_tensor(above[:, :, :], above[:, :, :], work[:, :, :], ALU.add))
            dve.tensor_tensor(gate[:, :, :], above[:, :, :], st[:, :, :], ALU.mult).then_inc(gates, NBG)
            for half in range(2):
                dve.wait_ge(g_t, half + 1)
                dve.tensor_copy(g_tok[:, half, :, :].rearrange("t b e -> t (b e)"), p_g[half][0:HALF, :])
            for n in range(2 * NBG * 4):
                g, half, sub = n // 8, n // 4 % 2, n % 4
                tiles = h[:, :].rearrange("t (b h f) -> t h b f", h=2, f=F)[:, half, g * BG + sub * 4:g * BG + sub * 4 + 4, :]
                dve.wait_ge(b2_done, n + 1)
                dve.tensor_tensor(tiles, p_b[n % 4][0:HALF, :].rearrange("t (b f) -> t b f", b=4), tiles, ALU.add).then_inc(b2_added, 1)
            dve.wait_ge(b2_added, 2 * NBG * 4)


def mixture0(nc, k, h, xf, g_tok, weights0):
    ctx = ExitStack()
    with ctx:
        CH = F0 // F
        w1, b1, w2 = weights0
        hid = k.sb(ctx, "hid", [F, 4, CH, QN])
        gq = k.sb(ctx, "gq", [HALF, 2, 2, E])
        acc = k.sb(ctx, "acc", [HALF, QF])
        p_1 = [[k.ps(ctx, f"p_1{r}{c}") for c in range(CH)] for r in range(2)]
        p_2 = [k.ps(ctx, f"p_2{r}") for r in range(4)]

        w1_done = k.sem("w1_done")
        gelu_done = k.sem("gelu_done")
        w2_done = k.sem("w2_done")
        acc_done = k.sem("acc_done")
        gq_copied = k.sem("gq_copied")
        block = ctx.enter_context(nc.Block())

        @block.tensor
        def _(pe):
            def down(n, e):
                pe.wait_ge(gelu_done, n * 2 + 2 + 4)
                pe.wait_ge(acc_done, n + 1)
                for j in range(QT):
                    for c in range(CH):
                        m = pe.matmul(p_2[e % 4][0:HALF, j * F:(j + 1) * F], hid[:, e % 4, c, j * HALF:(j + 1) * HALF],
                                      w2[:, e, c, :], start=(c == 0), stop=(c == CH - 1))
                m.then_inc(w2_done, 1)

            with pe.Fori(0, NQ) as i:
                for e in range(E):
                    n = i * E + e
                    pe.wait_ge(gelu_done, n * 2 + 2)
                    for c in range(CH):
                        pe.matmul(p_1[e % 2][c][:, 0:QN], w1[:, e, c * F:(c + 1) * F], xf[:, bass.ds(i * QN, QN)],
                                  start=True, stop=True).then_inc(w1_done, 1)
                    if e:
                        down(n - 1, e - 1)
                down(i * E + E - 1, E - 1)

        @block.scalar
        def _(act):
            act.sem_inc(gelu_done, 4)
            with act.Fori(0, NQ) as i:
                for e in range(E):
                    n = i * E + e
                    act.wait_ge(w2_done, n + 1)
                    for c in range(CH):
                        act.wait_ge(w1_done, n * 2 + c + 1)
                        act.activation(hid[:, e % 4, c, :], p_1[e % 2][c][:, 0:QN], ACT.Gelu,
                                       bias=b1[:, e, c:c + 1]).then_inc(gelu_done, 1)

        @block.vector
        def _(dve):
            dve.sem_inc(w2_done, 4)
            dve.sem_inc(acc_done, 4)
            with dve.Fori(0, NQ) as i:
                dve.wait_ge(acc_done, i * E + 4)
                apart(dve)
                dve.tensor_copy(gq[:, :, :, :], g_tok[:, :, bass.ds(i * 2, 2), :]).then_inc(gq_copied, 1)
                dve.wait_ge(gq_copied, i + 1)
                for e in range(E):
                    n = i * E + e
                    dve.wait_ge(acc_done, n + 4)
                    dve.wait_ge(w2_done, n + 1 + 4)
                    apart(dve)
                    for j in range(QT):
                        at = bass.ds(i * QF + j * F, F)
                        a = acc[:, j * F:(j + 1) * F]
                        m = dve.scalar_tensor_tensor(h[:, at] if e == E - 1 else a, p_2[e % 4][0:HALF, j * F:(j + 1) * F],
                                                     gq[:, j % 2, j // 2, e:e + 1], h[:, at] if e == 0 else a,
                                                     ALU.mult, ALU.add)
                    m.then_inc(acc_done, 1)


def retain_and_route(nc, k, d, ident, small, h, base, xs_dram, h3_dram):
    ctx = ExitStack()
    with ctx:
        HG = 4
        STEP = [(b, half, g) for b in range(2) for half in (1, 0) for g in range(HEADS // HG)]
        NH = len(STEP)
        WL = 96
        wq = k.sb(ctx, "wq", [F, F])
        wk = k.sb(ctx, "wk", [F, F])
        wvg = k.sb(ctx, "wvg", [F, 2 * F])
        bvg = k.sb(ctx, "bvg", [HALF, 2 * F])
        wg1 = k.sb(ctx, "wg1", [F, WL])
        bg1 = k.sb(ctx, "bg1", [HALF, E])
        prio = k.sb(ctx, "prio", [HALF, E])
        before_f = k.sb(ctx, "before_f", [HALF, HALF])
        before = k.sb(ctx, "before", [HALF, HALF], BF16)
        ones = k.sb(ctx, "ones_g", [HALF, HALF], BF16)
        decay = k.sb(ctx, "decay", [HALF, HEADS, HALF])
        decay_i = k.sb(ctx, "decay_i", [F, HALF])
        decay_j = k.sb(ctx, "decay_j", [HALF, F])
        same = k.sb(ctx, "same", [F, F])
        bk_row = k.sb(ctx, "bk_row", [HALF, F])
        nhalf = k.sb(ctx, "nhalf_g", [HALF, QT])

        def norm_buffers(name):
            return (k.sb(ctx, "lst_" + name, [HALF, 2, QT, 6]), k.sb(ctx, "lmv_" + name, [HALF, 2, QT, 2]),
                    k.sb(ctx, "lve_" + name, [HALF, 2, QT]), k.sb(ctx, "lrs_" + name, [HALF, 2, QT]))

        prep_norm = norm_buffers("p")
        route_norm = norm_buffers("r")
        xn = k.sb(ctx, "xn_g", [HALF, 2, QF])
        xt = k.sb(ctx, "xt_g", [F, 2, QN])
        qm = k.sb(ctx, "qm", [F, 2, HEADS, QN])
        kt = k.sb(ctx, "kt", [F, 2, QN])
        q_first = k.sb(ctx, "q_first", [F, 2, HALF])
        q_decay = k.sb(ctx, "q_decay", [F, 2, 2, HALF])
        k_sum = k.sb(ctx, "k_sum", [HALF, 2, F])
        k_decay = k.sb(ctx, "k_decay", [HALF, 2, F])
        state = k.sb(ctx, "state", [F, 2, F])
        vp = k.sb(ctx, "vp", [HALF, 2, QT, HEADS, F])
        gate = k.sb(ctx, "gate_g", [HALF, QF])
        silu = k.sb(ctx, "silu", [HALF, 2, QF])
        probs = k.sb(ctx, "probs_g", [HALF, 4, QN])
        gated = k.sb(ctx, "gated", [HALF, QF])
        h3 = k.sb(ctx, "h3", [HALF, 2, QF])
        xr = k.sb(ctx, "xr", [HALF, 2, QF])
        xrt = k.sb(ctx, "xrt", [F, QN])
        xs = k.sb(ctx, "xs", [HALF, 2, QF])
        lg = k.sb(ctx, "lg", [HALF, QT, E])
        ez = k.sb(ctx, "ez", [HALF, QT, E])
        eq = k.sb(ctx, "eq", [HALF, QT, E])
        hot = k.sb(ctx, "hot", [HALF, QT + 1, E], BF16)
        pz = k.sb(ctx, "pz", [HALF, QT, E])
        r4 = k.sb(ctx, "r4", [HALF, 6, QT])
        idx = k.sb(ctx, "idx", [HALF, 2, QT], I32)
        p_a = k.ps(ctx, "p_a")
        p_b = k.ps(ctx, "p_bq")
        p_s = [k.ps(ctx, f"p_sc{r}") for r in range(2)]
        p_o = [k.ps(ctx, f"p_o{u}") for u in range(2)]
        p_r = k.ps(ctx, "p_r")
        p_l = k.ps(ctx, "p_lr")

        consts = k.sem("consts_g")
        set_up = k.sem("set_up")
        wg1_cleared = k.sem("wg1_cleared")
        prep_step = k.sem("prep_step")
        route_step = k.sem("route_step")
        k_step = k.sem("k_step")
        pool_prep = k.sem("pool_prep")
        pool_route = k.sem("pool_route")
        var_p = k.sem("var_p")
        var_r = k.sem("var_r")
        rstd_p = k.sem("rstd_p")
        rstd_r = k.sem("rstd_r")
        xn_ready = k.sem("xn_ready_g")
        xt_done = k.sem("xt_done_g")
        xt_copied = k.sem("xt_copied_g")
        q_done = k.sem("q_done")
        q_copied = k.sem("q_copied")
        k_done = k.sem("k_done")
        k_copied = k.sem("k_copied")
        vg_done = k.sem("vg_done")
        v_added = k.sem("v_added")
        k_tok_done = k.sem("k_tok_done")
        k_decayed = k.sem("k_decayed")
        q_decayed = k.sem("q_decayed")
        state_done = k.sem("state_done")
        state_copied = k.sem("state_copied")
        silu_done = k.sem("silu_done")
        s_done = k.sem("s_done")
        decayed = k.sem("decayed")
        av_done = k.sem("av_done")
        h3_done = k.sem("h3_done")
        h3_out = [k.sem(f"h3_out{u}") for u in range(2)]
        xr_ready = k.sem("xr_ready")
        xr_done = k.sem("xr_done")
        xr_copied = k.sem("xr_copied")
        lg_done = k.sem("lg_done")
        z_ready = k.sem("z_ready")
        ez_done = k.sem("ez_done")
        hot_ready = k.sem("hot_ready")
        pre_done = k.sem("pre_done")
        idx_done = k.sem("idx_done")
        sent = [k.sem(f"sent{u}") for u in range(2)]
        xs_free = k.sem("xs_free")
        block = ctx.enter_context(nc.Block())

        def ahead(q, prep):
            return prep and not (isinstance(q, int) and q == NQ - 2)

        @block.sync
        def _(sp):
            for name, to in (("wq", wq), ("wk", wk), ("wvg", wvg), ("before", before_f), ("decay_i", decay_i), ("decay_j", decay_j), ("same", same)):
                sp.dma_start(to[:, :], d[name]).then_inc(consts, 16)
            sp.dma_start(decay[:, :, :], d["decay"]).then_inc(consts, 16)
            sp.wait_ge(wg1_cleared, 1)
            sp.dma_start(wg1[:, 0:E], d["wg1"]).then_inc(consts, 16)
            for name, to, n in (("bvg", bvg, 2 * F), ("bg1", bg1, E), ("prio", prio, E), ("bk", bk_row, F), ("region", base, E)):
                sp.dma_start(to[:, :], bass.AP(d[name].tensor, 0, [[0, HALF], [1, n]])).then_inc(consts, 16)

            def store(q, u):
                sp.wait_ge(h3_done, q + 1 + 2)
                dst = h3_dram[bass.ds(q * QN, QN), :].rearrange("(j t) f -> t j f", j=QT)
                sp.dma_start(dst, h3[:, u, :].rearrange("t (j f) -> t j f", j=QT)).then_inc(h3_out[u], 16)

            with sp.Fori(0, NQ // 2) as j:
                for u in range(2):
                    store(j * 2 + u, u)
            for u in range(2):
                sp.wait_ge(h3_out[u], 16 * (NQ // 2 + 1))

        @block.tensor
        def _(pe):
            pe.wait_ge(consts, 224)
            pe.wait_ge(set_up, 5)

            def prep_x(q, u):
                pe.wait_ge(xn_ready, q + 1)
                pe.wait_ge(state_copied, q + 1)
                for j in range(QT):
                    m = pe.transpose(p_a[:, j * HALF:(j + 1) * HALF], xn[:, u, j * F:(j + 1) * F], ident[0:HALF, 0:HALF])
                m.then_inc(xt_done, 1)

            def prep_q(q, u):
                pe.wait_ge(xt_copied, q + 1)
                pe.matmul(p_b[:, 0:QN], wq[:, :], xt[:, u, :], start=True, stop=True).then_inc(q_done, 1)

            def prep_k(q, u):
                pe.matmul(p_a[:, 0:QN], wk[:, :], xt[:, u, :], start=True, stop=True).then_inc(k_done, 1)

            def prep_v(q, u):
                pe.wait_ge(q_copied, q + 1)
                for b in range(2):
                    if b:
                        pe.wait_ge(k_copied, q + 1)
                    for half in range(2):
                        j = 2 * b + half
                        m = pe.matmul((p_b, p_a)[b][0:HALF, half * 2 * F:(half + 1) * 2 * F],
                                      xt[:, u, j * HALF:(j + 1) * HALF], wvg[:, :], start=True, stop=True)
                    m.then_inc(vg_done, 1)

            def scores(q, u, n):
                if n == 0:
                    pe.wait_ge(q_copied, q + 1)
                    pe.wait_ge(k_copied, q + 1)
                pe.wait_ge(decayed, q * NH + n + 1)
                b, half, g = STEP[n]
                tile = slice((2 * b + half) * HALF, (2 * b + half + 1) * HALF)
                pe.matmul(p_s[n % 2][0:HALF, 0:QN], kt[:, u, tile], qm[:, u, g * HG:(g + 1) * HG, tile],
                          start=True, stop=True).then_inc(s_done, 1)

            def prep_k_tokens(q, u):
                pe.wait_ge(v_added, q * 2 + 1 + 2)
                for b in range(2):
                    m = pe.matmul(p_b[0:HALF, b * F:(b + 1) * F], xt[:, u, (2 * b + 1) * HALF:(2 * b + 2) * HALF], wk[:, :],
                                  start=True, stop=True)
                m.then_inc(k_tok_done, 1)

            def prep_state(q, u):
                pe.wait_ge(v_added, q * 2 + 2 + 2)
                pe.wait_ge(k_decayed, q + 1)
                for b in range(2):
                    m = pe.matmul(p_a[:, b * F:(b + 1) * F], k_decay[:, b, :], vp[:, u, 2 * b + 1, :, 0:HD], start=True, stop=True)
                m.then_inc(state_done, 1)

            def values(q, u, n):
                if n == 0:
                    pe.wait_ge(h3_done, q + 1)
                    pe.wait_ge(v_added, q * 2 + 2 + 2)
                pe.wait_ge(decayed, q * NH + n + 1 + 2)
                b, half, g = STEP[n]
                first, last = g == 0, g == HEADS // HG - 1
                flat = vp[:, u, 2 * b + half, :, :].rearrange("t h x -> t (h x)")
                to = p_o[u][0:HALF, (2 * b + half) * F:(2 * b + half + 1) * F]
                for c in range(HG):
                    head = g * HG + c
                    at = head * (F - HD)
                    m = pe.matmul(to, probs[:, n % 4, c * HALF:(c + 1) * HALF], flat[:, at:at + F],
                                  start=(first and c == 0), stop=(last and half == 1 and c == HG - 1))
                if last and half == 0:
                    pe.wait_ge(q_decayed, q + 1 + 1)
                    pe.wait_ge(state_copied, q + 1 + 1)
                    m = pe.matmul(to, q_decay[:, u, b, :], state[:, b, :], start=False, stop=True)
                m.then_inc(av_done, 1)

            def route_x(q, u):
                pe.wait_ge(xr_ready, q + 1)
                pe.wait_ge(xr_copied, q + 1)
                for j in range(QT):
                    m = pe.transpose(p_r[:, j * HALF:(j + 1) * HALF], xr[:, u, j * F:(j + 1) * F], ident[0:HALF, 0:HALF])
                m.then_inc(xr_done, 1)

            def route_logits(q):
                pe.wait_ge(xr_copied, q + 2)
                pe.wait_ge(idx_done, q + 1)
                for j in range(QT):
                    m = pe.matmul(p_l[0:HALF, j * WL:(j + 1) * WL], xrt[:, j * HALF:(j + 1) * HALF], wg1[:, :],
                                  start=True, stop=True)
                m.then_inc(lg_done, 1)

            def route_places(q):
                pe.wait_ge(hot_ready, q + 1)
                to = p_l[0:HALF, QT * WL:QT * WL + (QT + 1) * E].rearrange("t (j e) -> t j e", e=E)
                pe.matmul(to, before[:, :], hot[:, :, :], start=True, stop=False)
                for j in range(QT):
                    m = pe.matmul(to[:, j + 1:, :], ones[:, :], hot[:, j, :].unsqueeze(1).to_broadcast([HALF, QT - j, E]),
                                  start=False, stop=(j == QT - 1))
                m.then_inc(pre_done, 1)

            def quad(q, u, prep, route, place):
                for n in range(NH):
                    scores(q, u, n)
                    if n:
                        values(q, u, n - 1)
                    if n == 0:
                        prep_state(q, u)
                    if place and n == 2:
                        route_places(q - 2)
                    if prep and n == 2:
                        prep_x(q + 1, 1 - u)
                    if prep and n == 3:
                        prep_q(q + 1, 1 - u)
                        prep_k(q + 1, 1 - u)
                    if prep and n == 6:
                        prep_v(q + 1, 1 - u)
                    if route and n == 6:
                        route_x(q - 1, 1 - u)
                    if route and n == 7:
                        route_logits(q - 1)
                if prep:
                    prep_k_tokens(q + 1, 1 - u)
                values(q, u, NH - 1)

            prep_x(0, 0)
            prep_q(0, 0)
            prep_k(0, 0)
            prep_v(0, 0)
            prep_k_tokens(0, 0)
            quad(0, 0, True, False, False)
            quad(1, 1, True, True, False)
            for q in (2, 3):
                quad(q, q % 2, True, True, True)
            with pe.Fori(2, NQ // 2 - 1) as t:
                for u in range(2):
                    quad(t * 2 + u, u, True, True, True)
            quad(NQ - 2, 0, True, True, True)
            quad(NQ - 1, 1, False, True, True)
            route_places(NQ - 2)
            route_x(NQ - 1, 1)
            route_logits(NQ - 1)
            route_places(NQ - 1)

        @block.scalar
        def _(act):
            act.sem_inc(xr_copied, 1)
            for u in range(2):
                act.sem_inc(h3_out[u], 16)
            act.wait_ge(set_up, 5)

            def prep_x(q, u):
                act.wait_ge(k_tok_done, q + 1)
                act.wait_ge(xt_done, q + 1 + 2)
                act.activation(xt[:, u, :], p_a[:, 0:QN], ACT.Copy).then_inc(xt_copied, 1)

            def prep_q(q, u):
                act.wait_ge(s_done, q * NH + NH)
                act.wait_ge(q_done, q + 1)
                for head in range(HEADS):
                    rows, odd = slice(head // 2 * 32, head // 2 * 32 + 32), head % 2
                    act.activation(qm[rows, u, head, :], p_b[rows, 0:QN], ACT.Identity, bias=small[rows, 6 + odd:7 + odd],
                                       scale=small[rows, 2 + odd:3 + odd])
                act.wait_ge(q_decayed, q + 1)
                act.activation(q_first[:, :, :], p_b[:, 0:QN].rearrange("f (b o t) -> f b o t", b=2, o=2)[:, :, 0, :],
                               ACT.Identity, bias=small[:, 4:5]).then_inc(q_copied, 1)

            def prep_k(q, u):
                act.wait_ge(s_done, q * NH + NH)
                act.wait_ge(k_done, q + 1)
                act.activation(kt[:, u, :], p_a[:, 0:QN], ACT.Identity, bias=small[:, 5:6]).then_inc(k_copied, 1)

            def prep_silu(q, u):
                act.wait_ge(h3_done, q + 1)
                act.wait_ge(v_added, q * 2 + 2 + 2)
                act.activation(silu[:, u, :], gate[:, :], ACT.Silu).then_inc(silu_done, 1)

            def route_x(q):
                act.wait_ge(lg_done, q + 1)
                act.wait_ge(xr_done, q + 1 + 2)
                act.activation(xrt[:, :], p_r[:, 0:QN], ACT.Copy).then_inc(xr_copied, 1)

            def route_exp(q):
                act.wait_ge(z_ready, q + 1)
                act.activation(ez[:, :, :], lg[:, :, :], ACT.Exp).then_inc(ez_done, 1)

            def quad(q, u, prep, route):
                if prep:
                    prep_x(q + 1, 1 - u)
                    prep_q(q + 1, 1 - u)
                    prep_k(q + 1, 1 - u)
                if route:
                    route_x(q - 1)
                    route_exp(q - 1)
                if prep:
                    prep_silu(q + 1, 1 - u)

            prep_x(0, 0)
            prep_q(0, 0)
            prep_k(0, 0)
            prep_silu(0, 0)
            quad(0, 0, True, False)
            for q in (1, 2, 3):
                quad(q, q % 2, True, True)
            with act.Fori(2, NQ // 2 - 1) as t:
                for u in range(2):
                    quad(t * 2 + u, u, True, True)
            quad(NQ - 2, 0, True, True)
            quad(NQ - 1, 1, False, True)
            route_x(NQ - 1)
            route_exp(NQ - 1)

        @block.gpsimd
        def _(pool):
            pool.memset(nhalf[:, :], -0.5)
            pool.memset(vp[:, :, :, :, :], 0.0).then_inc(set_up, 1)
            pool.wait_ge(set_up, 5)

            def rstd(q, u, var, bufs, step, done):
                _, lmv, lve, lrs = bufs
                pool.wait_ge(var, q + 1)
                apart(pool)
                ch = Chain(pool, step, q, 1)
                ch.link(pool.tensor_scalar(lve[:, u, :], lmv[:, u, :, 1], EPS, None, ALU.add))
                pool.tensor_tensor(out=lrs[:, u, :], in0=lve[:, u, :], in1=nhalf[:, :], op=ALU.pow).then_inc(done, 1)

            def send(q, u, t):
                if not (isinstance(q, int) and q == 0):
                    pool.wait_ge(sent[1 - u], (t + u) * 64)
                    pool.sem_inc(xs_free, 1)
                pool.wait_ge(idx_done, q + 2)
                apart(pool)
                for j in range(QT):
                    pool.indirect_dma_start(xs_dram[:, :], bass.IndirectOffsetOnAxis(ap=idx[:, u, j:j + 1], axis=0),
                                            xs[:, u, j * F:(j + 1) * F], None).then_inc(sent[u], 16)

            def quad(q, u, t, prep, route, place):
                if route:
                    rstd(q - 1, 1 - u, var_r, route_norm, pool_route, rstd_r)
                if ahead(q, prep):
                    rstd(q + 2, u, var_p, prep_norm, pool_prep, rstd_p)
                if place:
                    send(q - 2, u, t - 1)

            for q in range(2):
                rstd(q, q, var_p, prep_norm, pool_prep, rstd_p)
            quad(0, 0, 0, True, False, False)
            quad(1, 1, 0, True, True, False)
            for q in (2, 3):
                quad(q, q % 2, 1, True, True, True)
            with pool.Fori(2, NQ // 2 - 1) as t:
                for u in range(2):
                    quad(t * 2 + u, u, t, True, True, True)
            quad(NQ - 2, 0, NQ // 2 - 1, True, True, True)
            quad(NQ - 1, 1, NQ // 2 - 1, False, True, True)
            send(NQ - 2, 0, NQ // 2 - 1)
            rstd(NQ - 1, 1, var_r, route_norm, pool_route, rstd_r)
            send(NQ - 1, 1, NQ // 2 - 1)
            for u in range(2):
                pool.wait_ge(sent[u], 64 * (NQ // 2))

        @block.vector
        def _(dve):
            for s, n in ((xt_done, 2), (vg_done, 4), (v_added, 2), (s_done, 2 * NH), (decayed, 2), (av_done, 2 * NH),
                         (h3_done, 2), (xr_done, 2), (lg_done, 1), (silu_done, 1), (idx_done, 1), (k_tok_done, 2),
                         (q_decayed, 1), (state_done, 1), (state_copied, 1), (xs_free, 2)):
                dve.sem_inc(s, n)
            dve.memset(wg1[:, :], 0.0).then_inc(wg1_cleared, 1)
            dve.memset(qm[:, :, :, :], 0.0).then_inc(set_up, 1)
            dve.wait_ge(consts, 224)
            dve.tensor_copy(before[:, :], before_f[:, :])
            dve.memset(hot[:, QT, :], 0.0)
            dve.memset(ones[:, :], 1.0).then_inc(set_up, 1)
            dve.tensor_tensor(small[:, 6:7], small[:, 4:5], small[:, 2:3], ALU.mult).then_inc(set_up, 1)
            dve.tensor_tensor(small[:, 7:8], small[:, 4:5], small[:, 3:4], ALU.mult).then_inc(set_up, 1)

            def stats(ch, u, bufs, src, var):
                lst, lmv, _, _ = bufs
                for j in range(QT):
                    m = dve.bn_stats(lst[:, u, j, :], src(j))
                ch.link(m)
                apart(dve)
                for j in range(QT):
                    m = dve.bn_aggr(lmv[:, u, j, :], lst[:, u, j, :])
                m.then_inc(var, 1)

            def normed(u, bufs, src, to):
                _, lmv, _, lrs = bufs
                for j in range(QT):
                    m = dve.tensor_scalar(to[:, u, j * F:(j + 1) * F], src(j), lmv[:, u, j, 0:1], lrs[:, u, j:j + 1],
                                          ALU.subtract, ALU.mult)
                return m

            def prep_stats(q, u):
                stats(Chain(dve, prep_step, q, 1), u, prep_norm, lambda j: h[:, bass.ds(q * QF + j * F, F)], var_p)

            def prep_xn(q, u):
                dve.wait_ge(xt_done, q + 1)
                dve.wait_ge(rstd_p, q + 1)
                apart(dve)
                normed(u, prep_norm, lambda j: h[:, bass.ds(q * QF + j * F, F)], xn).then_inc(xn_ready, 1)

            def prep_vg(q, u):
                dve.wait_ge(av_done, q * NH + NH)
                dve.wait_ge(silu_done, q + 1)
                for b in range(2):
                    dve.wait_ge(vg_done, q * 2 + b + 1 + 4)
                    src = (p_b, p_a)[b][0:HALF, :].rearrange("t (j n) -> t j n", j=2)
                    for half in range(2):
                        dve.tensor_tensor(vp[:, u, 2 * b + half, :, 0:HD], src[:, half, 0:F].rearrange("t (h x) -> t h x", h=HEADS),
                                          bvg[:, 0:F].rearrange("t (h x) -> t h x", h=HEADS), ALU.add)
                    dve.tensor_tensor(gate[:, b * 2 * F:(b + 1) * 2 * F].rearrange("t (j f) -> t j f", j=2), src[:, :, F:2 * F],
                                      bvg[:, F:2 * F].unsqueeze(1).to_broadcast([HALF, 2, F]), ALU.add).then_inc(v_added, 1)

            def prep_q_decay(q, u):
                dve.wait_ge(av_done, q * NH + NH)
                dve.wait_ge(q_copied, q + 1)
                dve.tensor_tensor(q_decay[:, u, :, :], q_first[:, :, :], decay_i[:, :].unsqueeze(1).to_broadcast([F, 2, HALF]),
                                  ALU.mult).then_inc(q_decayed, 1)

            def prep_k_decay(q):
                ch = Chain(dve, k_step, q, 1)
                dve.wait_ge(k_tok_done, q + 1 + 2)
                ch.link(dve.tensor_tensor(k_sum[:, :, :], p_b[0:HALF, 0:2 * F].rearrange("t (b f) -> t b f", b=2),
                                          bk_row[:, :].unsqueeze(1).to_broadcast([HALF, 2, F]), ALU.add))
                dve.wait_ge(state_done, q + 1)
                dve.tensor_tensor(k_decay[:, :, :], k_sum[:, :, :], decay_j[:, :].unsqueeze(1).to_broadcast([HALF, 2, F]),
                                  ALU.mult).then_inc(k_decayed, 1)

            def keep_state(q):
                dve.wait_ge(av_done, q * NH + 2 * NH)
                dve.wait_ge(state_done, q + 1 + 1)
                dve.tensor_tensor(state[:, :, :], p_a[:, 0:2 * F].rearrange("p (b f) -> p b f", b=2),
                                  same[:, :].unsqueeze(1).to_broadcast([F, 2, F]), ALU.mult).then_inc(state_copied, 1)

            def decaying(q, n):
                g = STEP[n][2]
                dve.wait_ge(av_done, q * NH + n - 3 + 2 * NH)
                dve.wait_ge(s_done, q * NH + n + 1 + 2 * NH)
                dve.tensor_tensor(probs[:, n % 4, :], p_s[n % 2][0:HALF, 0:QN],
                                  decay[:, g * HG:(g + 1) * HG, :].rearrange("t h x -> t (h x)"), ALU.mult).then_inc(decayed, 1)

            def finish(ch, q, u, t):
                dve.wait_ge(av_done, q * NH + NH + 2 * NH)
                dve.wait_ge(silu_done, q + 1 + 1)
                ch.link(dve.tensor_tensor(gated[:, :], p_o[u][0:HALF, :], silu[:, u, :], ALU.mult))
                dve.wait_ge(h3_out[u], t * 16 + 16)
                apart(dve)
                dve.tensor_tensor(h3[:, u, :], gated[:, :], h[:, bass.ds(q * QF, QF)], ALU.add).then_inc(h3_done, 1)

            def route_stats(ch, q, u):
                dve.wait_ge(h3_done, q + 1 + 2)
                stats(ch, u, route_norm, lambda j: h3[:, u, j * F:(j + 1) * F], var_r)

            def route_xn(q, u):
                dve.wait_ge(xr_done, q + 1)
                dve.wait_ge(rstd_r, q + 1)
                normed(u, route_norm, lambda j: h3[:, u, j * F:(j + 1) * F], xr).then_inc(xr_ready, 1)

            def over_e(r):
                return r4[:, r, :].unsqueeze(2).to_broadcast([HALF, QT, E])

            def over_j(c):
                return c[:, :].unsqueeze(1).to_broadcast([HALF, QT, E])

            def logits(ch, q):
                dve.wait_ge(lg_done, q + 1 + 1)
                ch.link(dve.tensor_tensor(lg[:, :, :], p_l[0:HALF, 0:QT * WL].rearrange("t (j e) -> t j e", j=QT)[:, :, 0:E], over_j(bg1), ALU.add))
                ch.link(dve.tensor_reduce(r4[:, 0, :], lg[:, :, :], AX.X, ALU.max))
                dve.tensor_tensor(lg[:, :, :], lg[:, :, :], over_e(0), ALU.subtract).then_inc(z_ready, 1)

            def choice(ch, q, u):
                dve.wait_ge(ez_done, q + 1)
                dve.tensor_reduce(r4[:, 1, :], ez[:, :, :], AX.X, ALU.add)
                ch.link(dve.tensor_reduce(r4[:, 2, :], ez[:, :, :], AX.X, ALU.max))
                dve.reciprocal(r4[:, 3, :], r4[:, 1, :])
                ch.link(dve.tensor_tensor(eq[:, :, :], ez[:, :, :], over_e(2), ALU.is_equal))
                dve.tensor_tensor(r4[:, 4, :], r4[:, 2, :], r4[:, 3, :], ALU.mult)
                ch.link(dve.tensor_tensor(eq[:, :, :], eq[:, :, :], over_j(prio), ALU.mult))
                ch.link(dve.tensor_reduce(r4[:, 5, :], eq[:, :, :], AX.X, ALU.max))
                dve.tensor_tensor(hot[:, 0:QT, :], eq[:, :, :], over_e(5), ALU.is_equal).then_inc(hot_ready, 1)

            def rows(q, u):
                dve.wait_ge(xs_free, q + 1)
                dve.tensor_tensor(xs[:, u, :].rearrange("t (j f) -> t j f", j=QT), xr[:, u, :].rearrange("t (j f) -> t j f", j=QT),
                                  r4[:, 4, :].unsqueeze(2).to_broadcast([HALF, QT, F]), ALU.mult)

            def places(ch, q, u):
                dve.wait_ge(pre_done, q + 1)
                pl = p_l[0:HALF, QT * WL:QT * WL + (QT + 1) * E]
                ch.link(dve.tensor_tensor(pz[:, :, :], pl[:, 0:QT * E].rearrange("t (j e) -> t j e", j=QT), over_j(base), ALU.add))
                dve.tensor_tensor(base[:, :], pl[:, QT * E:(QT + 1) * E], base[:, :], ALU.add)
                ch.link(dve.tensor_tensor(pz[:, :, :], pz[:, :, :], hot[:, 0:QT, :], ALU.mult))
                ch.link(dve.tensor_reduce(r4[:, 0, :], pz[:, :, :], AX.X, ALU.add))
                dve.tensor_copy(idx[:, u, :], r4[:, 0, :]).then_inc(idx_done, 1)

            ROUTE_LINKS, LATE_LINKS = 11, 7

            def late(q):
                return Chain(dve, route_step, q, ROUTE_LINKS, ROUTE_LINKS - LATE_LINKS)

            def quad(q, u, t, prep, route, place):
                if route:
                    ch = Chain(dve, route_step, q - 1, ROUTE_LINKS)
                if place:
                    ch_late = late(q - 2)
                for n in range(NH):
                    decaying(q, n)
                    if place and n == 0:
                        choice(ch_late, q - 2, u)
                    if prep and n == 1:
                        prep_xn(q + 1, 1 - u)
                    if n == 1:
                        keep_state(q)
                    if place and n == 1:
                        rows(q - 2, u)
                    if place and n == 2:
                        places(ch_late, q - 2, u)
                        assert ch_late.n == LATE_LINKS
                    if route and n == 2:
                        finish(ch, q - 1, 1 - u, t - 1 if u == 0 else t)
                    if route and n == 3:
                        route_stats(ch, q - 1, 1 - u)
                    if route and n == 4:
                        route_xn(q - 1, 1 - u)
                    if prep and n == 5:
                        prep_q_decay(q + 1, 1 - u)
                    if ahead(q, prep) and n == 5:
                        prep_stats(q + 2, u)
                    if prep and n == 6:
                        prep_vg(q + 1, 1 - u)
                if prep:
                    prep_k_decay(q + 1)
                if route:
                    logits(ch, q - 1)
                    assert ch.n == ROUTE_LINKS - LATE_LINKS

            prep_stats(0, 0)
            prep_stats(1, 1)
            prep_xn(0, 0)
            prep_q_decay(0, 0)
            prep_vg(0, 0)
            prep_k_decay(0)
            quad(0, 0, 0, True, False, False)
            quad(1, 1, 0, True, True, False)
            for q in (2, 3):
                quad(q, q % 2, 1, True, True, True)
            with dve.Fori(2, NQ // 2 - 1) as t:
                for u in range(2):
                    quad(t * 2 + u, u, t, True, True, True)
            quad(NQ - 2, 0, NQ // 2 - 1, True, True, True)
            quad(NQ - 1, 1, NQ // 2 - 1, False, True, True)
            ch = late(NQ - 2)
            choice(ch, NQ - 2, 0)
            rows(NQ - 2, 0)
            places(ch, NQ - 2, 0)
            ch = Chain(dve, route_step, NQ - 1, ROUTE_LINKS)
            finish(ch, NQ - 1, 1, NQ // 2 - 1)
            route_stats(ch, NQ - 1, 1)
            route_xn(NQ - 1, 1)
            logits(ch, NQ - 1)
            choice(ch, NQ - 1, 1)
            rows(NQ - 1, 1)
            places(ch, NQ - 1, 1)


def plan_tiles(nc, k, d, base, tab, xs_dram, h3_dram, weights1):
    ctx = ExitStack()
    with ctx:
        zeros = k.sb(ctx, "zeros", [128, RB // 128 * F])
        v = k.sb(ctx, "v_h", [1, 10, E])
        vi = k.sb(ctx, "vi_h", [1, 3, E], I32)
        kk = k.sb(ctx, "kk", [1, NK, E])
        a = k.sb(ctx, "a_h", [1, NK, E])
        ind = k.sb(ctx, "ind", [1, NK, E])
        val = k.sb(ctx, "val", [1, 2, NK, E])
        tf = k.sb(ctx, "tf", [1, 3, NK])
        consts = k.sem("consts_h")
        zero_set = k.sem("zero_set")
        ends_ready = k.sem("ends_ready")
        zero_out = k.sem("zero_out")
        weights_in = k.sem("weights_in")
        step = k.sem("step_h")
        block = ctx.enter_context(nc.Block())

        @block.gpsimd
        def _(pool):
            pool.memset(zeros[:, :], 0.0).then_inc(zero_set, 1)

        def rows(ap):
            return ap.rearrange("(p r) f -> p (r f)", p=128)

        @block.sync
        def _(sp):
            sp.dma_start(kk[:, :, :], d["kk"]).then_inc(consts, 16)
            sp.dma_start(v[:, 8, :], d["region"]).then_inc(consts, 16)
            sp.dma_start(v[:, 9, :], d["number"]).then_inc(consts, 16)
            w1, b1, w2, b2 = weights1
            for name, to in (("w1_1", w1), ("b1_1", b1), ("w2_1", w2)):
                sp.dma_start(to, d[name]).then_inc(weights_in, 16)
            sp.dma_start(b2, bass.AP(d["b2_1"].tensor, 0, [[0, 128], [1, E * F]])).then_inc(weights_in, 16)
            sp.wait_ge(zero_set, 1)
            sp.dma_start(rows(h3_dram[TOK:TOK + RB, :]), zeros[:, :]).then_inc(zero_out, 16)
            sp.dma_start(rows(xs_dram[DUMMY_IN:DUMMY_IN + RB, :]), zeros[:, :]).then_inc(zero_out, 16)
            sp.wait_ge(ends_ready, 1)
            for e in range(E):
                row = sp.value_load(vi[0:1, 0, e:e + 1], min_val=e * REG, max_val=e * REG + TOK)
                sp.dma_start(rows(xs_dram[bass.ds(row, RB), :]), zeros[:, :]).then_inc(zero_out, 16)
            sp.wait_ge(zero_out, 16 * (E + 2))
            sp.wait_ge(weights_in, 64)

        @block.vector
        def _(dve):
            ch = Chain(dve, step)
            count, tiles, off, first, ones, last, region, number = (v[:, r, :] for r in (0, 1, 2, 3, 4, 5, 8, 9))
            ch.link(dve.memset(ones, 1.0))
            dve.wait_ge(consts, 48)
            dve.tensor_copy(vi[:, 0, :], base[0:1, :]).then_inc(ends_ready, 1)
            ch.link(dve.tensor_tensor(count, base[0:1, :], region, ALU.subtract))
            ch.link(dve.tensor_scalar(tiles, count, float(RB - 1), None, ALU.add))
            ch.link(dve.tensor_copy(vi[:, 1, :], tiles))
            ch.link(dve.tensor_scalar(vi[:, 2, :], vi[:, 1, :], RB.bit_length() - 1, None, ALU.logical_shift_right))
            ch.link(dve.tensor_copy(tiles, vi[:, 2, :]))
            ch.link(dve.tensor_tensor_scan(off, ones, count, 0.0, ALU.mult, ALU.add))
            ch.link(dve.tensor_tensor(off, off, count, ALU.subtract))
            ch.link(dve.tensor_tensor_scan(last, ones, tiles, 0.0, ALU.mult, ALU.add))
            ch.link(dve.tensor_tensor(first, last, tiles, ALU.subtract))

            def wide(r):
                return r.unsqueeze(1).to_broadcast([1, NK, E])

            ch.link(dve.tensor_tensor(a[:, :, :], kk[:, :, :], wide(last), ALU.is_lt))
            ch.link(dve.tensor_tensor(ind[:, :, :], kk[:, :, :], wide(first), ALU.is_ge))
            ch.link(dve.tensor_tensor(ind[:, :, :], ind[:, :, :], a[:, :, :], ALU.mult))
            ch.link(dve.tensor_tensor(a[:, :, :], kk[:, :, :], wide(first), ALU.subtract))
            ch.link(dve.tensor_scalar(a[:, :, :], a[:, :, :], float(RB), None, ALU.mult))
            for r, (start, none) in enumerate(((region, DUMMY_IN), (off, DUMMY_OUT))):
                ch.link(dve.tensor_tensor(val[:, r, :, :], a[:, :, :], wide(start), ALU.add))
                ch.link(dve.tensor_scalar(val[:, r, :, :], val[:, r, :, :], -float(none), None, ALU.add))
                ch.link(dve.tensor_tensor(val[:, r, :, :], val[:, r, :, :], ind[:, :, :], ALU.mult))
                ch.link(dve.tensor_reduce(tf[:, r, :], val[:, r, :, :], AX.X, ALU.add))
                ch.link(dve.tensor_scalar(tf[:, r, :], tf[:, r, :], float(none), None, ALU.add))
            ch.link(dve.tensor_tensor(a[:, :, :], ind[:, :, :], wide(number), ALU.mult))
            ch.link(dve.tensor_reduce(tf[:, 2, :], a[:, :, :], AX.X, ALU.add))
            ch.link(dve.tensor_copy(tab[:, :, :], tf[:, :, :]))


def mixture1(nc, k, ident, tab, xs_dram, h3_dram, out, weights1):
    ctx = ExitStack()
    with ctx:
        CH = F1 // F
        RP = RB // 128
        RING = 4
        TURNS = (NK - RING) // RING
        w1, b1, w2, b2 = weights1
        w1e = k.sb(ctx, "w1e", [F, 2, F1])
        b1e = k.sb(ctx, "b1e", [F, 2, CH])
        xs = k.sb(ctx, "xs_i", [128, RING, RP, F])
        xt = k.sb(ctx, "xt_i", [F, 2, RB])
        h3 = k.sb(ctx, "h3_i", [128, RING, RP, F])
        hid = k.sb(ctx, "hid_i", [F, 2, CH, RB])
        y = k.sb(ctx, "y_i", [128, 2, RP, F])
        res = k.sb(ctx, "res", [128, RING, RP, F])
        p_x = [k.ps(ctx, f"p_xi{u}") for u in range(2)]
        p_u = [[k.ps(ctx, f"p_ui{u}{r}") for r in range(2)] for u in range(2)]
        p_y = [k.ps(ctx, f"p_yi{u}") for u in range(2)]
        w1e_copied = k.sem("w1e_copied")
        xs_in = [k.sem(f"xs_in{u}") for u in range(RING)]
        h3_in = [k.sem(f"h3_in{u}") for u in range(RING)]
        stored = k.sem("stored")
        x_done = k.sem("x_done")
        x_copied = k.sem("x_copied")
        up_done = k.sem("up_done")
        relu_done = k.sem("relu_done_i")
        y_done = k.sem("y_done_i")
        y_step = k.sem("y_step")
        res_done = k.sem("res_done")
        block = ctx.enter_context(nc.Block())

        @block.sync
        def _(sp):
            def load_x(t, u):
                row = sp.value_load(tab[0:1, 0, bass.ds(t, 1)], min_val=0, max_val=DUMMY_IN)
                sp.wait_ge(x_done, t + 1)
                sp.dma_start(xs[:, u, :, :], xs_dram[bass.ds(row, RB), :].rearrange("(p r) f -> p r f", r=RP)).then_inc(xs_in[u], 16)

            def load_h(t, u):
                row = sp.value_load(tab[0:1, 1, bass.ds(t, 1)], min_val=0, max_val=DUMMY_OUT)
                sp.wait_ge(res_done, t + 1)
                sp.dma_start(h3[:, u, :, :], h3_dram[bass.ds(row, RB), :].rearrange("(p r) f -> p r f", r=RP)).then_inc(h3_in[u], 16)

            def store(t, u):
                row = sp.value_load(tab[0:1, 1, bass.ds(t, 1)], min_val=0, max_val=DUMMY_OUT)
                sp.wait_ge(res_done, t + 1 + RING)
                sp.wait_ge(stored, t * 16 + 32)
                sp.dma_start(out[bass.ds(row, RB), :].rearrange("(p r) f -> p r f", r=RP), res[:, u, :, :]).then_inc(stored, 16)

            for u in range(RING):
                load_x(u, u)
                load_h(u, u)

            def turn(t, u, more):
                if more:
                    load_x(t + RING, u)
                    load_h(t + RING, u)
                store(t, u)

            with sp.Fori(0, TURNS) as i:
                for u in range(RING):
                    turn(i * RING + u, u, True)
            for t in range(TURNS * RING, NK):
                turn(t, t % RING, t + RING < NK)
            sp.wait_ge(stored, NK * 16 + 32)

        @block.gpsimd
        def _(pool):
            def weights(t, u):
                e = pool.value_load(tab[0:1, 2, bass.ds(t, 1)], min_val=0, max_val=E - 1)
                pool.wait_ge(up_done, t * 2 + 2)
                pool.wait_ge(relu_done, t * 2 + 2)
                apart(pool)
                pool.tensor_copy(b1e[:, u, :], b1[:, bass.ds(e * CH, CH)])
                pool.tensor_copy(w1e[:, u, :], w1[:, bass.ds(e * F1, F1)]).then_inc(w1e_copied, 1)

            with pool.Fori(0, NK // 2) as i:
                for u in range(2):
                    weights(i * 2 + u, u)

        @block.tensor
        def _(pe):
            def transpose_x(t, r4, turn):
                u = r4 % 2
                pe.wait_ge(xs_in[r4], turn * 16 + 16)
                pe.wait_ge(x_copied, t + 1)
                for r in range(RP):
                    m = pe.transpose(p_x[u][:, r * 128:(r + 1) * 128], xs[:, r4, r, :], ident[:, :])
                m.then_inc(x_done, 1)

            def first(t, u):
                pe.wait_ge(w1e_copied, t + 1)
                pe.wait_ge(x_copied, t + 1 + 2)
                for c in range(CH):
                    if c % 2 == 0:
                        pe.wait_ge(relu_done, t * 2 + c // 2 + 1)
                    m = pe.matmul(p_u[u][c // 2][:, c % 2 * RB:(c % 2 + 1) * RB], w1e[:, u, c * F:(c + 1) * F], xt[:, u, :],
                                  start=True, stop=True)
                    if c % 2:
                        m.then_inc(up_done, 1)

            def second(t, u):
                e = pe.value_load(tab[0:1, 2, bass.ds(t, 1)], min_val=0, max_val=E - 1)
                pe.wait_ge(relu_done, t * 2 + 2 + 4)
                pe.wait_ge(res_done, t + RING - 1)
                for r in range(RP):
                    for c in range(CH):
                        m = pe.matmul(p_y[u][:, r * F:(r + 1) * F], hid[:, u, c, r * 128:(r + 1) * 128],
                                      w2[:, bass.ds(e * (CH * F) + c * F, F)], start=(c == 0), stop=(c == CH - 1))
                m.then_inc(y_done, 1)

            def turn(t, u, i):
                first(t, u % 2)
                transpose_x(t + 1, (u + 1) % RING, i + (u + 1) // RING)
                second(t - 1, (u + 1) % 2)

            transpose_x(0, 0, 0)
            first(0, 0)
            transpose_x(1, 1, 0)
            for t in range(1, RING):
                turn(t, t, 0)
            with pe.Fori(1, TURNS) as i:
                for u in range(RING):
                    turn(i * RING + u, u, i)
            for t in range(TURNS * RING, NK - 1):
                turn(t, t % RING, t // RING)
            first(NK - 1, 1)
            second(NK - 2, 0)
            second(NK - 1, 1)

        @block.scalar
        def _(act):
            act.sem_inc(x_copied, 2)
            act.sem_inc(stored, 32)
            act.sem_inc(relu_done, 4)
            act.sem_inc(x_done, RING)
            with act.Fori(0, NK // 2) as i:
                for u in range(2):
                    t = i * 2 + u
                    act.wait_ge(y_done, t + 1)
                    for c in range(CH):
                        if c % 2 == 0:
                            act.wait_ge(up_done, t * 2 + c // 2 + 1 + 4)
                        m = act.activation(hid[:, u, c, :], p_u[u][c // 2][:, c % 2 * RB:(c % 2 + 1) * RB], ACT.Relu,
                                           bias=b1e[:, u, c:c + 1])
                        if c % 2:
                            m.then_inc(relu_done, 1)

        @block.vector
        def _(dve):
            dve.sem_inc(up_done, 4)
            dve.sem_inc(y_done, 2)
            dve.sem_inc(res_done, RING)

            def copy_x(t, u):
                dve.wait_ge(up_done, t * 2 + 2)
                dve.wait_ge(x_done, t + 1 + RING)
                dve.tensor_copy(xt[:, u, :], p_x[u][:, 0:RB]).then_inc(x_copied, 1)

            def result(t, r4, turn):
                u = r4 % 2
                e = dve.value_load(tab[0:1, 2, bass.ds(t, 1)], min_val=0, max_val=E - 1)
                dve.wait_ge(y_done, t + 1 + 2)
                apart(dve)
                ch = Chain(dve, y_step, t, 1)
                ch.link(dve.tensor_tensor(y[:, u, :, :], p_y[u][:, 0:RB].rearrange("p (r f) -> p r f", r=RP),
                                          b2[:, bass.ds(e * F, F)].unsqueeze(1).to_broadcast([128, RP, F]), ALU.add))
                dve.wait_ge(h3_in[r4], turn * 16 + 16)
                if not (isinstance(t, int) and t < RING - 2):
                    dve.wait_ge(stored, (t - RING + 1) * 16 + 32)
                dve.tensor_tensor(res[:, r4, :, :], y[:, u, :, :], h3[:, r4, :, :], ALU.add).then_inc(res_done, 1)

            copy_x(0, 0)
            copy_x(1, 1)

            def turn(t, u, i):
                if not (isinstance(t, int) and t + 2 >= NK):
                    copy_x(t + 2, u % 2)
                result(t, u, i)

            for u in range(RING):
                turn(u, u, 0)
            with dve.Fori(1, TURNS) as i:
                for u in range(RING):
                    turn(i * RING + u, u, i)
            for t in range(TURNS * RING, NK):
                turn(t, t % RING, t // RING)


def audio_tower(nc, d, out):
    top = ExitStack()
    with top:
        k = Tools(nc, top)
        h0_dram = nc.dram_tensor("h0_dram", [HALF, NT * F], FP32)
        att_dram = nc.dram_tensor("att_dram", [NG, HALF, 2, B * CG], FP32)
        filt_dram = nc.dram_tensor("filt_dram", [2, STAGES, F, PAD], FP32)

        ident = k.sb(top, "ident", [128, 128])
        small = k.sb(top, "small", [128, 8])
        bn = k.sb(top, "bn", [128, 2])
        front = ExitStack()
        with front:
            fm = k.sb(front, "fm", [F, TOK])
            fm_rev = k.sb(front, "fm_rev", [F, TOK])
            tdnn(nc, k, d, ident, small, bn, fm, filt_dram)
            first_norm(nc, k, d, ident, bn, fm, fm_rev, h0_dram)
            convolutions(nc, k, d, fm, fm_rev, filt_dram, att_dram)
        h = k.sb(top, "h", [HALF, NT * F])
        middle = ExitStack()
        with middle:
            xf = k.sb(middle, "xf", [F, TOK])
            s_tok = k.sb(middle, "s_tok", [HALF, 2, B, E])
            g_tok = k.sb(middle, "g_tok", [HALF, 2, B, E])
            attach_norm(nc, k, d, ident, h0_dram, att_dram, h, xf, s_tok)
            weights0 = (k.sb(middle, "w1_0", [F, E, F0])[:, :, :], k.sb(middle, "b1_0", [F, E, F0 // F])[:, :, :],
                        k.sb(middle, "w2_0", [F, E, F0 // F, F])[:, :, :, :])
            choose(nc, k, d, ident, h, s_tok, g_tok, weights0)
            mixture0(nc, k, h, xf, g_tok, weights0)
        xs_dram = nc.dram_tensor("xs_dram", [DUMMY_IN + RB, F], FP32)
        h3_dram = nc.dram_tensor("h3_dram", [TOK + RB, F], FP32)
        base = k.sb(top, "base", [HALF, E])
        tab = k.sb(top, "tab", [1, 3, NK], I32)
        retain_and_route(nc, k, d, ident, small, h, base, xs_dram, h3_dram)
        weights1 = (k.sb(top, "w1_1", [F, E * F1])[:, :], k.sb(top, "b1_1", [F, E * F1 // F])[:, :],
                    k.sb(top, "w2_1", [F, E * F1])[:, :], k.sb(top, "b2_1", [128, E * F])[:, :])
        plan_tiles(nc, k, d, base, tab, xs_dram, h3_dram, weights1)
        mixture1(nc, k, ident, tab, xs_dram, h3_dram, out, weights1)


def constants():
    import numpy as np

    half = F // 2
    freqs = np.float32(10000.0) ** (-np.arange(half, dtype=np.float32) / np.float32(half))
    phi = np.arange(L, dtype=np.float32)[:, None] * freqs.astype(np.float32)[None, :]
    pe = np.concatenate([np.sin(phi), np.cos(phi)], axis=-1).astype(np.float32)
    gamma = 1.0 - 2.0 ** (-5.0 - np.arange(HEADS, dtype=np.float64))
    rel = np.arange(HALF)[:, None, None] - np.arange(HALF)
    decay = (np.where(rel >= 0, gamma[:, None] ** np.maximum(rel, 0), 0.0) / np.sqrt(HD)).astype(np.float32)
    head = np.arange(F) // HD
    decay_i = (gamma[head][:, None] ** (HALF - np.arange(HALF))).astype(np.float32)
    decay_j = (gamma[head][None, :] ** np.arange(HALF)[:, None] / np.sqrt(HD)).astype(np.float32)
    same = (head[:, None] == head[None, :]).astype(np.float32)
    even = (np.arange(F) // HD % 2 == 0).astype(np.float32)
    more = {"decay": decay, "decay_i": decay_i, "decay_j": decay_j, "same": same, "even": even, "before": np.triu(np.ones((HALF, HALF), np.float32), 1),
            "prio": (E - np.arange(E, dtype=np.float32))[None, :], "region": (REG * np.arange(E, dtype=np.float32))[None, :],
            "number": np.arange(E, dtype=np.float32)[None, :],
            "kk": np.repeat(np.arange(NK, dtype=np.float32), E).reshape(1, NK, E)}
    return {**more, "ident": np.eye(128, dtype=np.float32), "flip": np.eye(HALF, dtype=np.float32)[::-1].copy(), "pe_t": np.ascontiguousarray(pe.T)}


def kernel(**inputs):
    import numpy as np
    import concourse.bacc as bacc
    from concourse.bass_utils import run_bass_kernel_spmd

    a = {n: np.asarray(v) for n, v in inputs.items()}
    rows = constants()
    rows["x"] = a["x"].reshape(-1)
    rows["tok_w"] = np.concatenate([a["L0_tok_W"].T, a["L0_tok_b"][None, :]], axis=0)
    even = rows.pop("even")
    rows["small"] = np.stack([a["L0_tok_gamma"], a["L0_tok_beta"], even, (even == 0).astype(np.float32), a["L1_attn_bq"],
                              a["L1_attn_bk"], np.zeros(F, np.float32), np.zeros(F, np.float32)], axis=1)
    rows["bk"] = a["L1_attn_bk"][None, :]
    rows["wq"] = a["L1_attn_wq"].T
    rows["wk"] = a["L1_attn_wk"].T
    rows["wvg"] = np.concatenate([a["L1_attn_wv"].T, a["L1_attn_wg"].T], axis=1)
    rows["bvg"] = np.concatenate([a["L1_attn_bv"], a["L1_attn_bg"]])[None, :]
    rows["wg1"] = a["L1_ffn_Wg"]
    rows["bg1"] = a["L1_ffn_bg"][None, :]
    rows["w1_1"] = a["L1_ffn_W1"].transpose(1, 0, 2).reshape(F, E * F1)
    rows["b1_1"] = a["L1_ffn_b1"].reshape(E * F1 // F, F).T
    rows["w2_1"] = a["L1_ffn_W2"].reshape(E * F1 // F, F, F).transpose(1, 0, 2).reshape(F, E * F1)
    rows["b2_1"] = a["L1_ffn_b2"].reshape(1, E * F)
    rows["w_filt"] = a["L0_attn_W_filt"].reshape(F, F * STAGES)
    rows["w_proj"] = a["L0_attn_W_proj"].reshape(F, NG, CG, 2, 2).transpose(0, 1, 4, 3, 2).reshape(F, NG, 2, 2 * CG)
    rows["wg0"] = a["L0_ffn_Wg"]
    rows["b2_0"] = a["L0_ffn_b2"]
    rows["w1_0"] = a["L0_ffn_W1"].transpose(1, 0, 2)
    rows["b1_0"] = a["L0_ffn_b1"].reshape(E, F0 // F, F).transpose(2, 0, 1)
    rows["w2_0"] = a["L0_ffn_W2"].reshape(E, F0 // F, F, F).transpose(2, 0, 1, 3)
    rows = {n: np.ascontiguousarray(v) for n, v in rows.items()}

    nc = bacc.Bacc("TRN2", target_bir_lowering=False, num_devices=1)
    d = {n: nc.dram_tensor(f"in_{n}", v.shape, mybir.dt.from_np(v.dtype), kind="ExternalInput").ap()
         for n, v in rows.items()}
    out = nc.dram_tensor("out", (TOK + RB, F), FP32, kind="ExternalOutput").ap()
    audio_tower(nc, d, out)
    r = run_bass_kernel_spmd(nc, [{f"in_{n}": v for n, v in rows.items()}], core_ids=[0])
    return r.results[0]["out"][:TOK].reshape(B, L, F)
```
